# Optimizing a Trainium2 kernel written in Bass

```python
import numpy as np
import jax
import jax.numpy as jnp

def _softmax(x, axis=-1):
    return jax.nn.softmax(x, axis=axis)

def _gelu(x):
    return jax.nn.gelu(x, approximate=True)

def _silu(x):
    return jax.nn.silu(x)

def _sigmoid(x):
    return jax.nn.sigmoid(x)

def _layernorm(x, axis=-1, eps=1e-05):
    m = jnp.mean(x, axis=axis, keepdims=True)
    v = jnp.var(x, axis=axis, keepdims=True)
    return (x - m) / jnp.sqrt(v + eps)

def _scatter_add(tgt, idx, src, axis=0):
    return tgt.at[idx].add(src)

def _segment_sum(src, seg, n):
    return jax.ops.segment_sum(src, seg, n)
kernel_name = 'mk_perceiver_d1_seqx_r4_f2b43d'

def setup_inputs(seed: int=0):
    np.random.seed(seed)
    _w = jnp.asarray

    def _rec_inputs():
        import jax
        import jax.numpy as jnp
        _rk = jax.random.key(seed)
        x = -0.0002928 + 1 * jax.random.normal(jax.random.fold_in(_rk, 1), (1, 256, 256), jnp.float32)
        _lenS = 256 - jax.random.randint(jax.random.fold_in(_rk, 7), (1,), 0, max(1, 256 // 4) + 1, jnp.int32)
        _lenS2 = 4096 - jax.random.randint(jax.random.fold_in(_rk, 8), (1,), 0, max(1, 4096 // 4) + 1, jnp.int32)
        _ctx_1024P = jax.random.normal(jax.random.fold_in(_rk, 11), (1, 16, 256), jnp.float32)
        _ctx_1024c = jax.random.dirichlet(jax.random.fold_in(_rk, 511), 0.3 * jnp.ones((16,), jnp.float32), (1, 4096))
        _ctx_1024t = jnp.einsum('bsk,bkd->bsd', _ctx_1024c, _ctx_1024P)
        _ctx_1024t = _ctx_1024t * jax.lax.rsqrt(jnp.mean(jnp.square(_ctx_1024t)) + 1e-12) * 0.953939
        ctx_1024 = -1.39393e-06 + 0.999914 * (_ctx_1024t + 0.3 * jax.random.normal(jax.random.fold_in(_rk, 611), (1, 4096, 256), jnp.float32))
        return (x, ctx_1024)
    x, ctx_1024 = _rec_inputs()

    def _L0_xattn_setup():
        import jax, jax.numpy as jnp
        import numpy as np
        D_MODEL = 256
        N_HEADS = 16
        D_K = D_MODEL // N_HEADS
        key = jax.random.key(seed)
        ks = jax.random.split(key, 11)
        B, L, S = (2, 512, 512)
        scale = 1.0 / np.sqrt(D_MODEL)
        return {'x_q': jax.random.normal(ks[0], (B, L, D_MODEL), jnp.float32), 'x_k': jax.random.normal(ks[1], (B, S, D_MODEL), jnp.float32), 'x_v': jax.random.normal(ks[2], (B, S, D_MODEL), jnp.float32), 'W_Q': jax.random.normal(ks[3], (D_MODEL, D_MODEL), jnp.float32) * scale, 'b_Q': jax.random.normal(ks[4], (D_MODEL,), jnp.float32) * 0.01, 'W_K': jax.random.normal(ks[5], (D_MODEL, D_MODEL), jnp.float32) * scale, 'b_K': jax.random.normal(ks[6], (D_MODEL,), jnp.float32) * 0.01, 'W_V': jax.random.normal(ks[7], (D_MODEL, D_MODEL), jnp.float32) * scale, 'b_V': jax.random.normal(ks[8], (D_MODEL,), jnp.float32) * 0.01, 'W_O': jax.random.normal(ks[9], (D_MODEL, D_MODEL), jnp.float32) * scale, 'b_O': jax.random.normal(ks[10], (D_MODEL,), jnp.float32) * 0.01}
    _L0_xattn_all = _L0_xattn_setup()
    _L0_xattn_in = {k: v for k, v in _L0_xattn_all.items() if k in ('W_Q', 'b_Q', 'W_K', 'b_K', 'W_V', 'b_V', 'W_O', 'b_O')}
    del _L0_xattn_all

    def _L0_attn_setup():
        import jax, jax.numpy as jnp
        import numpy as np
        B, L = (2, 256)
        D_MODEL, D_CKV, D_CQ = (256, 64, 128)
        N_HEAD, D_HEAD, D_ROPE = (8, 64, 32)
        N_IDX_HEAD = 4
        K_TS, LW = (96, 64)
        ROPE_BASE = 10000.0

        def _pope(x, angles):
            cos, sin = (jnp.cos(angles), jnp.sin(angles))
            mu1, mu2 = jnp.split(jax.nn.softplus(x), 2, axis=-1)
            return jnp.concatenate([mu1 * cos - mu2 * sin, mu1 * sin + mu2 * cos], axis=-1)

        def _forward(x, W_dkv, W_uk, W_uv, W_dq, W_uq, W_qr, W_kr, W_out, idx_wq, idx_wk, idx_w, raw_delta):
            B_, L_, _ = x.shape
            c_kv = x @ W_dkv
            q_i = (x @ idx_wq).reshape(B_, L_, N_IDX_HEAD, D_HEAD)
            k_i = x @ idx_wk
            s_i = jax.nn.relu(jnp.einsum('bthd,bsd->bths', q_i, k_i))
            I = jnp.einsum('bths,h->bts', s_i, idx_w)
            qpos = jnp.arange(L_)[:, None]
            kpos = jnp.arange(L_)[None, :]
            local = (kpos >= qpos - LW + 1) & (kpos <= qpos)
            causal = kpos > qpos
            I = jnp.where(local[None], jnp.inf, I)
            I = jnp.where(causal[None], -jnp.inf, I)
            kk = min(K_TS, L_)
            _, idx = jax.lax.top_k(I, kk)
            bi = jnp.arange(B_)[:, None, None]
            key_c = (c_kv @ W_uk)[bi, idx].reshape(B_, L_, kk, N_HEAD, D_HEAD)
            value = (c_kv @ W_uv)[bi, idx].reshape(B_, L_, kk, N_HEAD, D_HEAD)
            c_q = x @ W_dq
            query_c = (c_q @ W_uq).reshape(B_, L_, N_HEAD, D_HEAD)
            half = D_ROPE // 2
            theta = 1.0 / ROPE_BASE ** (2.0 * jnp.arange(half, dtype=jnp.float32) / D_ROPE)
            delta = -2.0 * jnp.pi * jax.nn.sigmoid(raw_delta)
            angles_q = jnp.arange(L_, dtype=jnp.float32)[:, None] * theta[None, :] + delta
            query_r = _pope((c_q @ W_qr).reshape(B_, L_, N_HEAD, D_ROPE), angles_q[None, :, None, :])
            kr_sel = (x @ W_kr)[bi, idx]
            angles_k = jnp.arange(kk, dtype=jnp.float32)[:, None] * theta[None, :] + delta
            key_r = _pope(kr_sel, angles_k[None, None, :, :])
            scale = (D_HEAD + D_ROPE) ** (-0.5)
            q_c = query_c.transpose(0, 2, 1, 3)
            q_r = query_r.transpose(0, 2, 1, 3)
            k_c = key_c.transpose(0, 3, 1, 2, 4)
            v = value.transpose(0, 3, 1, 2, 4)
            scores = (jnp.einsum('bhld,bhlkd->bhlk', q_c, k_c) + jnp.einsum('bhld,blkd->bhlk', q_r, key_r)) * scale
            attn = jax.nn.softmax(scores.astype(jnp.float32), axis=-1).astype(v.dtype)
            out = jnp.einsum('bhlk,bhlkd->bhld', attn, v)
            out = out.transpose(0, 2, 1, 3).reshape(B_, L_, N_HEAD * D_HEAD)
            return out @ W_out
        key = jax.random.key(seed)
        ks = jax.random.split(key, 14)

        def w(k, shape, fan_in):
            return jax.random.normal(k, shape, dtype=jnp.float32) * fan_in ** (-0.5)
        return {'x': jax.random.normal(ks[0], (B, L, D_MODEL), dtype=jnp.float32), 'W_dkv': w(ks[1], (D_MODEL, D_CKV), D_MODEL), 'W_uk': w(ks[2], (D_CKV, N_HEAD * D_HEAD), D_CKV), 'W_uv': w(ks[3], (D_CKV, N_HEAD * D_HEAD), D_CKV), 'W_dq': w(ks[4], (D_MODEL, D_CQ), D_MODEL), 'W_uq': w(ks[5], (D_CQ, N_HEAD * D_HEAD), D_CQ), 'W_qr': w(ks[6], (D_CQ, N_HEAD * D_ROPE), D_CQ), 'W_kr': w(ks[7], (D_MODEL, D_ROPE), D_MODEL), 'W_out': w(ks[8], (N_HEAD * D_HEAD, D_MODEL), N_HEAD * D_HEAD), 'idx_wq': w(ks[9], (D_MODEL, N_IDX_HEAD * D_HEAD), D_MODEL), 'idx_wk': w(ks[10], (D_MODEL, D_HEAD), D_MODEL), 'idx_w': jnp.ones((N_IDX_HEAD,), dtype=jnp.float32), 'raw_delta': jax.random.normal(ks[11], (D_ROPE // 2,), dtype=jnp.float32) * 0.1}
    _L0_attn_all = _L0_attn_setup()
    _L0_attn_in = {k: v for k, v in _L0_attn_all.items() if k in ('W_dkv', 'W_uk', 'W_uv', 'W_dq', 'W_uq', 'W_qr', 'W_kr', 'W_out', 'idx_wq', 'idx_wk', 'idx_w', 'raw_delta')}
    del _L0_attn_all

    def _L0_ffn_setup():
        import jax, jax.numpy as jnp
        import numpy as np
        HIDDEN = 256
        INNER = 1024

        def _weight_quant(w):
            scale = 1.0 / jnp.clip(jnp.mean(jnp.abs(w)), 1e-05)
            wq = jnp.clip(jnp.round(w * scale), -1.0, 1.0) / scale
            return w + jax.lax.stop_gradient(wq - w)

        def _act_quant(x):
            scale = 127.0 / jnp.clip(jnp.max(jnp.abs(x), axis=-1, keepdims=True), 1e-05)
            xq = jnp.clip(jnp.round(x * scale), -128.0, 127.0) / scale
            return x + jax.lax.stop_gradient(xq - x)

        def _bitlinear(x, w):
            return jnp.einsum('bsi,oi->bso', _act_quant(x), _weight_quant(w))
        key = jax.random.key(seed)
        k0, k1, k2, k3 = jax.random.split(key, 4)
        x = jax.random.normal(k0, (4, 512, HIDDEN), dtype=jnp.float32)
        w_gate = jax.random.normal(k1, (INNER, HIDDEN), dtype=jnp.float32) / np.sqrt(HIDDEN)
        w_up = jax.random.normal(k2, (INNER, HIDDEN), dtype=jnp.float32) / np.sqrt(HIDDEN)
        w_down = jax.random.normal(k3, (HIDDEN, INNER), dtype=jnp.float32) / np.sqrt(INNER)
        return {'x': x, 'w_gate': w_gate, 'w_up': w_up, 'w_down': w_down}
    _L0_ffn_all = _L0_ffn_setup()
    _L0_ffn_in = {k: v for k, v in _L0_ffn_all.items() if k in ('w_gate', 'w_up', 'w_down')}
    del _L0_ffn_all
    return {'x': x, 'ctx_1024': ctx_1024, 'L0_xattn_W_Q': _L0_xattn_in['W_Q'], 'L0_xattn_b_Q': _L0_xattn_in['b_Q'], 'L0_xattn_W_K': _L0_xattn_in['W_K'], 'L0_xattn_b_K': _L0_xattn_in['b_K'], 'L0_xattn_W_V': _L0_xattn_in['W_V'], 'L0_xattn_b_V': _L0_xattn_in['b_V'], 'L0_xattn_W_O': _L0_xattn_in['W_O'], 'L0_xattn_b_O': _L0_xattn_in['b_O'], 'L0_attn_W_dkv': _L0_attn_in['W_dkv'], 'L0_attn_W_uk': _L0_attn_in['W_uk'], 'L0_attn_W_uv': _L0_attn_in['W_uv'], 'L0_attn_W_dq': _L0_attn_in['W_dq'], 'L0_attn_W_uq': _L0_attn_in['W_uq'], 'L0_attn_W_qr': _L0_attn_in['W_qr'], 'L0_attn_W_kr': _L0_attn_in['W_kr'], 'L0_attn_W_out': _L0_attn_in['W_out'], 'L0_attn_idx_wq': _L0_attn_in['idx_wq'], 'L0_attn_idx_wk': _L0_attn_in['idx_wk'], 'L0_attn_idx_w': _L0_attn_in['idx_w'], 'L0_attn_raw_delta': _L0_attn_in['raw_delta'], 'L0_ffn_w_gate': _L0_ffn_in['w_gate'], 'L0_ffn_w_up': _L0_ffn_in['w_up'], 'L0_ffn_w_down': _L0_ffn_in['w_down']}

def reference(x, ctx_1024, L0_xattn_W_Q, L0_xattn_b_Q, L0_xattn_W_K, L0_xattn_b_K, L0_xattn_W_V, L0_xattn_b_V, L0_xattn_W_O, L0_xattn_b_O, L0_attn_W_dkv, L0_attn_W_uk, L0_attn_W_uv, L0_attn_W_dq, L0_attn_W_uq, L0_attn_W_qr, L0_attn_W_kr, L0_attn_W_out, L0_attn_idx_wq, L0_attn_idx_wk, L0_attn_idx_w, L0_attn_raw_delta, L0_ffn_w_gate, L0_ffn_w_up, L0_ffn_w_down):
    import jax
    import jax.numpy as jnp

    def _L0_xattn_ref(x_q, x_k, x_v, W_Q, b_Q, W_K, b_K, W_V, b_V, W_O, b_O):
        import jax, jax.numpy as jnp
        import numpy as np
        D_MODEL = 256
        N_HEADS = 16
        D_K = D_MODEL // N_HEADS
        B, L, _ = x_q.shape
        S = x_k.shape[1]
        H, dk = (N_HEADS, D_K)
        Q = (x_q @ W_Q + b_Q).reshape(B, L, H, dk).transpose(0, 2, 1, 3)
        K = (x_k @ W_K + b_K).reshape(B, S, H, dk).transpose(0, 2, 1, 3)
        V = (x_v @ W_V + b_V).reshape(B, S, H, dk).transpose(0, 2, 1, 3)
        scores = jnp.einsum('bhld,bhsd->bhls', Q, K) / jnp.sqrt(jnp.float32(dk))
        attn = jax.nn.softmax(scores, axis=-1)
        ctx = jnp.einsum('bhls,bhsd->bhld', attn, V)
        ctx = ctx.transpose(0, 2, 1, 3).reshape(B, L, H * dk)
        out = ctx @ W_O + b_O
        return out

    def _L0_attn_ref(x, W_dkv, W_uk, W_uv, W_dq, W_uq, W_qr, W_kr, W_out, idx_wq, idx_wk, idx_w, raw_delta):
        import jax, jax.numpy as jnp
        import numpy as np
        B, L = (2, 256)
        D_MODEL, D_CKV, D_CQ = (256, 64, 128)
        N_HEAD, D_HEAD, D_ROPE = (8, 64, 32)
        N_IDX_HEAD = 4
        K_TS, LW = (96, 64)
        ROPE_BASE = 10000.0

        def _pope(x, angles):
            cos, sin = (jnp.cos(angles), jnp.sin(angles))
            mu1, mu2 = jnp.split(jax.nn.softplus(x), 2, axis=-1)
            return jnp.concatenate([mu1 * cos - mu2 * sin, mu1 * sin + mu2 * cos], axis=-1)

        def _forward(x, W_dkv, W_uk, W_uv, W_dq, W_uq, W_qr, W_kr, W_out, idx_wq, idx_wk, idx_w, raw_delta):
            B_, L_, _ = x.shape
            c_kv = x @ W_dkv
            q_i = (x @ idx_wq).reshape(B_, L_, N_IDX_HEAD, D_HEAD)
            k_i = x @ idx_wk
            s_i = jax.nn.relu(jnp.einsum('bthd,bsd->bths', q_i, k_i))
            I = jnp.einsum('bths,h->bts', s_i, idx_w)
            qpos = jnp.arange(L_)[:, None]
            kpos = jnp.arange(L_)[None, :]
            local = (kpos >= qpos - LW + 1) & (kpos <= qpos)
            causal = kpos > qpos
            I = jnp.where(local[None], jnp.inf, I)
            I = jnp.where(causal[None], -jnp.inf, I)
            kk = min(K_TS, L_)
            _, idx = jax.lax.top_k(I, kk)
            bi = jnp.arange(B_)[:, None, None]
            key_c = (c_kv @ W_uk)[bi, idx].reshape(B_, L_, kk, N_HEAD, D_HEAD)
            value = (c_kv @ W_uv)[bi, idx].reshape(B_, L_, kk, N_HEAD, D_HEAD)
            c_q = x @ W_dq
            query_c = (c_q @ W_uq).reshape(B_, L_, N_HEAD, D_HEAD)
            half = D_ROPE // 2
            theta = 1.0 / ROPE_BASE ** (2.0 * jnp.arange(half, dtype=jnp.float32) / D_ROPE)
            delta = -2.0 * jnp.pi * jax.nn.sigmoid(raw_delta)
            angles_q = jnp.arange(L_, dtype=jnp.float32)[:, None] * theta[None, :] + delta
            query_r = _pope((c_q @ W_qr).reshape(B_, L_, N_HEAD, D_ROPE), angles_q[None, :, None, :])
            kr_sel = (x @ W_kr)[bi, idx]
            angles_k = jnp.arange(kk, dtype=jnp.float32)[:, None] * theta[None, :] + delta
            key_r = _pope(kr_sel, angles_k[None, None, :, :])
            scale = (D_HEAD + D_ROPE) ** (-0.5)
            q_c = query_c.transpose(0, 2, 1, 3)
            q_r = query_r.transpose(0, 2, 1, 3)
            k_c = key_c.transpose(0, 3, 1, 2, 4)
            v = value.transpose(0, 3, 1, 2, 4)
            scores = (jnp.einsum('bhld,bhlkd->bhlk', q_c, k_c) + jnp.einsum('bhld,blkd->bhlk', q_r, key_r)) * scale
            attn = jax.nn.softmax(scores.astype(jnp.float32), axis=-1).astype(v.dtype)
            out = jnp.einsum('bhlk,bhlkd->bhld', attn, v)
            out = out.transpose(0, 2, 1, 3).reshape(B_, L_, N_HEAD * D_HEAD)
            return out @ W_out
        return _forward(x, W_dkv, W_uk, W_uv, W_dq, W_uq, W_qr, W_kr, W_out, idx_wq, idx_wk, idx_w, raw_delta)

    def _L0_ffn_ref(x, w_gate, w_up, w_down):
        import jax, jax.numpy as jnp
        import numpy as np
        HIDDEN = 256
        INNER = 1024

        def _weight_quant(w):
            scale = 1.0 / jnp.clip(jnp.mean(jnp.abs(w)), 1e-05)
            wq = jnp.clip(jnp.round(w * scale), -1.0, 1.0) / scale
            return w + jax.lax.stop_gradient(wq - w)

        def _act_quant(x):
            scale = 127.0 / jnp.clip(jnp.max(jnp.abs(x), axis=-1, keepdims=True), 1e-05)
            xq = jnp.clip(jnp.round(x * scale), -128.0, 127.0) / scale
            return x + jax.lax.stop_gradient(xq - x)

        def _bitlinear(x, w):
            return jnp.einsum('bsi,oi->bso', _act_quant(x), _weight_quant(w))
        gate = jax.nn.silu(_bitlinear(x, w_gate))
        up = _bitlinear(x, w_up)
        return _bitlinear(gate * up, w_down)
    x = x + _L0_xattn_ref(_layernorm(x, axis=-1), ctx_1024, ctx_1024, L0_xattn_W_Q, L0_xattn_b_Q, L0_xattn_W_K, L0_xattn_b_K, L0_xattn_W_V, L0_xattn_b_V, L0_xattn_W_O, L0_xattn_b_O)
    x = x + _L0_attn_ref(_layernorm(x, axis=-1), L0_attn_W_dkv, L0_attn_W_uk, L0_attn_W_uv, L0_attn_W_dq, L0_attn_W_uq, L0_attn_W_qr, L0_attn_W_kr, L0_attn_W_out, L0_attn_idx_wq, L0_attn_idx_wk, L0_attn_idx_w, L0_attn_raw_delta)
    x = x + _L0_ffn_ref(_layernorm(x, axis=-1), L0_ffn_w_gate, L0_ffn_w_up, L0_ffn_w_down)
    return x

_drawn_inputs = setup_inputs


def setup_inputs(seed=0):
    import zlib

    import numpy as np

    out = dict(_drawn_inputs(seed))
    spreads = {'L0_attn_idx_w': (1.0, 0.6)}
    factors = {'L0_xattn_b_Q': 8.0,
     'L0_xattn_b_K': 8.0,
     'L0_xattn_b_V': 4.419,
     'L0_xattn_b_O': 4.107,
     'L0_attn_raw_delta': 8.0}
    for name, (base, spread) in spreads.items():
        noise = np.random.default_rng([zlib.crc32(name.encode()), seed]).standard_normal(out[name].shape)
        drawn = base * np.exp(spread * noise) if base else spread * noise
        out[name] = jnp.asarray(drawn.astype(out[name].dtype))
    for name, factor in factors.items():
        out[name] = (out[name] * factor).astype(out[name].dtype)
    return out
```

```python
import concourse.bass as bass
from concourse import mybir
from contextlib import ExitStack
import numpy as np

fp32 = mybir.dt.float32
bf16 = mybir.dt.bfloat16
u32 = mybir.dt.uint32
ALU = mybir.AluOpType
ACT = mybir.ActivationFunctionType
AX = mybir.AxisListType

T, D = 256, 256
S = 4096
NT = T // 128
H1, DK = 16, 16
KT = S // 128
CH = 8
CK = S // CH
TPC = KT // CH
NBLK = 6
QROWS = NBLK * DK
SROWS = QROWS + 2
KBLK = [0, 0, 0, 1, 1, 2]
QBLK = [0, 1, 2, 0, 1, 0]
NKST = 3
ASCHED = [3, 3, 3, 3, 2, 2, 0, 0]
H2, DH, DR, DC = 8, 64, 32, 64
NI = 4
HALF = DR // 2
LW, KK = 64, 96
NR = KK - LW
G = T // 16
GR = G - LW // 16
W80 = LW + 16
SCALE2 = (DH + DR) ** -0.5
BIG = 1e30
FMIN = -3.4e38
MAGIC = 12582912.0
F = 1024
EPS = 1e-5

_COLS = [("ident", 128), ("lmask", W80), ("rmask", 32), ("iota", 2), ("cidx", 2 * HALF), ("sidx", 2 * HALF),
         ("cloc", 2 * HALF), ("sloc", 2 * HALF), ("tabx", NR), ("taby", NR), ("keep", 2 * 192), ("fill", 2 * 192)]
COL, NCONST = {}, 0
for _n, _w in _COLS:
    COL[_n] = (NCONST, NCONST + _w)
    NCONST += _w


def constants():
    c = np.zeros((128, NCONST), np.float64)

    def put(name, value):
        a, b = COL[name]
        c[:, a:b] = value.reshape(128, b - a)

    p = np.arange(128)
    put("ident", np.eye(128))
    q = 4 * (p // 32) + p % 4
    j = np.arange(W80)
    put("lmask", np.where((j[None] >= q[:, None] + 1) & (j[None] <= q[:, None] + LW), 0.0, -BIG))
    put("rmask", np.where((p // 32)[:, None] == (np.arange(32) % 4)[None], 0.0, -BIG))
    put("iota", np.stack([p, p + 128], 1).astype(float))
    theta = (np.float32(1.0) / np.float32(10000.0) ** (np.float32(2.0) * np.arange(HALF, dtype=np.float32)
                                                       / np.float32(DR))).astype(np.float32).astype(np.float64)
    t = p[:, None] + 128 * np.arange(2)[None]
    ang = t[:, :, None] * theta
    put("cidx", np.cos(ang)); put("sidx", np.sin(ang))
    ang = (t + np.maximum(0, t - (LW - 1)))[:, :, None] * theta
    put("cloc", np.cos(ang)); put("sloc", np.sin(ang))
    rank = LW + np.arange(NR)
    a = rank[None] * np.tile(theta, 8)[:, None]
    x, y = np.ones((128, NR)), np.zeros((128, NR))
    x[64:96], y[64:96] = np.cos(a[64:96]), -np.sin(a[64:96])
    x[96:112], y[96:112] = -np.sin(a[96:112]), -np.cos(a[96:112])
    x[112:], y[112:] = np.sin(a[112:]), np.cos(a[112:])
    put("tabx", x); put("taby", y)
    keep, fill = np.zeros((128, 2, 192)), np.full((128, 2, 192), -3.3e38)
    s = np.arange(192)
    for tile in range(2):
        past = s[None] <= t[:, tile][:, None] - LW
        keep[:, tile][past] = 1.0
        fill[:, tile][past] = 0.0
    ahead = (s[None] > t[:, 0][:, None]) & (s[None] < KK) | ((t[:, 0] < LW)[:, None] & (s[None] < KK))
    fill[:, 0] = np.where(ahead, -(2e38 + s * 1e35)[None], fill[:, 0])
    put("keep", keep); put("fill", fill)
    return c.astype(np.float32)


SEMS = """const_in x_in wq_in wkv_in bq_in bias_in ctx_in0 ctx_in1 ctx_in2 ctx_in3 wo_in aw_in rd_in fw_in0 fw_in1 fw_in2
    ident_b eps_set x_std xn_done xnT_ps xnT_sb q_ps qs_done qaT_ps qa_sb bq4 qsum
    ctxT_ps ctxT_a ctxT_v kT_ps k1_done kr_done k23_done kd_out0 kd_out1 v_ps v_done v_ones kst_ones kst_in0 kst_in1 kst_in2
    a_done a_read m_split mT_ps m_ready b_done exp_done pv_done o_read oT_ps oT_sb y1_ps x1_done xb_done
    wuT_ps wuT_sb wa_ps wa_sb wb_ps wb_sb fsum fsum_ps fscale_ps fscale fq fqT_ps fqT_sb fones
    dl_sig dl_sin dl_v tabs_done
    std2 xn2 xT2_ps xT2_sb qi_ps qi_sb ki_ps ki_sb ck_ps ck_sb cq_ps cq_sb cw_ps cw_sb
    ix0_ps ix1_ps relu0 relu1 idx_done d_done qa2_ps qa2_sb mu_ps mu_ln mu_done kmu_ln
    kmu_done krot kaug cko_done rot_rank rot_loc klT_ps klT_sb qrT_ps qrT_sb sl_ps sl_max cw_ones cs_ones
    bc_ps e_done kg_ps kg_sb cs_ps cs_sb sr_ps sr_sb srT_ps sr_max nm_done nmT_ps nmT_sb st_ps p_loc p_rank
    pv2_ps oc_done ocT_ps ocT_sb y2_ps x2_done
    std3 dq xn3 hq_done hqT_ps hqT_sb gu_ps silu pr_done pq_done pqT_ps pqT_sb y3_ps out_done out_dma
    dve_chain act_chain pool_chain""".split()


def build(nc, consts, a, out):
    ctx = ExitStack()
    with ctx:
        def sb(name, shape, dt=fp32):
            return ctx.enter_context(nc.sbuf_tensor(name, shape, dt))

        s = {n: ctx.enter_context(nc.semaphore(n)) for n in SEMS}
        PS = ctx.enter_context(nc.psum_tensor("PS", [128, 8, 512], fp32))
        kd = nc.dram_tensor("k_parts", (3, D, S), bf16, kind="Internal").ap()

        C = sb("C", [128, NCONST])

        def const(name):
            return C[:, COL[name][0]:COL[name][1]]

        ident = const("ident")
        identb = sb("identb", [128, 128], bf16)
        onesb = sb("onesb", [128, 128], bf16)
        onesf = sb("onesf", [128, 128])
        lmaskb = sb("lmaskb", [128, W80], bf16)
        rmaskb = sb("rmaskb", [128, 32], bf16)
        xres = sb("xres", [128, NT, D])
        ln = sb("ln", [128, NT, 16])
        mv = sb("mv", [128, NT, 2])
        std = sb("std", [128, NT])
        rstd = sb("rstd", [128, NT])
        eps = sb("eps", [128, 1])
        halfpi = sb("halfpi", [128, 1])
        bqkvo = sb("bqkvo", [128, 3, D])
        bkcol = sb("bkcol", [128, 2])
        small = sb("small", [128, 64])
        Wuq = sb("Wuq", [128, 512]); Wuk = sb("Wuk", [64, 512]); Wuv = sb("Wuv", [64, 512])
        Wout = sb("Wout", [128, 4, 256]); Wdq = sb("Wdq", [128, 2, 128]); Wqr = sb("Wqr", [128, 256])
        Wiq = sb("Wiq", [128, 2, 256]); Wik = sb("Wik", [128, 2, 64]); Wck = sb("Wck", [128, 2, 96])
        iwb = sb("iwb", [128, NI])
        WA = sb("WA", [128, 512])
        WB = sb("WB", [64, H2, 256])
        rdel = sb("rdel", [128, 17])
        trig = sb("trig", [128, 4, 17])
        ctab = sb("ctab", [128, 4, 2 * HALF])
        rtab = sb("rtab", [128, NR])
        tmp32 = sb("tmp32", [128, 4 * HALF])
        WgT = sb("WgT", [128, 2, F], bf16); WuT = sb("WuT", [128, 2, F], bf16); WdT = sb("WdT", [128, 8, D], bf16)
        fstat = sb("fstat", [128, 12])

        ARENA = sb("ARENA", [128, 150016 // 4])
        here = [0]

        def part(shape, dt=fp32, at=None):
            n = int(np.prod(shape)) * (2 if dt == bf16 else 4)
            o = here[0] if at is None else at
            if at is None:
                here[0] += (n + 31) // 32 * 32
                assert here[0] <= 150016, here
            v = ARENA[:, o // 4:(o + n + 3) // 4]
            if dt != fp32:
                v = v.bitcast(dt)
            if len(shape) > 1:
                names = "abcd"[:len(shape)]
                v = v.rearrange(f"p ({' '.join(names)}) -> p {' '.join(names)}",
                                **{k: n_ for k, n_ in zip(names, shape)})
            return v

        V = part([KT, H1, DK + 1])
        Kst = [part([S], bf16) for _ in range(NKST)]
        QA = part([H1, T], bf16)
        kring = [[part([2, CK], bf16) for _ in range(3)] for _ in range(2)]
        kres = part([2, CK])
        ctxr = [part([TPC, D]) for _ in range(4)]
        p_at = here[0]
        Pm = [part([TPC, T]) for _ in range(3)]
        ctxT = [part([2, CK], at=p_at + 4096 * i) for i in range(2)]
        QS = part([NT, H1, SROWS], bf16)
        WQ, WK, WV, WO = (part([2, D]) for _ in range(4))
        xb = part([NT, D])
        xn = part([NT, D], at=p_at + 8192); xnT = part([2, T], at=p_at + 10240)
        mxp = part([2, NT, 8]); nm1 = part([2, NT]); rec1 = part([2, NT])
        O = part([NT, D]); OT = part([2, T])
        fraw = [part([8 * 256], at=here_) for here_ in (p_at - 16384, p_at - 8192)]
        qf = part([NT, D], at=here[0]); q2f = part([NT, D], at=here[0] + 2048)
        fq_a = part([2048], bf16); fq_b = part([2048], bf16)
        WuqT = part([4, 128]); WukT = part([4, 64]); WuvT = part([4, 64])

        here[0] = 0
        DD = part([GR * 16, NR], bf16)
        SR = part([GR, 128], at=0); PR = part([GR * 128], at=GR * 128 * 4)
        e_at = here[0]
        E0 = part([GR * 512], bf16); E1 = part([4 * 512], bf16)
        OC = part([G, 64], at=e_at); OCT = part([H2, T], at=e_at + 4096)
        KGs = part([GR * 512])
        CS = part([GR, 4, DC + 1])
        q_at = here[0]
        QR = part([NT, H2, 128]); QL = part([NT, H2, 96])
        PL = part([G * 128], at=q_at)
        QRT = part([G * 4, H2, 4]); QLT = part([G * 4, H2, 4])
        xn2 = part([NT, D]); xT = part([2, T])
        qiT = part([NI, T]); kiT = part([T]); cqT = part([T])
        CK2 = part([NT, 96]); CW0 = part([DC + 1]); CW = part([GR, DC + 1])
        rl = [part([NI, 96]), part([NI, 192])]
        IX = [part([96]), part([192])]
        topv = part([NT, NR]); topi = part([NT, NR]); topf = part([NT, NR], bf16)
        mu = part([NT, H2 * DR]); mua = part([NT, H2 * DR]); rot = part([NT, H2, HALF])
        rot2 = part([NT, H2, HALF])
        kmu = part([NT, DR]); kmua = part([NT, DR]); krt = part([NT, HALF]); krt2 = part([NT, HALF])
        KA = part([NT, 128]); KAr = part([NT, 128]); KA1, KA2, KA3 = (part([NT, 128], bf16) for _ in range(3))
        KL = part([NT, 96]); KLT = part([T])
        mxl = part([G]); mxr = part([G]); nm2 = part([G]); nmT = part([128]); rec2 = part([G])

        here[0] = 0
        h3 = part([NT, D]); hr = part([NT, D]); hq = part([NT, D], bf16); hqT = part([2, T], bf16)
        sg = part([NT, F]); pr = part([NT, F]); pr2 = part([NT, F]); pq = part([NT, F], bf16)
        pqT = part([8, T], bf16)
        res = part([NT, D])

        ctx_v = a["ctx_1024"].rearrange("b (p t) n -> (b p) t n", p=128)
        x_v = a["x"].rearrange("b (t p) n -> p (b t) n", p=128)
        out_v = out.rearrange("b (t p) n -> p (b t) n", p=128)
        kst_in = [s["kst_in0"], s["kst_in1"], s["kst_in2"]]
        ctx_in = [s["ctx_in0"], s["ctx_in1"], s["ctx_in2"], s["ctx_in3"]]
        kd_out = [s["kd_out0"], s["kd_out1"]]
        fw_in = [s["fw_in0"], s["fw_in1"], s["fw_in2"]]
        NA = 2 * CH
        NB = KT // TPC
        STEPS = H1 * NB
        fw = [a["L0_ffn_w_gate"].rearrange("(t p) n -> p t n", p=128),
              a["L0_ffn_w_up"].rearrange("(t p) n -> p t n", p=128),
              a["L0_ffn_w_down"].rearrange("(t p) n -> p t n", p=128)]
        FHEAD = [3, 6, 9]

        def bank(b, n=1):
            return PS[:, b:b + n, :].rearrange("p a b -> p (a b)")

        def bc(v, shape):
            return v.broadcast_to(shape)

        block = ctx.enter_context(nc.Block())

        @block.sync
        def _(sp):
            sp.dma_start(C[:, :], consts).then_inc(s["const_in"], 16)
            sp.dma_start(xres[:, :, :], x_v).then_inc(s["x_in"], 16)

            def w256(dst, src, sem):
                sp.dma_start(dst, src.rearrange("(c p) n -> p c n", p=128)).then_inc(sem, 16)

            def load_ctx(c):
                if c >= 4:
                    sp.wait_ge(s["ctxT_ps"], c - 3)
                sp.dma_start(ctxr[c % 4], ctx_v[:, c * TPC:(c + 1) * TPC, :]).then_inc(ctx_in[c % 4], 16)

            w256(WQ, a["L0_xattn_W_Q"], s["wq_in"])
            sp.dma_start(bqkvo[:, 0, :], a["L0_xattn_b_Q"].partition_broadcast(128)).then_inc(s["bq_in"], 16)
            load_ctx(0)
            w256(WK, a["L0_xattn_W_K"], s["wkv_in"])
            w256(WV, a["L0_xattn_W_V"], s["wkv_in"])
            for m in range(2):
                sp.dma_start(bkcol[:, m:m + 1], a["L0_xattn_b_K"][128 * m:128 * m + 128].rearrange("(p o) -> p o", o=1))\
                  .then_inc(s["bias_in"], 16)
            sp.dma_start(bqkvo[:, 1, :], a["L0_xattn_b_V"].partition_broadcast(128)).then_inc(s["bias_in"], 16)
            sp.dma_start(bqkvo[:, 2, :], a["L0_xattn_b_O"].partition_broadcast(128)).then_inc(s["bias_in"], 16)
            load_ctx(1)
            load_ctx(2)
            load_ctx(3)
            w256(WO, a["L0_xattn_W_O"], s["wo_in"])
            w256(Wdq[:, :, :], a["L0_attn_W_dq"], s["aw_in"])
            w256(Wiq[:, :, :], a["L0_attn_idx_wq"], s["aw_in"])
            w256(Wik[:, :, :], a["L0_attn_idx_wk"], s["aw_in"])
            w256(Wck[:, :, 0:64], a["L0_attn_W_dkv"], s["aw_in"])
            w256(Wck[:, :, 64:96], a["L0_attn_W_kr"], s["aw_in"])
            sp.dma_start(Wuq[:, :], a["L0_attn_W_uq"]).then_inc(s["aw_in"], 16)
            sp.dma_start(Wqr[:, :], a["L0_attn_W_qr"]).then_inc(s["aw_in"], 16)
            sp.dma_start(Wuk[:, :], a["L0_attn_W_uk"]).then_inc(s["aw_in"], 16)
            sp.dma_start(Wuv[:, :], a["L0_attn_W_uv"]).then_inc(s["aw_in"], 16)
            sp.dma_start(Wout[:, :, :], a["L0_attn_W_out"].rearrange("(c p) n -> p c n", p=128)).then_inc(s["aw_in"], 16)
            sp.dma_start(iwb[:, :], a["L0_attn_idx_w"].partition_broadcast(128)).then_inc(s["aw_in"], 16)
            rd = a["L0_attn_raw_delta"]
            sp.dma_start(rdel[:, 0:16], rd.partition_broadcast(128)).then_inc(s["rd_in"], 16)
            for k in range(8):
                sp.dma_start(rdel[16 * k:16 * k + 16, 16:17], rd.rearrange("(p o) -> p o", o=1)).then_inc(s["rd_in"], 16)

            def store_k(c):
                for n in range(3):
                    sp.wait_ge(s["k1_done"] if n == 0 else s["k23_done"], c + 1 if n == 0 else 2 * c + n)
                    sp.dma_start(kd[n, :, c * CK:(c + 1) * CK].rearrange("(m p) n -> p m n", p=128),
                                 kring[c % 2][n]).then_inc(kd_out[c % 2], 16)

            for c in range(CH):
                if c + 4 < CH:
                    load_ctx(c + 4)
                store_k(c)
            for n in range(2):
                sp.wait_ge(kd_out[n], CH // 2 * 3 * 16)
            for h in range(H1):
                if h >= NKST:
                    sp.wait_ge(s["b_done"], NB * (h - NKST + 1))
                else:
                    sp.wait_ge(s["kst_ones"], NKST)
                for b in range(NBLK):
                    sp.dma_start(Kst[h % NKST][16 * b:16 * b + 16, :], kd[KBLK[b], 16 * h:16 * h + 16, :])\
                      .then_inc(kst_in[h % NKST], 16)
                if h in (1, 2):
                    sp.wait_ge(s["ctxT_ps"], CH)
                    sp.dma_start(fraw[h - 1].rearrange("p (t n) -> p t n", t=8), fw[h - 1]).then_inc(fw_in[h - 1], 16)
            sp.wait_ge(s["fq"], 1)
            sp.dma_start(fraw[0].rearrange("p (t n) -> p t n", t=2), fw[2]).then_inc(s["fw_in2"], 16)
            sp.wait_ge(s["out_done"], 1)
            sp.dma_start(out_v, res).then_inc(s["out_dma"], 16)
            sp.wait_ge(s["out_dma"], 16)

        @block.gpsimd
        def _(pool):
            n_link = [0]

            def link(ins):
                n_link[0] += 1
                ins.then_inc(s["pool_chain"], 1)
                pool.wait_ge(s["pool_chain"], n_link[0])

            pool.memset(eps[:, :], EPS)
            pool.memset(halfpi[:, :], float(np.pi / 2)).then_inc(s["eps_set"], 1)
            pool.memset(V[:, :, :, DK:DK + 1], 1.0).then_inc(s["v_ones"], 1)
            pool.memset(onesf[:, :], 1.0).then_inc(s["fones"], 1)
            pool.memset(onesb[:, :], 1.0).then_inc(s["fones"], 1)
            pool.wait_ge(s["fones"], 2)
            for b in range(NKST):
                pool.memset(Kst[b][QROWS:SROWS, :], 1.0).then_inc(s["kst_ones"], 1)
                pool.wait_ge(s["kst_ones"], b + 1)
            pool.wait_ge(s["x_in"], 16)
            pool.wait_ge(s["bias_in"], 64)
            pool.tensor_tensor(xb, xres[:, :, :], bc(bqkvo[:, 2:3, :], [128, NT, D]), ALU.add).then_inc(s["xb_done"], 1)
            for c in range(CH):
                pool.wait_ge(s["kr_done"], 2 * (c + 1))
                if c >= 2:
                    pool.wait_ge(kd_out[c % 2], 48 * (c // 2))
                pool.tensor_copy(kring[c % 2][1], kres).then_inc(s["k23_done"], 1)
                pool.wait_ge(s["k23_done"], 2 * c + 1)
                pool.tensor_tensor(kring[c % 2][2], kres, kring[c % 2][1], ALU.subtract).then_inc(s["k23_done"], 1)
            pool.wait_ge(s["dl_v"], 1)
            pool.wait_ge(s["const_in"], 16)
            cd = bc(trig[:, 2:3, 0:16], [128, 2, 16])
            sd = bc(trig[:, 3:4, 0:16], [128, 2, 16])
            for n, (cn, sn) in enumerate((("cidx", "sidx"), ("cloc", "sloc"))):
                cc = const(cn).rearrange("p (a b) -> p a b", a=2)
                ss = const(sn).rearrange("p (a b) -> p a b", a=2)
                t1 = tmp32[:, 0:32].rearrange("p (a b) -> p a b", a=2)
                t2 = tmp32[:, 32:64].rearrange("p (a b) -> p a b", a=2)
                oc = ctab[:, 2 * n, :].rearrange("p (a b) -> p a b", a=2)
                os_ = ctab[:, 2 * n + 1, :].rearrange("p (a b) -> p a b", a=2)
                pool.tensor_tensor(t1, cc, cd, ALU.mult)
                link(pool.tensor_tensor(t2, ss, sd, ALU.mult))
                link(pool.tensor_tensor(oc, t1, t2, ALU.subtract))
                pool.tensor_tensor(t1, ss, cd, ALU.mult)
                link(pool.tensor_tensor(t2, cc, sd, ALU.mult))
                link(pool.tensor_tensor(os_, t1, t2, ALU.add))
            link(pool.tensor_copy(rtab[:, :], const("tabx")))
            link(pool.tensor_scalar(rtab[64:128, :], const("tabx")[64:128, :], trig[64:128, 2, 16:17], None, ALU.mult))
            link(pool.tensor_scalar(tmp32[64:128, 0:32], const("taby")[64:128, :], trig[64:128, 3, 16:17], None, ALU.mult))
            pool.tensor_tensor(rtab[64:128, :], rtab[64:128, :], tmp32[64:128, 0:32], ALU.add).then_inc(s["tabs_done"], 1)
            pool.wait_ge(s["tabs_done"], 1)
            for n in range(3):
                w = fraw[n % 2]
                pool.wait_ge(s["fscale"], n + 1)
                if n:
                    pool.wait_ge(s["fqT_ps"], 2 * n)
                sc = fstat[:, 8 + n:9 + n]
                link(pool.tensor_scalar(fq_a, w, sc, 0.5, ALU.mult, ALU.is_gt))
                link(pool.tensor_scalar(fq_b, w, sc, -0.5, ALU.mult, ALU.is_lt))
                pool.tensor_tensor(fq_b, fq_a, fq_b, ALU.subtract).then_inc(s["fq"], 1)

            pool.wait_ge(s["x1_done"], 2)
            pool.memset(CW0[:, DC:DC + 1], 1.0)
            pool.memset(CW[:, :, DC:DC + 1], 1.0)
            pool.memset(CS[:, :, :, DC:DC + 1], 1.0).then_inc(s["cs_ones"], 1)
            pool.wait_ge(s["ck_sb"], 1)
            pool.tensor_copy(KA[:, :, 0:64], CK2[:, :, 0:64])
            pool.tensor_copy(CW0[:, 0:64], CK2[:, 0, 0:64]).then_inc(s["cko_done"], 1)
            pool.tensor_copy(KL[:, :, 0:64], CK2[:, :, 0:64])
            pool.wait_ge(s["kmu_done"], 1)
            pool.tensor_copy(KA[:, :, 64:96], kmu)
            pool.tensor_copy(KA[:, :, 96:112], kmu[:, :, 16:32])
            link(pool.tensor_copy(KA[:, :, 112:128], kmu[:, :, 0:16]))
            link(pool.tensor_copy(KA1, KA))
            link(pool.tensor_tensor(KAr, KA, KA1, ALU.subtract))
            link(pool.tensor_copy(KA2, KAr))
            pool.tensor_tensor(KA3, KAr, KA2, ALU.subtract).then_inc(s["kaug"], 1)
            ci = ctab[:, 0, :].rearrange("p (a b) -> p a b", a=2)
            si = ctab[:, 1, :].rearrange("p (a b) -> p a b", a=2)
            pool.tensor_tensor(krt, kmu[:, :, 0:16], ci, ALU.mult)
            link(pool.tensor_tensor(krt2, kmu[:, :, 16:32], si, ALU.mult))
            link(pool.tensor_tensor(KL[:, :, 64:80], krt, krt2, ALU.subtract))
            pool.tensor_tensor(krt, kmu[:, :, 0:16], si, ALU.mult)
            link(pool.tensor_tensor(krt2, kmu[:, :, 16:32], ci, ALU.mult))
            pool.tensor_tensor(KL[:, :, 80:96], krt, krt2, ALU.add).then_inc(s["krot"], 1)
            pool.wait_ge(s["mu_done"], 1)
            m = mu.rearrange("p t (h d) -> p t h d", h=H2)
            for n, dst in ((1, QL), (0, QR)):
                for tile in range(NT):
                    cc = bc(ctab[:, 2 * n, 16 * tile:16 * tile + 16].unsqueeze(1), [128, H2, 16])
                    ss = bc(ctab[:, 2 * n + 1, 16 * tile:16 * tile + 16].unsqueeze(1), [128, H2, 16])
                    m1, m2 = m[:, tile, :, 0:16], m[:, tile, :, 16:32]
                    r1, r2 = rot[:, tile], rot2[:, tile]
                    pool.tensor_tensor(r1, m1, cc, ALU.mult)
                    link(pool.tensor_tensor(r2, m2, ss, ALU.mult))
                    link(pool.tensor_tensor(dst[:, tile, :, 64:80], r1, r2, ALU.subtract))
                    pool.tensor_tensor(r1, m1, ss, ALU.mult)
                    link(pool.tensor_tensor(r2, m2, cc, ALU.mult))
                    last = pool.tensor_tensor(dst[:, tile, :, 80:96], r1, r2, ALU.add)
                    if n:
                        last.then_inc(s["rot_loc"], 1)
                    else:
                        link(last)
                        pool.tensor_copy(dst[:, tile, :, 96:128], dst[:, tile, :, 64:96]).then_inc(s["rot_rank"], 1)
            for j in range(GR * 16 // 32):
                t0 = 64 + 32 * j
                tile, tt = t0 // 128, t0 % 128
                pool.wait_ge(s["idx_done"], tile + 1)
                pool.tensor_tensor(DD[:, 32 * j:32 * j + 32, :],
                                   bc(identb[:, tt:tt + 32].unsqueeze(2), [128, 32, NR]),
                                   bc(topf[:, tile, :].unsqueeze(1), [128, 32, NR]), ALU.mult).then_inc(s["d_done"], 1)

        @block.scalar
        def _(act):
            n_link = [0]

            def link(ins):
                n_link[0] += 1
                ins.then_inc(s["act_chain"], 1)
                act.wait_ge(s["act_chain"], n_link[0])

            act.wait_ge(s["eps_set"], 1)
            act.wait_ge(s["bq4"], 1)
            act.activation(std[:, :], mv[:, :, 1], ACT.Sqrt, bias=eps[:, :]).then_inc(s["x_std"], 1)
            act.wait_ge(s["xnT_ps"], 1)
            act.activation(xnT, bank(6).rearrange("p (a b) -> p a b", a=2), ACT.Copy).then_inc(s["xnT_sb"], 1)
            act.wait_ge(s["bias_in"], 64)

            def chunk(c):
                act.wait_ge(s["ctxT_ps"], c + 1)
                if c >= 2:
                    act.wait_ge(s["v_ps"], c - 1)
                act.activation(ctxT[c % 2][:, 0, :], bank(0), ACT.Copy).then_inc(s["ctxT_a"], 1)

            def k1(c):
                act.wait_ge(s["kT_ps"], c + 1)
                if c >= 2:
                    act.wait_ge(kd_out[c % 2], 48 * (c // 2))
                for m in range(2):
                    last = act.activation(kring[c % 2][0][:, m, :], bank(2 + m), ACT.Identity, bias=bkcol[:, m:m + 1])
                last.then_inc(s["k1_done"], 1)

            chunk(0)
            for g in range(4):
                act.wait_ge(s["qaT_ps"], g + 1)
                act.activation(QA[0:QROWS, 4 * g:4 * g + 4, :],
                               PS[0:QROWS, 6 + g % 2, :].bitcast(bf16).rearrange("p (a b) -> p a b", a=4),
                               ACT.Copy).then_inc(s["qa_sb"], 1)
            for c in range(CH):
                k1(c)
                if c + 1 < CH:
                    chunk(c + 1)
            act.wait_ge(s["rd_in"], 16 * 9)
            link(act.activation(trig[:, 0, :], rdel[:, :], ACT.Sigmoid))
            act.activation(trig[:, 2, :], trig[:, 0, :], ACT.Sin, scale=float(np.pi)).then_inc(s["dl_sin"], 1)
            act.activation(trig[:, 3, :], trig[:, 0, :], ACT.Sin, scale=-float(np.pi), bias=halfpi[:, :])\
               .then_inc(s["dl_sin"], 1)
            for n, src in enumerate((4, 5, 6)):
                act.wait_ge(s["wuT_ps"], n + 1)
                dst = (WuqT, WukT, WuvT)[n]
                w = dst.shape[2]
                act.activation(dst, bank(src)[:, 0:4 * w].rearrange("p (a b) -> p a b", a=4), ACT.Copy)\
                   .then_inc(s["wuT_sb"], 1)
            act.wait_ge(s["wa_ps"], 1)
            for e in range(2):
                last = act.activation(WA[:, :].rearrange("p (k e n) -> p k e n", e=2, n=64)[:, :, e, :],
                                      bank(7 - e)[:, 0:256].rearrange("p (k n) -> p k n", k=4), ACT.Copy)
            last.then_inc(s["wa_sb"], 1)
            act.wait_ge(s["wb_ps"], 1)
            for e in range(2):
                last = act.activation(WB[:, :, :].rearrange("p (k e) n -> p k e n", e=2)[:, :, e, :],
                                      PS[0:64, 2 + 2 * e:4 + 2 * e, :].rearrange("p a (b n) -> p (a b) n", b=2), ACT.Copy)
            last.then_inc(s["wb_sb"], 1)
            for n in range(STEPS):
                act.wait_ge(s["b_done"], n + 1)
                if n >= 3:
                    act.wait_ge(s["pv_done"], n - 2)
                b = 2 + 2 * (n % 2)
                act.activation(Pm[n % 3], PS[:, b:b + 2, :].rearrange("p a (b n) -> p (a b) n", b=2), ACT.Exp)\
                   .then_inc(s["exp_done"], 1)
            act.wait_ge(s["oT_ps"], 1)
            act.activation(OT, bank(0).rearrange("p (a b) -> p a b", a=2), ACT.Copy).then_inc(s["oT_sb"], 1)

            act.wait_ge(s["x1_done"], 2)
            act.activation(std[:, :], mv[:, :, 1], ACT.Sqrt, bias=eps[:, :]).then_inc(s["std2"], 1)
            act.wait_ge(s["xT2_ps"], 1)
            act.activation(xT, bank(0).rearrange("p (a b) -> p a b", a=2), ACT.Copy).then_inc(s["xT2_sb"], 1)
            act.wait_ge(s["qi_ps"], 1)
            act.activation(qiT[0:64], PS[0:64, 1:3, :].rearrange("p a (b n) -> p (a b) n", b=2), ACT.Copy)\
               .then_inc(s["qi_sb"], 1)
            act.wait_ge(s["cq_ps"], 1)
            act.activation(cqT, bank(5)[:, 0:256], ACT.Copy).then_inc(s["cq_sb"], 1)
            for n in range(2):
                act.wait_ge(s["ix0_ps"] if n == 0 else s["ix1_ps"], 1)
                src = bank(0)[:, 0:384].rearrange("p (a b) -> p a b", a=4) if n == 0 else \
                    bank(1, 2).rearrange("p (a b) -> p a b", a=4)[:, :, 0:192]
                act.activation(rl[n], src, ACT.Relu).then_inc(s["relu0"] if n == 0 else s["relu1"], 1)
            act.wait_ge(s["ck_sb"], 1)
            link(act.activation(kmua, CK2[:, :, 64:96], ACT.Abs))
            link(act.activation(kmua, kmua, ACT.Exp, scale=-1.0))
            act.wait_ge(s["mu_ps"], 1)
            link(act.activation(mua, bank(7).rearrange("p (a b) -> p a b", a=2), ACT.Abs))
            link(act.activation(mua, mua, ACT.Exp, scale=-1.0))
            act.activation(kmua, kmua, ACT.Ln, bias=1.0).then_inc(s["kmu_ln"], 1)
            act.activation(mua, mua, ACT.Ln, bias=1.0).then_inc(s["mu_ln"], 1)
            act.wait_ge(s["cs_ones"], 1)
            act.wait_ge(s["cw_ps"], 1)
            act.activation(CW[0:W80, :, 0:64], PS[0:W80, 6:8, :].rearrange("p a (b n) -> p (a b) n", b=8)[:, 0:GR, :],
                           ACT.Copy).then_inc(s["cw_sb"], 1)
            for tile in range(NT):
                act.wait_ge(s["qa2_ps"], tile + 1)
                src = bank(3 + 2 * tile).rearrange("p (h n) -> p h n", h=H2)
                act.activation(QL[:, tile, :, 0:64], src, ACT.Copy)
                act.activation(QR[:, tile, :, 0:64], src, ACT.Copy).then_inc(s["qa2_sb"], 1)
            act.wait_ge(s["klT_ps"], 1)
            act.activation(KLT[0:96], bank(4)[0:96, 0:256], ACT.Copy).then_inc(s["klT_sb"], 1)
            for n in range(8):
                act.wait_ge(s["qrT_ps"], n + 1)
                loc, tile, hh = n < 4, n % 4 // 2, n % 2
                rows = 96 if loc else 128
                dst = (QLT if loc else QRT)[0:rows, 32 * tile:32 * tile + 32, 4 * hh:4 * hh + 4, :]\
                    .rearrange("p c h q -> p h c q")
                src = PS[0:rows, (0, 1, 2, 7)[n % 4], :].rearrange("p (h c q) -> p h c q", h=4, c=32)
                act.activation(dst, src, ACT.Copy).then_inc(s["qrT_sb"], 1)
            for c in range(GR):
                act.wait_ge(s["cs_ps"], c + 1)
                act.activation(CS[:, c, :, 0:64], bank(4 + c % 2)[:, 0:256].rearrange("p (a b) -> p a b", a=4),
                               ACT.Copy).then_inc(s["cs_sb"], 1)
            act.wait_ge(s["sr_ps"], 3)
            for b in range(3):
                act.activation(SR[:, 4 * b:4 * b + 4, :], bank(b).rearrange("p (a n) -> p a n", a=4), ACT.Copy)\
                   .then_inc(s["sr_sb"], 1)
            act.wait_ge(s["nmT_ps"], 1)
            act.activation(nmT[0:16], bank(7)[0:16, 0:128], ACT.Copy).then_inc(s["nmT_sb"], 1)
            for b in range(4):
                act.wait_ge(s["st_ps"], b + 1)
                w = KK if b == 0 else W80
                act.activation(PL[0:w, 512 * b:512 * b + 512], bank(3 + b)[0:w, :], ACT.Exp, scale=SCALE2)\
                   .then_inc(s["p_loc"], 1)
            for b in range(3):
                act.wait_ge(s["st_ps"], 5 + b)
                act.activation(PR[:, 512 * b:512 * b + 512], bank(b), ACT.Exp, scale=SCALE2).then_inc(s["p_rank"], 1)
            for b in range(4):
                act.wait_ge(s["ocT_ps"], b + 1)
                act.activation(OCT[0:64, :, 64 * b:64 * b + 64].rearrange("p h (c q) -> p c h q", q=4),
                               bank(3 + b)[0:64, :].rearrange("p (c h q) -> p c h q", c=16, h=H2), ACT.Copy)\
                   .then_inc(s["ocT_sb"], 1)

            act.wait_ge(s["x2_done"], 2)
            act.activation(std[:, :], mv[:, :, 1], ACT.Sqrt, bias=eps[:, :]).then_inc(s["std3"], 1)
            act.wait_ge(s["hqT_ps"], 1)
            act.activation(hqT, PS[:, 0, 0:256].bitcast(bf16).rearrange("p (a b) -> p a b", a=2), ACT.Copy)\
               .then_inc(s["hqT_sb"], 1)
            for tile in range(NT):
                act.wait_ge(s["gu_ps"], 2 * tile + 1)
                act.wait_ge(s["dq"], 2 * tile + 2)
                act.activation(sg[:, tile, :], bank(4 * tile, 2), ACT.Silu, scale=small[:, 4 + tile:5 + tile])\
                   .then_inc(s["silu"], 1)
            for tile in range(NT):
                act.wait_ge(s["pqT_ps"], tile + 1)
                act.activation(pqT[:, :, 128 * tile:128 * tile + 128],
                               PS[:, tile, :].bitcast(bf16).rearrange("p (a b) -> p a b", a=8), ACT.Copy)\
                   .then_inc(s["pqT_sb"], 1)

        @block.tensor
        def _(pe):
            def mm(o, l, r, start=True, stop=True, shared=False):
                return pe.matmul(o, l, r, start=start, stop=stop, skip_group_check=shared)

            pe.wait_ge(s["const_in"], 16)
            for tile in range(NT):
                pe.wait_ge(s["xn_done"], tile + 1)
                for c in range(2):
                    last = pe.transpose(bank(6)[:, 256 * c + 128 * tile:256 * c + 128 * tile + 128],
                                        xn[:, tile, 128 * c:128 * c + 128], ident)
            last.then_inc(s["xnT_ps"], 1)
            pe.wait_ge(s["xnT_sb"], 1)
            pe.wait_ge(s["wq_in"], 16)
            for tile in range(NT):
                for c in range(2):
                    last = mm(bank(7)[:, 256 * tile:256 * tile + 256], xnT[:, c, 128 * tile:128 * tile + 128],
                              WQ[:, c, :], start=c == 0, stop=c == 1)
            last.then_inc(s["q_ps"], 1)

            def transpose_ctx(c):
                pe.wait_ge(ctx_in[c % 4], 16 * (c // 4 + 1))
                if c:
                    pe.wait_ge(s["ctxT_a"], c)
                    pe.wait_ge(s["ctxT_v"], c)
                for cc in range(2):
                    for k in range(TPC):
                        last = pe.transpose(bank(cc)[:, 128 * k:128 * k + 128],
                                            ctxr[c % 4][:, k, 128 * cc:128 * cc + 128], ident)
                last.then_inc(s["ctxT_ps"], 1)

            def project_k(c):
                pe.wait_ge(s["ctxT_a"], c + 1)
                pe.wait_ge(s["ctxT_v"], c + 1)
                if c == 0:
                    pe.wait_ge(s["wkv_in"], 32)
                else:
                    pe.wait_ge(s["kr_done"], 2 * c)
                for m in range(2):
                    for cc in range(2):
                        last = mm(bank(2 + m), WK[:, cc, 128 * m:128 * m + 128], ctxT[c % 2][:, cc, :],
                                  start=cc == 0, stop=cc == 1)
                last.then_inc(s["kT_ps"], 1)

            def project_v(c):
                if c:
                    pe.wait_ge(s["v_done"], c)
                for k in range(TPC):
                    for cc in range(2):
                        last = mm(bank(4 + k // 2)[:, 256 * (k % 2):256 * (k % 2) + 256],
                                  ctxT[c % 2][:, cc, 128 * k:128 * k + 128], WV[:, cc, :], start=cc == 0, stop=cc == 1)
                last.then_inc(s["v_ps"], 1)

            transpose_ctx(0)
            pe.wait_ge(s["qs_done"], 1)
            pe.wait_ge(s["ident_b"], 1)
            for g in range(4):
                if g >= 2:
                    pe.wait_ge(s["qa_sb"], g - 1)
                o = PS[:, 6 + g % 2, :].bitcast(bf16)
                for h in range(4):
                    for tile in range(NT):
                        n = 256 * h + 128 * tile
                        last = pe.transpose(o[0:QROWS, n:n + 128], QS[:, tile, 4 * g + h, 0:QROWS], identb[:, :])
                last.then_inc(s["qaT_ps"], 1)
            for c in range(CH):
                project_k(c)
                if c + 1 < CH:
                    transpose_ctx(c + 1)
                project_v(c)

            pe.wait_ge(s["aw_in"], 16 * 11)
            pe.wait_ge(s["v_done"], CH)
            for k in range(4):
                last = pe.transpose(bank(4)[:, 128 * k:128 * k + 128], Wuq[:, 128 * k:128 * k + 128], ident)
            last.then_inc(s["wuT_ps"], 1)
            for n, w in enumerate((Wuk, Wuv)):
                if n == 1:
                    pe.wait_ge(s["qa_sb"], 4)
                for k in range(4):
                    last = pe.transpose(bank(5 + n)[:, 64 * k:64 * k + 64], w[:, 128 * k:128 * k + 128], ident[0:64, 0:64])
                last.then_inc(s["wuT_ps"], 1)
            pe.wait_ge(s["wuT_sb"], 3)
            pe.wait_ge(s["kr_done"], 2 * CH)
            for h in range(H2):
                lo, k = 64 * (h % 2), h // 2
                last = mm(bank(7 - h % 2)[:, 64 * k:64 * k + 64], WuqT[lo:lo + 64, k, :], WukT[lo:lo + 64, k, :])
            last.then_inc(s["wa_ps"], 1)
            for h in range(H2):
                lo, k = 64 * (h % 2), h // 2
                last = mm(PS[0:64, 2 + 2 * (h % 2) + k // 2, 256 * (k % 2):256 * (k % 2) + 256], WuvT[lo:lo + 64, k, :],
                          Wout[lo:lo + 64, k, :])
            last.then_inc(s["wb_ps"], 1)
            pe.wait_ge(s["ctxT_v"], CH)
            pe.wait_ge(s["wa_sb"], 1)
            pe.wait_ge(s["wb_sb"], 1)

            def a_unit(h, u):
                n = NA * h + u
                if u == 0:
                    pe.wait_ge(kst_in[h % NKST], 16 * NBLK * (h // NKST + 1))
                if n >= 2:
                    pe.wait_ge(s["a_read"], n - 1)
                tile, c = u // CH, u % CH
                mm(bank(n % 2), QA[0:QROWS, h, 128 * tile:128 * tile + 128],
                   Kst[h % NKST][0:QROWS, CK * c:CK * c + CK]).then_inc(s["a_done"], 1)

            def max_rows(h):
                pe.wait_ge(s["m_split"], 2 * h + 2)
                if h >= 2:
                    pe.wait_ge(s["o_read"], h - 1)
                o = PS[:, 6 + h % 2, :].bitcast(bf16)
                for tile in range(NT):
                    last = pe.transpose(o[0:SROWS, 128 * tile:128 * tile + 128], QS[:, tile, h, :], identb[:, :])
                last.then_inc(s["mT_ps"], 1)

            def b_step(h, st):
                n = NB * h + st
                if st == 0:
                    pe.wait_ge(s["m_ready"], h + 1)
                if n >= 2:
                    pe.wait_ge(s["exp_done"], n - 1)
                for k in range(TPC):
                    b = 2 + 2 * (n % 2) + k // 2
                    key = 128 * (TPC * st + k)
                    last = mm(bank(b)[:, 256 * (k % 2):256 * (k % 2) + 256], Kst[h % NKST][0:SROWS, key:key + 128],
                              QA[0:SROWS, h, :])
                last.then_inc(s["b_done"], 1)

            def pv_step(n):
                h, st = n // NB, n % NB
                pe.wait_ge(s["exp_done"], n + 1)
                for k in range(TPC):
                    for tile in range(NT):
                        last = mm(PS[:, 6 + h % 2, 32 * tile:32 * tile + DK + 1], Pm[n % 3][:, k, 128 * tile:128 * tile + 128],
                                  V[:, TPC * st + k, h, :], start=st == 0 and k == 0 and tile == 0,
                                  stop=st == NB - 1 and k == TPC - 1, shared=True)
                last.then_inc(s["pv_done"], 1)

            for u in range(NA):
                a_unit(0, u)
            max_rows(0)
            for h in range(H1):
                u = 0
                for st in range(NB):
                    if h + 1 < H1:
                        for _ in range(ASCHED[st]):
                            a_unit(h + 1, u)
                            u += 1
                    b_step(h, st)
                    if st == NB - 1 and h + 1 < H1:
                        max_rows(h + 1)
                    if NB * h + st:
                        pv_step(NB * h + st - 1)
            pv_step(STEPS - 1)

            pe.wait_ge(s["o_read"], H1)
            pe.wait_ge(s["a_read"], NA * H1)
            for tile in range(NT):
                for c in range(2):
                    last = pe.transpose(bank(0)[:, 256 * c + 128 * tile:256 * c + 128 * tile + 128],
                                        O[:, tile, 128 * c:128 * c + 128], ident)
            last.then_inc(s["oT_ps"], 1)
            pe.wait_ge(s["oT_sb"], 1)
            pe.wait_ge(s["wo_in"], 16)
            for tile in range(NT):
                for c in range(2):
                    last = mm(bank(2 + tile)[:, 0:256], OT[:, c, 128 * tile:128 * tile + 128], WO[:, c, :],
                              start=c == 0, stop=c == 1)
                last.then_inc(s["y1_ps"], 1)

            pe.wait_ge(s["fones"], 2)
            for n in range(3):
                pe.wait_ge(s["fsum"], n + 1)
                mm(PS[:, 4, n:n + 1], onesf[:, :], fstat[:, n:n + 1]).then_inc(s["fsum_ps"], 1)
                for half in range(2):
                    pe.wait_ge(s["fq"], n + 1)
                    o = PS[:, 5 + half, :].bitcast(bf16)
                    if n:
                        pe.wait_ge(s["fqT_sb"], 2 * n - 1 + half)
                    for k in range(8):
                        if n < 2:
                            src = fq_b[:, 256 * k + 128 * half:256 * k + 128 * half + 128]
                        else:
                            src = fq_b[:, 1024 * half + 128 * k:1024 * half + 128 * k + 128]
                        last = pe.transpose(o[:, 128 * k:128 * k + 128], src, identb[:, :])
                    last.then_inc(s["fqT_ps"], 1)

            for tile in range(NT):
                pe.wait_ge(s["xn2"], tile + 1)
                for c in range(2):
                    last = pe.transpose(bank(0)[:, 256 * c + 128 * tile:256 * c + 128 * tile + 128],
                                        xn2[:, tile, 128 * c:128 * c + 128], ident)
            last.then_inc(s["xT2_ps"], 1)
            pe.wait_ge(s["xT2_sb"], 1)
            for h in range(NI):
                for c in range(2):
                    last = mm(PS[0:64, 1 + h // 2, 256 * (h % 2):256 * (h % 2) + 256], Wiq[:, c, 64 * h:64 * h + 64],
                              xT[:, c, :], start=c == 0, stop=c == 1)
            last.then_inc(s["qi_ps"], 1)
            for c in range(2):
                last = mm(PS[0:64, 3, 0:256], Wik[:, c, :], xT[:, c, :], start=c == 0, stop=c == 1)
            last.then_inc(s["ki_ps"], 1)
            for tile in range(NT):
                for c in range(2):
                    last = mm(bank(4)[:, 96 * tile:96 * tile + 96], xT[:, c, 128 * tile:128 * tile + 128], Wck[:, c, :],
                              start=c == 0, stop=c == 1)
            last.then_inc(s["ck_ps"], 1)
            for c in range(2):
                last = mm(bank(5)[:, 0:256], Wdq[:, c, :], xT[:, c, :], start=c == 0, stop=c == 1)
            last.then_inc(s["cq_ps"], 1)
            pe.wait_ge(s["qi_sb"], 1)
            pe.wait_ge(s["ki_sb"], 1)
            for h in range(NI):
                last = mm(bank(0)[:, 96 * h:96 * h + 96], qiT[0:64, h, 0:128], kiT[0:64, 0:96])
            last.then_inc(s["ix0_ps"], 1)
            for h in range(NI):
                last = mm(bank(1 + h // 2)[:, 256 * (h % 2):256 * (h % 2) + 192], qiT[0:64, h, 128:256], kiT[0:64, 0:192])
            last.then_inc(s["ix1_ps"], 1)
            pe.wait_ge(s["cq_sb"], 1)
            pe.wait_ge(s["fqT_sb"], 6)
            for tile in range(NT):
                last = mm(bank(7)[:, 256 * tile:256 * tile + 256], cqT[:, 128 * tile:128 * tile + 128], Wqr[:, :])
            last.then_inc(s["mu_ps"], 1)
            for tile in range(NT):
                mm(bank(3 + 2 * tile), cqT[:, 128 * tile:128 * tile + 128], WA[:, :]).then_inc(s["qa2_ps"], 1)
            pe.wait_ge(s["mu_done"], 1)
            for g in range(GR):
                for c in range(2):
                    last = mm(PS[0:W80, 6 + g // 8, 64 * (g % 8):64 * (g % 8) + 64], xT[:, c, 16 * g:16 * g + W80],
                              Wck[:, c, 0:64], start=c == 0, stop=c == 1)
            last.then_inc(s["cw_ps"], 1)
            pe.wait_ge(s["krot"], 1)
            pe.wait_ge(s["ck_sb"], 1)
            for tile in range(NT):
                last = pe.transpose(bank(4)[0:96, 128 * tile:128 * tile + 128], KL[:, tile, :], ident)
            last.then_inc(s["klT_ps"], 1)
            pe.wait_ge(s["relu0"], 1)
            pe.wait_ge(s["relu1"], 1)
            pe.wait_ge(s["cw_sb"], 1)
            for n in range(8):
                loc, tile, hh = n < 4, n % 4 // 2, n % 2
                pe.wait_ge(s["rot_loc"] if loc else s["rot_rank"], tile + 1)
                pe.wait_ge(s["qa2_sb"], tile + 1)
                if n >= 4:
                    pe.wait_ge(s["qrT_sb"], n - 3)
                rows = 96 if loc else 128
                for h in range(4):
                    last = pe.transpose(PS[0:rows, (0, 1, 2, 7)[n % 4], 128 * h:128 * h + 128],
                                        (QL if loc else QR)[:, tile, 4 * hh + h, :], ident)
                last.then_inc(s["qrT_ps"], 1)
            pe.wait_ge(s["qrT_sb"], 4)
            pe.wait_ge(s["klT_sb"], 1)
            qlt = QLT.rearrange("p c h q -> p (c h q)")
            qrt = QRT.rearrange("p c h q -> p (c h q)")
            for g in range(G):
                w, k0 = (KK, 0) if g < 4 else (W80, 16 * g - LW)
                o = bank(3 + g // 4)[:, 128 * (g % 4):128 * (g % 4) + w]
                if g >= 4:
                    mm(o, identb[:, :], lmaskb[:, :], start=g % 4 == 0, stop=False, shared=True)
                last = mm(o, qlt[0:96, 128 * g:128 * g + 128], KLT[0:96, k0:k0 + w],
                          start=g < 4 and g % 4 == 0, stop=True, shared=True)
                if g % 4 == 3:
                    last.then_inc(s["sl_ps"], 1)
            pe.wait_ge(s["kaug"], 1)
            pe.wait_ge(s["qrT_sb"], 8)
            pe.wait_ge(s["sl_max"], 4)
            DDf = DD.rearrange("p t r -> p (t r)")
            for c in range(GR + 1):
                if c < GR:
                    pe.wait_ge(s["d_done"], c // 2 + 1)
                    if c >= 2:
                        pe.wait_ge(s["e_done"], c - 1)
                    mm(bank(c % 2), onesb[:, :], DDf[:, 512 * c:512 * c + 512]).then_inc(s["bc_ps"], 1)
                if c:
                    g = c - 1
                    pe.wait_ge(s["e_done"], g + 1)
                    if g >= 2:
                        pe.wait_ge(s["kg_sb"], g - 1)
                        pe.wait_ge(s["cs_sb"], g - 1)
                    terms = [(E0[:, 512 * g:512 * g + 512], 0)]
                    if g >= 8:
                        terms.append((E1[:, 512 * (g - 8):512 * (g - 8) + 512], 1))
                    todo = [(e, tile, k) for e, tile in terms for k in (KA1, KA2, KA3)]
                    for n, (e, tile, k) in enumerate(todo):
                        last = mm(bank(2 + g % 2), k[:, tile, :], e, start=n == 0, stop=n == len(todo) - 1)
                    last.then_inc(s["kg_ps"], 1)
                    for cc in range(4):
                        for n, (e, tile, k) in enumerate(todo):
                            last = mm(bank(4 + g % 2)[:, 64 * cc:64 * cc + 64], e[:, 128 * cc:128 * cc + 128],
                                      k[:, tile, 0:64], start=n == 0, stop=n == len(todo) - 1)
                    last.then_inc(s["cs_ps"], 1)
            pe.wait_ge(s["kg_sb"], GR)
            rmb = bc(rmaskb[:, :].unsqueeze(1), [128, 16, 32])
            for b in range(3):
                mm(bank(b).rearrange("p (a n) -> p a n", a=16), identb[:, :], rmb, start=True, stop=False, shared=True)
                for k in range(16):
                    col = 16 * b + k
                    last = mm(bank(b)[:, 32 * k:32 * k + 32], KGs[:, 128 * col:128 * col + 128],
                              qrt[:, 32 * (col + 16):32 * (col + 16) + 32], start=False, stop=False, shared=True)
                last.then_inc(s["sr_ps"], 1)
            pe.wait_ge(s["cs_sb"], GR)
            for gi in range(GR):
                pe.wait_ge(s["sr_sb"], gi // 4 + 1)
                last = pe.transpose(bank(3 + gi // 4)[:, 128 * (gi % 4):128 * (gi % 4) + 128], SR[:, gi, :], ident)
                if gi % 4 == 3:
                    last.then_inc(s["srT_ps"], 1)
            pe.wait_ge(s["nm_done"], 1)
            pe.transpose(bank(7)[0:16, 0:128], nm2, ident).then_inc(s["nmT_ps"], 1)
            pe.wait_ge(s["sr_max"], 3)
            for g in range(G):
                w, k0 = (KK, 0) if g < 4 else (W80, 16 * g - LW)
                o = PS[0:w, 3 + g // 4, 128 * (g % 4):128 * (g % 4) + 128]
                if g >= 4:
                    mm(o, lmaskb[:, :], identb[:, :], start=g % 4 == 0, stop=False, shared=True)
                mm(o, KLT[0:96, k0:k0 + w], qlt[0:96, 128 * g:128 * g + 128], start=g < 4 and g % 4 == 0, stop=False,
                   shared=True)
                if g == 0:
                    pe.wait_ge(s["nmT_sb"], 1)
                last = mm(o, bc(ident[0:16, g:g + 1], [16, w]), nmT[0:16], start=False, stop=True, shared=True)
                if g % 4 == 3:
                    last.then_inc(s["st_ps"], 1)
            for gi in range(GR):
                last = mm(bank(gi // 4)[:, 128 * (gi % 4):128 * (gi % 4) + 128], bc(ident[0:16, 4 + gi:5 + gi], [16, 128]),
                          nmT[0:16], start=False, stop=True, shared=True)
                if gi % 4 == 3:
                    last.then_inc(s["st_ps"], 1)
            pe.wait_ge(s["cko_done"], 1)
            for g in range(G):
                bo = (7, 0, 1, 2)[g // 4]
                o = bank(bo)[:, 128 * (g % 4):128 * (g % 4) + DC + 1]
                w = KK if g < 4 else W80
                pe.wait_ge(s["p_loc"], g // 4 + 1)
                if g >= 4:
                    pe.wait_ge(s["p_rank"], 3)
                mm(o, PL[0:w, 128 * g:128 * g + 128], CW0[0:KK] if g < 4 else CW[0:W80, g - 4, :],
                   start=g % 4 == 0, stop=g < 4, shared=True)
                last = None
                if g >= 4:
                    for cc in range(4):
                        n = 128 * (g - 4) + 32 * cc
                        last = mm(PS[32 * cc:32 * cc + 32, bo, 128 * (g % 4):128 * (g % 4) + DC + 1], PR[:, n:n + 32],
                                  CS[:, g - 4, cc, :], start=False, stop=True, shared=True)
                if g == 3:
                    pass
                if g % 4 == 3:
                    if last is None:
                        last = pe.transpose(bank(3)[0:16, 0:128], nm2, ident)
                    last.then_inc(s["pv2_ps"], 1)
            for g in range(G):
                pe.wait_ge(s["oc_done"], g // 4 + 1)
                last = pe.transpose(PS[0:64, 3 + g // 4, 128 * (g % 4):128 * (g % 4) + 128], OC[:, g, :], ident)
                if g % 4 == 3:
                    last.then_inc(s["ocT_ps"], 1)
            for tile in range(NT):
                pe.wait_ge(s["ocT_sb"], 2 * tile + 2)
                for h in range(H2):
                    last = mm(bank(tile)[:, 0:256], OCT[0:64, h, 128 * tile:128 * tile + 128], WB[:, h, :],
                              start=h == 0, stop=h == H2 - 1)
                last.then_inc(s["y2_ps"], 1)

            for tile in range(NT):
                pe.wait_ge(s["hq_done"], tile + 1)
                for c in range(2):
                    o = PS[:, 0, :].bitcast(bf16)
                    last = pe.transpose(o[:, 256 * c + 128 * tile:256 * c + 128 * tile + 128],
                                        hq[:, tile, 128 * c:128 * c + 128], identb[:, :])
            last.then_inc(s["hqT_ps"], 1)
            pe.wait_ge(s["hqT_sb"], 1)
            for tile in range(NT):
                for k, w in enumerate((WgT, WuT)):
                    for half in range(2):
                        for c in range(2):
                            last = mm(bank(4 * tile + 2 * k + half), hqT[:, c, 128 * tile:128 * tile + 128],
                                      w[:, c, 512 * half:512 * half + 512], start=c == 0, stop=c == 1)
                    last.then_inc(s["gu_ps"], 1)
            for tile in range(NT):
                pe.wait_ge(s["pq_done"], tile + 1)
                o = PS[:, tile, :].bitcast(bf16)
                for k in range(8):
                    last = pe.transpose(o[:, 128 * k:128 * k + 128], pq[:, tile, 128 * k:128 * k + 128], identb[:, :])
                last.then_inc(s["pqT_ps"], 1)
            for tile in range(NT):
                pe.wait_ge(s["pqT_sb"], tile + 1)
                for k in range(8):
                    last = mm(bank(2 + tile)[:, 0:256], pqT[:, k, 128 * tile:128 * tile + 128], WdT[:, k, :],
                              start=k == 0, stop=k == 7)
                last.then_inc(s["y3_ps"], 1)

        @block.vector
        def _(v):
            n_link = [0]

            def link(ins):
                n_link[0] += 1
                ins.then_inc(s["dve_chain"], 1)
                v.wait_ge(s["dve_chain"], n_link[0])

            def stats(tile):
                link(v.bn_stats(ln[:, tile, 0:6], xres[:, tile, :]))
                return v.bn_aggr(mv[:, tile, :], ln[:, tile, 0:6])

            def normalise(dst, std_sem, done):
                v.wait_ge(std_sem, 1)
                link(v.reciprocal(rstd[:, :], std[:, :]))
                for tile in range(NT):
                    v.tensor_scalar(dst[:, tile, :], xres[:, tile, :], mv[:, tile, 0:1], rstd[:, tile:tile + 1],
                                    ALU.subtract, ALU.mult).then_inc(done, 1)

            v.wait_ge(s["x_in"], 16)
            for tile in range(NT):
                link(stats(tile))
            v.wait_ge(s["bq_in"], 16)
            v.tensor_scalar(bqkvo[:, 0, :], bqkvo[:, 0, :], 0.25, None, ALU.mult).then_inc(s["bq4"], 1)
            normalise(xn, s["x_std"], s["xn_done"])
            v.wait_ge(s["const_in"], 16)
            v.tensor_copy(lmaskb[:, :], const("lmask"))
            v.tensor_copy(rmaskb[:, :], const("rmask"))
            v.tensor_copy(identb[:, :], ident).then_inc(s["ident_b"], 1)
            v.wait_ge(s["q_ps"], 1)
            v.wait_ge(s["bq4"], 1)
            link(v.scalar_tensor_tensor(qf, bank(7).rearrange("p (a b) -> p a b", a=2), 0.25,
                                        bc(bqkvo[:, 0:1, :], [128, NT, D]), ALU.mult, ALU.add))

            def blk(b, tile):
                return QS[:, tile, :, 16 * b:16 * b + 16]

            def hd(x_, tile):
                return x_[:, tile, :].rearrange("p (h d) -> p h d", h=H1)

            for b in (0, 3, 5):
                for tile in range(NT):
                    last = v.tensor_copy(blk(b, tile), hd(qf, tile))
            link(last)
            for tile in range(NT):
                last = v.tensor_tensor(hd(q2f, tile), hd(qf, tile), blk(0, tile), ALU.subtract)
            link(last)
            for b in (1, 4):
                for tile in range(NT):
                    last = v.tensor_copy(blk(b, tile), hd(q2f, tile))
            link(last)
            for tile in range(NT):
                last = v.tensor_tensor(blk(2, tile), hd(q2f, tile), blk(1, tile), ALU.subtract)
            last.then_inc(s["qs_done"], 1)

            def ctx_evac(c):
                v.wait_ge(s["ctxT_ps"], c + 1)
                if c >= 2:
                    v.wait_ge(s["v_ps"], c - 1)
                v.tensor_copy(ctxT[c % 2][:, 1, :], bank(1)).then_inc(s["ctxT_v"], 1)

            ctx_evac(0)
            v.wait_ge(s["bias_in"], 64)
            v.wait_ge(s["v_ones"], 1)
            for c in range(CH):
                v.wait_ge(s["k1_done"], c + 1)
                if c:
                    v.wait_ge(s["k23_done"], 2 * c)
                for m in range(2):
                    v.scalar_tensor_tensor(kres[:, m, :], bank(2 + m), bkcol[:, m:m + 1], kring[c % 2][0][:, m, :],
                                           ALU.add, ALU.subtract).then_inc(s["kr_done"], 1)
                if c + 1 < CH:
                    ctx_evac(c + 1)
                v.wait_ge(s["v_ps"], c + 1)
                for k in range(2):
                    last = v.tensor_tensor(V[:, TPC * c + 2 * k:TPC * c + 2 * k + 2, :, 0:DK],
                                           bank(4 + k).rearrange("p (a h d) -> p a h d", a=2, h=H1),
                                           bc(bqkvo[:, 1, :].rearrange("p (h d) -> p h d", h=H1).unsqueeze(1),
                                              [128, 2, H1, DK]), ALU.add)
                last.then_inc(s["v_done"], 1)
            v.wait_ge(s["dl_sin"], 2)
            link(v.tensor_tensor(trig[:, 0, :], trig[:, 2, :], trig[:, 2, :], ALU.mult))
            link(v.tensor_tensor(trig[:, 1, :], trig[:, 2, :], trig[:, 3, :], ALU.mult))
            link(v.tensor_scalar(trig[:, 2, :], trig[:, 0, :], -2.0, 1.0, ALU.mult, ALU.add))
            v.tensor_scalar(trig[:, 3, :], trig[:, 1, :], -2.0, None, ALU.mult).then_inc(s["dl_v"], 1)

            def a_unit(h, u):
                n = NA * h + u
                v.wait_ge(s["a_done"], n + 1)
                return v.tensor_reduce(mxp[:, h % 2, u // CH, u % CH:u % CH + 1], bank(n % 2), axis=AX.X, op=ALU.max)\
                    .then_inc(s["a_read"], 1)

            def max_split(h):
                v.wait_ge(s["a_read"], NA * (h + 1))
                link(v.tensor_reduce(nm1[:, h % 2, :], mxp[:, h % 2, :, :], axis=AX.X, op=ALU.max, negate=True))
                v.tensor_copy(QS[:, :, h, QROWS], nm1[:, h % 2, :]).then_inc(s["m_split"], 1)
                v.wait_ge(s["m_split"], 2 * h + 1)
                v.tensor_tensor(QS[:, :, h, QROWS + 1], nm1[:, h % 2, :], QS[:, :, h, QROWS], ALU.subtract)\
                 .then_inc(s["m_split"], 1)
                v.wait_ge(s["mT_ps"], h + 1)
                v.tensor_copy(QA[QROWS:SROWS, h, :], PS[QROWS:SROWS, 6 + h % 2, 0:128].bitcast(bf16))\
                 .then_inc(s["m_ready"], 1)

            def head_out(h):
                v.wait_ge(s["pv_done"], NB * (h + 1))
                o = PS[:, 6 + h % 2, 0:64].rearrange("p (a b) -> p a b", a=2)
                link(v.reciprocal(rec1[:, h % 2, :], o[:, :, DK]))
                v.tensor_tensor(O[:, :, DK * h:DK * h + DK], o[:, :, 0:DK], bc(rec1[:, h % 2, :].unsqueeze(2), [128, NT, DK]),
                                ALU.mult).then_inc(s["o_read"], 1)

            for u in range(NA):
                a_unit(0, u)
            max_split(0)
            fw_sums = {4: 0, 5: 1, 9: 2}
            for h in range(H1):
                for u in range(NA):
                    if h + 1 < H1:
                        a_unit(h + 1, u)
                    if u == 5 and h:
                        head_out(h - 1)
                if h + 1 < H1:
                    max_split(h + 1)
            head_out(H1 - 1)
            v.wait_ge(s["xb_done"], 1)
            for tile in range(NT):
                v.wait_ge(s["y1_ps"], tile + 1)
                v.tensor_tensor(xres[:, tile, :], bank(2 + tile)[:, 0:256], xb[:, tile, :], ALU.add)\
                 .then_inc(s["dve_chain"], 1)
                n_link[0] += 1
                v.wait_ge(s["dve_chain"], n_link[0])
            for n in range(3):
                v.wait_ge(fw_in[n], 16)
                v.tensor_reduce(fstat[:, n:n + 1], fraw[n % 2], axis=AX.X, op=ALU.add, apply_absolute_value=True)\
                 .then_inc(s["fsum"], 1)
                v.wait_ge(s["fsum_ps"], n + 1)
                link(v.tensor_scalar(fstat[:, 4 + n:5 + n], PS[:, 4, n:n + 1], 1.0 / (F * D), 1e-5, ALU.mult, ALU.max))
                v.reciprocal(fstat[:, 8 + n:9 + n], fstat[:, 4 + n:5 + n]).then_inc(s["fscale"], 1)
                for half in range(2):
                    v.wait_ge(s["fqT_ps"], 2 * n + half + 1)
                    o = PS[:, 5 + half, :].bitcast(bf16)
                    if n < 2:
                        dst, src = (WgT, WuT)[n][:, half, :], o
                    else:
                        dst = WdT[:, :, 128 * half:128 * half + 128]
                        src = o.rearrange("p (a b) -> p a b", a=8)
                    v.tensor_copy(dst, src).then_inc(s["fqT_sb"], 1)

            for tile in range(NT):
                stats(tile).then_inc(s["x1_done"], 1)
            v.wait_ge(s["x1_done"], 2)
            normalise(xn2, s["std2"], s["xn2"])
            v.wait_ge(s["ki_ps"], 1)
            v.tensor_copy(kiT[0:64], PS[0:64, 3, 0:256]).then_inc(s["ki_sb"], 1)
            v.wait_ge(s["ck_ps"], 1)
            v.tensor_copy(CK2, bank(4)[:, 0:192].rearrange("p (a b) -> p a b", a=2)).then_inc(s["ck_sb"], 1)
            v.wait_ge(s["ck_sb"], 1)
            mups = bank(7).rearrange("p (a b) -> p a b", a=2)
            v.wait_ge(s["kmu_ln"], 1)
            v.scalar_tensor_tensor(kmu, CK2[:, :, 64:96], 0.0, kmua, ALU.max, ALU.add).then_inc(s["kmu_done"], 1)
            v.wait_ge(s["mu_ln"], 1)
            v.scalar_tensor_tensor(mu, mups, 0.0, mua, ALU.max, ALU.add).then_inc(s["mu_done"], 1)
            for tile in range(NT):
                v.wait_ge(s["relu0"] if tile == 0 else s["relu1"], 1)
                n = (96, 192)[tile]
                kp = const("keep").rearrange("p (a b) -> p a b", a=2)[:, tile, 0:n]
                fl = const("fill").rearrange("p (a b) -> p a b", a=2)[:, tile, 0:n]
                link(v.tensor_scalar(IX[tile], rl[tile][:, 0, :], iwb[:, 0:1], None, ALU.mult))
                for h in range(1, NI):
                    link(v.scalar_tensor_tensor(IX[tile], rl[tile][:, h, :], iwb[:, h:h + 1], IX[tile], ALU.mult, ALU.add))
                link(v.tensor_tensor(IX[tile], IX[tile], kp, ALU.mult))
                link(v.tensor_tensor(IX[tile], IX[tile], fl, ALU.add))
                for r in range(NR // 8):
                    tv, ti = topv[:, tile, 8 * r:8 * r + 8], topi[:, tile, 8 * r:8 * r + 8].bitcast(u32)
                    link(v.max(tv, IX[tile]))
                    last = v.max_index(ti, tv, IX[tile])
                    link(last)
                    if r < NR // 8 - 1:
                        link(v.match_replace(IX[tile], tv, IX[tile], FMIN))
                v.tensor_copy(topf[:, tile, :], topi[:, tile, :].bitcast(u32)).then_inc(s["idx_done"], 1)
            for b in range(4):
                v.wait_ge(s["sl_ps"], b + 1)
                w = KK if b == 0 else W80
                v.tensor_reduce(mxl[:, 4 * b:4 * b + 4], bank(3 + b).rearrange("p (a n) -> p a n", a=4)[:, :, 0:w],
                                axis=AX.X, op=ALU.max).then_inc(s["sl_max"], 1)
            v.wait_ge(s["tabs_done"], 1)
            for c in range(GR + 1):
                if c < GR:
                    v.wait_ge(s["bc_ps"], c + 1)
                    last = v.tensor_scalar(E0[:, 512 * c:512 * c + 512], bank(c % 2), const("iota")[:, 0:1], None,
                                           ALU.is_equal)
                    if c >= 8:
                        last = v.tensor_scalar(E1[:, 512 * (c - 8):512 * (c - 8) + 512], bank(c % 2),
                                               const("iota")[:, 1:2], None, ALU.is_equal)
                    last.then_inc(s["e_done"], 1)
                if c:
                    g = c - 1
                    v.wait_ge(s["kg_ps"], g + 1)
                    v.tensor_tensor(KGs[:, 512 * g:512 * g + 512].rearrange("p (a r) -> p a r", a=16),
                                    bank(2 + g % 2).rearrange("p (a r) -> p a r", a=16),
                                    bc(rtab[:, :].unsqueeze(1), [128, 16, NR]), ALU.mult).then_inc(s["kg_sb"], 1)
            for b in range(3):
                v.wait_ge(s["srT_ps"], b + 1)
                v.tensor_reduce(mxr[:, 4 * b:4 * b + 4], bank(3 + b).rearrange("p (a n) -> p a n", a=4),
                                axis=AX.X, op=ALU.max).then_inc(s["sr_max"], 1)
            v.wait_ge(s["sr_max"], 3)
            v.wait_ge(s["sl_max"], 4)
            v.tensor_scalar(nm2[:, 0:4], mxl[:, 0:4], -1.0, None, ALU.mult)
            link(v.tensor_tensor(nm2[:, 4:16], mxl[:, 4:16], mxr[:, 0:12], ALU.max))
            v.tensor_scalar(nm2[:, 4:16], nm2[:, 4:16], -1.0, None, ALU.mult).then_inc(s["nm_done"], 1)
            for b in range(4):
                v.wait_ge(s["pv2_ps"], b + 1)
                o = bank((7, 0, 1, 2)[b]).rearrange("p (a n) -> p a n", a=4)
                link(v.reciprocal(rec2[:, 4 * b:4 * b + 4], o[:, :, DC]))
                v.tensor_tensor(OC[:, 4 * b:4 * b + 4, :], o[:, :, 0:64], bc(rec2[:, 4 * b:4 * b + 4].unsqueeze(2), [128, 4, 64]),
                                ALU.mult).then_inc(s["oc_done"], 1)
            for tile in range(NT):
                v.wait_ge(s["y2_ps"], tile + 1)
                link(v.tensor_tensor(xres[:, tile, :], xres[:, tile, :], bank(tile)[:, 0:256], ALU.add))

            for tile in range(NT):
                stats(tile).then_inc(s["x2_done"], 1)
            v.wait_ge(s["x2_done"], 2)
            normalise(h3, s["std3"], s["xn3"])
            v.wait_ge(s["xn3"], 2)

            def quantise(tile, src, work, dst, col, done):
                am, sc, dq = small[:, 16 + tile:17 + tile], small[:, 20 + tile:21 + tile], small[:, col + tile:col + tile + 1]
                link(v.tensor_reduce(am, src, axis=AX.X, op=ALU.max, apply_absolute_value=True))
                link(v.tensor_scalar(am, am, 1e-5, None, ALU.max))
                link(v.reciprocal(sc, am))
                link(v.tensor_scalar(sc, sc, 127.0, None, ALU.mult))
                v.tensor_scalar(dq, am, 1.0 / 127.0, None, ALU.mult)
                link(v.tensor_scalar(work, src, sc, -128.0, ALU.mult, ALU.max))
                link(v.tensor_scalar(work, work, 127.0, MAGIC, ALU.min, ALU.add))
                v.tensor_scalar(dst, work, MAGIC, None, ALU.subtract).then_inc(done, 1)

            for tile in range(NT):
                quantise(tile, h3[:, tile, :], hr[:, tile, :], hq[:, tile, :], 0, s["hq_done"])
                v.wait_ge(s["hq_done"], tile + 1)
                for n in range(2):
                    v.tensor_scalar(small[:, 4 + 2 * n + tile:5 + 2 * n + tile], small[:, tile:tile + 1],
                                    fstat[:, 4 + n:5 + n], None, ALU.mult).then_inc(s["dq"], 1)
            v.wait_ge(s["dq"], 4)
            for tile in range(NT):
                v.wait_ge(s["gu_ps"], 2 * tile + 2)
                v.wait_ge(s["silu"], tile + 1)
                link(v.scalar_tensor_tensor(pr[:, tile, :], bank(4 * tile + 2, 2), small[:, 6 + tile:7 + tile], sg[:, tile, :],
                                            ALU.mult, ALU.mult))
                quantise(tile, pr[:, tile, :], pr2[:, tile, :], pq[:, tile, :], 8, s["pq_done"])
                link(v.tensor_scalar(small[:, 12 + tile:13 + tile], small[:, 8 + tile:9 + tile], fstat[:, 6:7], None, ALU.mult))
            for tile in range(NT):
                v.wait_ge(s["y3_ps"], tile + 1)
                last = v.scalar_tensor_tensor(res[:, tile, :], bank(2 + tile)[:, 0:256], small[:, 12 + tile:13 + tile],
                                              xres[:, tile, :], ALU.mult, ALU.add)
            last.then_inc(s["out_done"], 1)


_INS = ['x', 'ctx_1024', 'L0_xattn_W_Q', 'L0_xattn_b_Q', 'L0_xattn_W_K', 'L0_xattn_b_K', 'L0_xattn_W_V',
        'L0_xattn_b_V', 'L0_xattn_W_O', 'L0_xattn_b_O', 'L0_attn_W_dkv', 'L0_attn_W_uk', 'L0_attn_W_uv',
        'L0_attn_W_dq', 'L0_attn_W_uq', 'L0_attn_W_qr', 'L0_attn_W_kr', 'L0_attn_W_out', 'L0_attn_idx_wq',
        'L0_attn_idx_wk', 'L0_attn_idx_w', 'L0_attn_raw_delta', 'L0_ffn_w_gate', 'L0_ffn_w_up', 'L0_ffn_w_down']


def kernel(**inputs):
    import numpy as _np
    import concourse.bacc as _bacc
    from concourse import mybir as _mybir
    from concourse.bass_utils import run_bass_kernel_spmd as _run

    nc = _bacc.Bacc("TRN2", target_bir_lowering=False, num_devices=1)
    arrays = {"consts_dram": constants()}
    consts = nc.dram_tensor("consts_dram", (128, NCONST), fp32, kind="ExternalInput").ap()
    args = {}
    for name in _INS:
        arr = _np.ascontiguousarray(inputs[name])
        arrays[f"in_{name}_dram"] = arr
        args[name] = nc.dram_tensor(f"in_{name}_dram", arr.shape, _mybir.dt.from_np(arr.dtype), kind="ExternalInput").ap()
    out = nc.dram_tensor("out_0_dram", (1, T, D), fp32, kind="ExternalOutput").ap()
    build(nc, consts, args, out)
    r = _run(nc, [arrays], core_ids=[0])
    return r.results[0]["out_0_dram"]
```

```python
import concourse.bass as bass
from concourse import mybir
from contextlib import ExitStack
import numpy as np

fp32 = mybir.dt.float32
bf16 = mybir.dt.bfloat16
u32 = mybir.dt.uint32
fp16 = mybir.dt.float16
ALU = mybir.AluOpType
ACT = mybir.ActivationFunctionType
AX = mybir.AxisListType

T, D = 256, 256
S = 4096
NT = T // 128
H1, DK = 16, 16
KT = S // 128
CH = 8
CK = S // CH
TPC = KT // CH
NBLK = 6
QROWS = NBLK * DK
SROWS = QROWS + 2
KBLK = [0, 0, 0, 1, 1, 2]
QBLK = [0, 1, 2, 0, 1, 0]
NKST = 3
NP = 4
LAG = 2
VW = 3 * DK + 1
LEAD = 1
H2, DH, DR, DC = 8, 64, 32, 64
NI = 4
HALF = DR // 2
LW, KK = 64, 96
NR = KK - LW
G = T // 16
GR = G - LW // 16
W80 = LW + 16
SCALE2 = (DH + DR) ** -0.5
BIG = 1e30
FMIN = -3.4e38
MAGIC = 12582912.0
F = 1024
EPS = 1e-5

_COLS = [("ident", 128), ("lmask", W80), ("rmask", 32), ("iota", 2), ("cidx", 2 * HALF), ("sidx", 2 * HALF),
         ("cloc", 2 * HALF), ("sloc", 2 * HALF), ("tabx", NR), ("taby", NR), ("keep", 2 * 192), ("fill", 2 * 192), ("vsum", DK + 1)]
COL, NCONST = {}, 0
for _n, _w in _COLS:
    COL[_n] = (NCONST, NCONST + _w)
    NCONST += _w


def constants():
    c = np.zeros((128, NCONST), np.float64)

    def put(name, value):
        a, b = COL[name]
        c[:, a:b] = value.reshape(128, b - a)

    p = np.arange(128)
    put("ident", np.eye(128))
    q = 4 * (p // 32) + p % 4
    j = np.arange(W80)
    put("lmask", np.where((j[None] >= q[:, None] + 1) & (j[None] <= q[:, None] + LW), 0.0, -BIG))
    put("rmask", np.where((p // 32)[:, None] == (np.arange(32) % 4)[None], 0.0, -BIG))
    put("iota", np.stack([p, p + 128], 1).astype(float))
    theta = (np.float32(1.0) / np.float32(10000.0) ** (np.float32(2.0) * np.arange(HALF, dtype=np.float32)
                                                       / np.float32(DR))).astype(np.float32).astype(np.float64)
    t = p[:, None] + 128 * np.arange(2)[None]
    ang = t[:, :, None] * theta
    put("cidx", np.cos(ang)); put("sidx", np.sin(ang))
    ang = (t + np.maximum(0, t - (LW - 1)))[:, :, None] * theta
    put("cloc", np.cos(ang)); put("sloc", np.sin(ang))
    rank = LW + np.arange(NR)
    a = rank[None] * np.tile(theta, 8)[:, None]
    x, y = np.ones((128, NR)), np.zeros((128, NR))
    x[64:96], y[64:96] = np.cos(a[64:96]), -np.sin(a[64:96])
    x[96:112], y[96:112] = -np.sin(a[96:112]), -np.cos(a[96:112])
    x[112:], y[112:] = np.sin(a[112:]), np.cos(a[112:])
    put("tabx", x); put("taby", y)
    keep, fill = np.zeros((128, 2, 192)), np.full((128, 2, 192), -3.3e38)
    s = np.arange(192)
    for tile in range(2):
        past = s[None] <= t[:, tile][:, None] - LW
        keep[:, tile][past] = 1.0
        fill[:, tile][past] = 0.0
    ahead = (s[None] > t[:, 0][:, None]) & (s[None] < KK) | ((t[:, 0] < LW)[:, None] & (s[None] < KK))
    fill[:, 0] = np.where(ahead, -(2e38 + s * 1e35)[None], fill[:, 0])
    put("keep", keep); put("fill", fill)
    vsum = np.zeros((128, DK + 1))
    for n in range(3):
        vsum[16 * n:16 * n + 16, 0:16] = np.eye(16)
    vsum[3 * DK, DK] = 1.0
    put("vsum", vsum)
    return c.astype(np.float32)


SEMS = """const_in x_in wq_in wkv_in bq_in bias_in ctx_in0 ctx_in1 ctx_in2 ctx_in3 wo_in aw_in rd_in fw_in ident_b
    eps_set x_std xn_done xnT_ps xnT_sb q_ps qs_done qaT_ps qa_sb bq4 ctxT_ps ctxT_a ctxT_v kT_ps k1_done
    kr_done kd_out0 kd_out1 v_ps v_ones kst_ones kst_in0 kst_in1 kst_in2 a_done a_read m_split mT_ps m_ready
    b_done exp_done pv_done o_read oT_ps oT_sb y1_ps x1_done xb_done vf_done v1_done vr_done v2_done v3_done
    k2_done k3_done lo_pool lo_dve po_sb comb_ps fabs wuT_ps wuT_sb wa_ps wa_sb wb_ps wb_sb fsum_ps fq fqT_ps
    fqT_sb fones dl_sin dl_v tabs_done std2 xn2 xT2_ps xT2_sb qi_ps qi_sb ki_ps ki_sb ck_ps ck_sb cq_ps cq_sb
    cw_ps cw_sb ix0_ps ix1_ps relu0 relu1 idx_done d_done qa2_ps qa2_sb mu_ps mu_ln mu_done kmu_ln kmu_done
    krot kaug cko_done rot_rank rot_loc klT_ps klT_sb qrT_ps qrT_sb sl_ps sl_max cs_ones bc_ps e_done kg_ps
    kg_sb cs_ps cs_sb sr_ps sr_sb srT_ps sr_max nm_done nmT_ps nmT_sb st_ps p_loc p_rank pv2_ps oc_done ocT_ps
    ocT_sb y2_ps x2_done std3 dq xn3 hq_done hqT_ps hqT_sb gu_ps silu pq_done pqT_ps pqT_sb y3_ps out_done
    out_dma dve_chain act_chain pool_chain""".split()


def build(nc, consts, a, out):
    ctx = ExitStack()
    with ctx:
        def sb(name, shape, dt=fp32):
            return ctx.enter_context(nc.sbuf_tensor(name, shape, dt))

        s = {n: ctx.enter_context(nc.semaphore(n)) for n in SEMS}
        PS = ctx.enter_context(nc.psum_tensor("PS", [128, 8, 512], fp32))
        kd = nc.dram_tensor("k_parts", (3, D, S), bf16, kind="Internal").ap()

        C = sb("C", [128, NCONST])

        def const(name):
            return C[:, COL[name][0]:COL[name][1]]

        ident = const("ident")
        identb = sb("identb", [128, 128], bf16)
        onesb = sb("onesb", [128, 128], bf16)
        onesf = sb("onesf", [128, 128])
        lmaskb = sb("lmaskb", [128, W80], bf16)
        rmaskb = sb("rmaskb", [128, 32], bf16)
        xres = sb("xres", [128, NT, D])
        ln = sb("ln", [128, NT, 16])
        mv = sb("mv", [128, NT, 2])
        std = sb("std", [128, NT])
        rstd = sb("rstd", [128, NT])
        eps = sb("eps", [128, 1])
        halfpi = sb("halfpi", [128, 1])
        bqkvo = sb("bqkvo", [128, 3, D])
        bkcol = sb("bkcol", [128, 2])
        small = sb("small", [128, 64])
        Wuq = sb("Wuq", [128, 512]); Wuk = sb("Wuk", [64, 512]); Wuv = sb("Wuv", [64, 512])
        Wout = sb("Wout", [128, 4, 256]); Wdq = sb("Wdq", [128, 2, 128]); Wqr = sb("Wqr", [128, 256])
        Wiq = sb("Wiq", [128, 2, 256]); Wik = sb("Wik", [128, 2, 64]); Wck = sb("Wck", [128, 2, 96])
        iwb = sb("iwb", [128, NI])
        WA = sb("WA", [128, 512])
        WB = sb("WB", [64, H2, 256])
        rdel = sb("rdel", [128, 17])
        trig = sb("trig", [128, 4, 17])
        ctab = sb("ctab", [128, 4, 2 * HALF])
        rtab = sb("rtab", [128, NR])
        tmp32 = sb("tmp32", [128, 4 * HALF])
        WgT = sb("WgT", [128, 2, F], bf16); WuT = sb("WuT", [128, 2, F], bf16); WdT = sb("WdT", [128, 8, D], bf16)
        fstat = sb("fstat", [128, 12])

        ARENA = sb("ARENA", [128, 160000 // 4])
        here = [0]

        def part(shape, dt=fp32, at=None):
            n = int(np.prod(shape)) * (2 if dt in (bf16, fp16) else 4)
            o = here[0] if at is None else at
            if at is None:
                here[0] += (n + 31) // 32 * 32
                assert here[0] <= 160000, here
            v = ARENA[:, o // 4:(o + n + 3) // 4]
            if dt != fp32:
                v = v.bitcast(dt)
            if len(shape) > 1:
                names = "abcd"[:len(shape)]
                v = v.rearrange(f"p ({' '.join(names)}) -> p {' '.join(names)}",
                                **{k: n_ for k, n_ in zip(names, shape)})
            return v

        V = part([KT, H1, VW], bf16)
        Kst = [part([S], bf16) for _ in range(NKST)]
        QA = part([H1, T], bf16)
        kring = [[part([2, CK], bf16) for _ in range(3)] for _ in range(2)]
        kres = part([2, CK])
        p_at = here[0]
        ctxr = [part([TPC, D]) for _ in range(4)]
        ctxT = [part([2, CK]) for _ in range(2)]
        Pm = [part([TPC, T], at=p_at + 4096 * i) for i in range(NP)]
        Plo = [part([TPC, T], fp16, at=p_at + 4096 * NP + 2048 * i) for i in range(NP)]
        QS = part([NT, H1, SROWS], bf16)
        w_at = here[0]
        WQ, WK, WV, WO = (part([2, D]) for _ in range(4))
        xb = part([NT, D])
        mxp = part([2, NT, 8]); nm1 = part([2, NT]); rec1 = part([2, NT])
        O = part([NT, D], at=w_at); OT = part([2, T], at=w_at + 2048)
        po = [part([T]) for _ in range(2)]
        fraw = [part([8 * 256], at=KT * H1 * VW * 2 + 8192 * i) for i in range(3)]
        f_at = here[0]
        fq = [part([2048], bf16) for _ in range(3)]
        qf = part([NT, D], at=f_at); q2f = part([NT, D], at=f_at + 2048)
        xn = part([NT, D], at=f_at + 4096); xnT = part([2, T], at=f_at + 6144)
        vf = part([TPC, D])
        WuqT = part([4, 128], at=f_at); WukT = part([4, 64], at=f_at + 2048)
        WuvT = part([4, 64], at=f_at + 3072)

        here[0] = 0
        DD = part([GR * 16, NR], bf16)
        SR = part([GR, 128], at=0); PR = part([GR * 128], at=GR * 128 * 4)
        e_at = here[0]
        E0 = part([GR * 512], bf16); E1 = part([4 * 512], bf16)
        OC = part([G, 64], at=e_at); OCT = part([H2, T], at=e_at + 4096)
        KGs = part([GR * 512])
        CS = part([GR, 4, DC + 1])
        q_at = here[0]
        QR = part([NT, H2, 128]); QL = part([NT, H2, 96])
        PL = part([G * 128], at=q_at)
        QRT = part([G * 4, H2, 4]); QLT = part([G * 4, H2, 4])
        xn2 = part([NT, D]); xT = part([2, T])
        qiT = part([NI, T]); kiT = part([T]); cqT = part([T])
        CK2 = part([NT, 96]); CW0 = part([DC + 1]); CW = part([GR, DC + 1])
        rl = [part([NI, 96]), part([NI, 192])]
        IX = [part([96]), part([192])]
        topv = part([NT, NR]); topi = part([NT, NR]); topf = part([NT, NR], bf16)
        mu = part([NT, H2 * DR]); mua = part([NT, H2 * DR]); rot = part([NT, H2, HALF])
        rot2 = part([NT, H2, HALF])
        kmu = part([NT, DR]); kmua = part([NT, DR]); krt = part([NT, HALF]); krt2 = part([NT, HALF])
        KA = part([NT, 128]); KAr = part([NT, 128]); KA1, KA2, KA3 = (part([NT, 128], bf16) for _ in range(3))
        KL = part([NT, 96]); KLT = part([T])
        mxl = part([G]); mxr = part([G]); nm2 = part([G]); nmT = part([128]); rec2 = part([G])

        here[0] = 0
        h3 = part([NT, D]); hr = part([NT, D]); hq = part([NT, D], bf16); hqT = part([2, T], bf16)
        sg = part([NT, F]); pr = part([NT, F]); pr2 = part([NT, F]); pq = part([NT, F], bf16)
        pqT = part([8, T], bf16)
        res = part([NT, D])

        ctx_v = a["ctx_1024"].rearrange("b (p t) n -> (b p) t n", p=128)
        x_v = a["x"].rearrange("b (t p) n -> p (b t) n", p=128)
        out_v = out.rearrange("b (t p) n -> p (b t) n", p=128)
        kst_in = [s["kst_in0"], s["kst_in1"], s["kst_in2"]]
        ctx_in = [s["ctx_in0"], s["ctx_in1"], s["ctx_in2"], s["ctx_in3"]]
        kd_out = [s["kd_out0"], s["kd_out1"]]
        NA = 2 * CH
        NB = KT // TPC
        STEPS = H1 * NB
        UPS = NA // NB
        AHEAD = NA + UPS * LEAD
        fw = [a["L0_ffn_w_gate"].rearrange("(t p) n -> p t n", p=128),
              a["L0_ffn_w_up"].rearrange("(t p) n -> p t n", p=128),
              a["L0_ffn_w_down"].rearrange("(t p) n -> p t n", p=128)]
        FQ_AT = [3, 4, 5]

        def bank(b, n=1):
            return PS[:, b:b + n, :].rearrange("p a b -> p (a b)")

        def bc(v, shape):
            return v.broadcast_to(shape)

        def pool_tiles(n):
            return TPC - 2 if n % 4 == 3 else TPC - 1

        def p_hi(n):
            return Pm[n % NP].rearrange("p a b -> p (a b)").bitcast(bf16).rearrange("p (a b e) -> p a b e", a=TPC, e=2)[:, :, :, 1]

        def vpart(c, n):
            return V[:, TPC * c:TPC * c + TPC, :, DK * n:DK * n + DK]

        vf_v = vf.rearrange("p a (h d) -> p a h d", h=H1)

        block = ctx.enter_context(nc.Block())

        @block.sync
        def _(sp):
            sp.dma_start(C[:, :], consts).then_inc(s["const_in"], 16)
            sp.dma_start(xres[:, :, :], x_v).then_inc(s["x_in"], 16)

            def w256(dst, src, sem):
                sp.dma_start(dst, src.rearrange("(c p) n -> p c n", p=128)).then_inc(sem, 16)

            def load_ctx(c):
                if c >= 4:
                    sp.wait_ge(s["ctxT_ps"], c - 3)
                sp.dma_start(ctxr[c % 4], ctx_v[:, c * TPC:(c + 1) * TPC, :]).then_inc(ctx_in[c % 4], 16)

            w256(WQ, a["L0_xattn_W_Q"], s["wq_in"])
            sp.dma_start(bqkvo[:, 0, :], a["L0_xattn_b_Q"].partition_broadcast(128)).then_inc(s["bq_in"], 16)
            load_ctx(0)
            w256(WK, a["L0_xattn_W_K"], s["wkv_in"])
            w256(WV, a["L0_xattn_W_V"], s["wkv_in"])
            for m in range(2):
                sp.dma_start(bkcol[:, m:m + 1], a["L0_xattn_b_K"][128 * m:128 * m + 128].rearrange("(p o) -> p o", o=1))\
                  .then_inc(s["bias_in"], 16)
            sp.dma_start(bqkvo[:, 1, :], a["L0_xattn_b_V"].partition_broadcast(128)).then_inc(s["bias_in"], 16)
            sp.dma_start(bqkvo[:, 2, :], a["L0_xattn_b_O"].partition_broadcast(128)).then_inc(s["bias_in"], 16)
            load_ctx(1)
            load_ctx(2)
            load_ctx(3)
            w256(WO, a["L0_xattn_W_O"], s["wo_in"])
            w256(Wdq[:, :, :], a["L0_attn_W_dq"], s["aw_in"])
            w256(Wiq[:, :, :], a["L0_attn_idx_wq"], s["aw_in"])
            w256(Wik[:, :, :], a["L0_attn_idx_wk"], s["aw_in"])
            w256(Wck[:, :, 0:64], a["L0_attn_W_dkv"], s["aw_in"])
            w256(Wck[:, :, 64:96], a["L0_attn_W_kr"], s["aw_in"])
            sp.dma_start(Wuq[:, :], a["L0_attn_W_uq"]).then_inc(s["aw_in"], 16)
            sp.dma_start(Wqr[:, :], a["L0_attn_W_qr"]).then_inc(s["aw_in"], 16)
            sp.dma_start(Wuk[:, :], a["L0_attn_W_uk"]).then_inc(s["aw_in"], 16)
            sp.dma_start(Wuv[:, :], a["L0_attn_W_uv"]).then_inc(s["aw_in"], 16)
            sp.dma_start(Wout[:, :, :], a["L0_attn_W_out"].rearrange("(c p) n -> p c n", p=128)).then_inc(s["aw_in"], 16)
            sp.dma_start(iwb[:, :], a["L0_attn_idx_w"].partition_broadcast(128)).then_inc(s["aw_in"], 16)
            rd = a["L0_attn_raw_delta"]
            sp.dma_start(rdel[:, 0:16], rd.partition_broadcast(128)).then_inc(s["rd_in"], 16)
            for k in range(8):
                sp.dma_start(rdel[16 * k:16 * k + 16, 16:17], rd.rearrange("(p o) -> p o", o=1)).then_inc(s["rd_in"], 16)

            def store_k(c):
                for n, done in enumerate((s["k1_done"], s["k2_done"], s["k3_done"])):
                    sp.wait_ge(done, c + 1)
                    sp.dma_start(kd[n, :, c * CK:(c + 1) * CK].rearrange("(m p) n -> p m n", p=128),
                                 kring[c % 2][n]).then_inc(kd_out[c % 2], 16)

            for n in range(3):
                sp.dma_start(fraw[n].rearrange("p (t n) -> p t n", t=8 if n < 2 else 2), fw[n]).then_inc(s["fw_in"], 16)
            for c in range(CH):
                if c + 4 < CH:
                    load_ctx(c + 4)
                store_k(c)
            for n in range(2):
                sp.wait_ge(kd_out[n], CH // 2 * 3 * 16)
            for h in range(H1):
                if h >= NKST:
                    sp.wait_ge(s["b_done"], NB * (h - NKST + 1))
                else:
                    sp.wait_ge(s["kst_ones"], h + 1)
                for b in range(NBLK):
                    sp.dma_start(Kst[h % NKST][16 * b:16 * b + 16, :], kd[KBLK[b], 16 * h:16 * h + 16, :])\
                      .then_inc(kst_in[h % NKST], 16)
            sp.wait_ge(s["out_done"], 1)
            sp.dma_start(out_v, res).then_inc(s["out_dma"], 16)
            sp.wait_ge(s["out_dma"], 16)

        @block.gpsimd
        def _(pool):
            n_link = [0]

            def link(ins):
                n_link[0] += 1
                ins.then_inc(s["pool_chain"], 1)
                pool.wait_ge(s["pool_chain"], n_link[0])

            pool.memset(eps[:, :], EPS)
            pool.memset(halfpi[:, :], float(np.pi / 2)).then_inc(s["eps_set"], 1)
            pool.memset(onesf[:, :], 1.0).then_inc(s["fones"], 1)
            pool.memset(onesb[:, :], 1.0).then_inc(s["fones"], 1)
            pool.memset(V[:, :, :, 3 * DK:VW], 1.0).then_inc(s["v_ones"], 1)
            pool.wait_ge(s["x_in"], 16)
            pool.wait_ge(s["bias_in"], 64)
            pool.tensor_tensor(xb, xres[:, :, :], bc(bqkvo[:, 2:3, :], [128, NT, D]), ALU.add).then_inc(s["xb_done"], 1)
            for c in range(CH):
                pool.wait_ge(s["k2_done"], c + 1)
                if c >= 2:
                    pool.wait_ge(kd_out[c % 2], 48 * (c // 2))
                pool.tensor_tensor(kring[c % 2][2], kres, kring[c % 2][1], ALU.subtract).then_inc(s["k3_done"], 1)
                pool.wait_ge(s["v2_done"], c + 1)
                pool.tensor_tensor(vpart(c, 2), vf_v, vpart(c, 1), ALU.subtract).then_inc(s["v3_done"], 1)
                if c - 1 in FQ_AT:
                    n = FQ_AT.index(c - 1)
                    pool.wait_ge(s["fq"], n + 1)
                    pool.wait_ge(s["v3_done"], c + 1)
                    pool.memset(Kst[n][QROWS:SROWS, :], 1.0).then_inc(s["kst_ones"], 1)
                    pool.wait_ge(s["kst_ones"], n + 1)
            pool.wait_ge(s["dl_v"], 1)
            pool.wait_ge(s["const_in"], 16)
            cd = bc(trig[:, 2:3, 0:16], [128, 2, 16])
            sd = bc(trig[:, 3:4, 0:16], [128, 2, 16])
            for n, (cn, sn) in enumerate((("cidx", "sidx"), ("cloc", "sloc"))):
                cc = const(cn).rearrange("p (a b) -> p a b", a=2)
                ss = const(sn).rearrange("p (a b) -> p a b", a=2)
                t1 = tmp32[:, 0:32].rearrange("p (a b) -> p a b", a=2)
                t2 = tmp32[:, 32:64].rearrange("p (a b) -> p a b", a=2)
                oc = ctab[:, 2 * n, :].rearrange("p (a b) -> p a b", a=2)
                os_ = ctab[:, 2 * n + 1, :].rearrange("p (a b) -> p a b", a=2)
                pool.tensor_tensor(t1, cc, cd, ALU.mult)
                link(pool.tensor_tensor(t2, ss, sd, ALU.mult))
                link(pool.tensor_tensor(oc, t1, t2, ALU.subtract))
                pool.tensor_tensor(t1, ss, cd, ALU.mult)
                link(pool.tensor_tensor(t2, cc, sd, ALU.mult))
                link(pool.tensor_tensor(os_, t1, t2, ALU.add))
            link(pool.tensor_copy(rtab[:, :], const("tabx")))
            link(pool.tensor_scalar(rtab[64:128, :], const("tabx")[64:128, :], trig[64:128, 2, 16:17], None, ALU.mult))
            link(pool.tensor_scalar(tmp32[64:128, 0:32], const("taby")[64:128, :], trig[64:128, 3, 16:17], None, ALU.mult))
            pool.tensor_tensor(rtab[64:128, :], rtab[64:128, :], tmp32[64:128, 0:32], ALU.add).then_inc(s["tabs_done"], 1)
            pool.wait_ge(s["tabs_done"], 1)
            for n in range(STEPS):
                pool.wait_ge(s["exp_done"], n + 1)
                k = pool_tiles(n)
                pool.tensor_tensor(Plo[n % NP][:, 0:k, :], Pm[n % NP][:, 0:k, :],
                                   p_hi(n)[:, 0:k, :], ALU.subtract).then_inc(s["lo_pool"], 1)

            pool.wait_ge(s["x1_done"], 2)
            pool.memset(CW0[:, DC:DC + 1], 1.0)
            pool.memset(CW[:, :, DC:DC + 1], 1.0)
            pool.memset(CS[:, :, :, DC:DC + 1], 1.0).then_inc(s["cs_ones"], 1)
            pool.wait_ge(s["ck_sb"], 1)
            pool.tensor_copy(KA[:, :, 0:64], CK2[:, :, 0:64])
            pool.tensor_copy(CW0[:, 0:64], CK2[:, 0, 0:64]).then_inc(s["cko_done"], 1)
            pool.tensor_copy(KL[:, :, 0:64], CK2[:, :, 0:64])
            pool.wait_ge(s["kmu_done"], 1)
            pool.tensor_copy(KA[:, :, 64:96], kmu)
            pool.tensor_copy(KA[:, :, 96:112], kmu[:, :, 16:32])
            link(pool.tensor_copy(KA[:, :, 112:128], kmu[:, :, 0:16]))
            link(pool.tensor_copy(KA1, KA))
            link(pool.tensor_tensor(KAr, KA, KA1, ALU.subtract))
            link(pool.tensor_copy(KA2, KAr))
            pool.tensor_tensor(KA3, KAr, KA2, ALU.subtract).then_inc(s["kaug"], 1)
            ci = ctab[:, 0, :].rearrange("p (a b) -> p a b", a=2)
            si = ctab[:, 1, :].rearrange("p (a b) -> p a b", a=2)
            pool.tensor_tensor(krt, kmu[:, :, 0:16], ci, ALU.mult)
            link(pool.tensor_tensor(krt2, kmu[:, :, 16:32], si, ALU.mult))
            link(pool.tensor_tensor(KL[:, :, 64:80], krt, krt2, ALU.subtract))
            pool.tensor_tensor(krt, kmu[:, :, 0:16], si, ALU.mult)
            link(pool.tensor_tensor(krt2, kmu[:, :, 16:32], ci, ALU.mult))
            pool.tensor_tensor(KL[:, :, 80:96], krt, krt2, ALU.add).then_inc(s["krot"], 1)
            pool.wait_ge(s["mu_done"], 1)
            m = mu.rearrange("p t (h d) -> p t h d", h=H2)
            for n, dst in ((1, QL), (0, QR)):
                for tile in range(NT):
                    cc = bc(ctab[:, 2 * n, 16 * tile:16 * tile + 16].unsqueeze(1), [128, H2, 16])
                    ss = bc(ctab[:, 2 * n + 1, 16 * tile:16 * tile + 16].unsqueeze(1), [128, H2, 16])
                    m1, m2 = m[:, tile, :, 0:16], m[:, tile, :, 16:32]
                    r1, r2 = rot[:, tile], rot2[:, tile]
                    pool.tensor_tensor(r1, m1, cc, ALU.mult)
                    link(pool.tensor_tensor(r2, m2, ss, ALU.mult))
                    link(pool.tensor_tensor(dst[:, tile, :, 64:80], r1, r2, ALU.subtract))
                    pool.tensor_tensor(r1, m1, ss, ALU.mult)
                    link(pool.tensor_tensor(r2, m2, cc, ALU.mult))
                    last = pool.tensor_tensor(dst[:, tile, :, 80:96], r1, r2, ALU.add)
                    if n:
                        last.then_inc(s["rot_loc"], 1)
                    else:
                        link(last)
                        pool.tensor_copy(dst[:, tile, :, 96:128], dst[:, tile, :, 64:96]).then_inc(s["rot_rank"], 1)
            for j in range(GR * 16 // 32):
                t0 = 64 + 32 * j
                tile, tt = t0 // 128, t0 % 128
                pool.wait_ge(s["idx_done"], tile + 1)
                pool.tensor_tensor(DD[:, 32 * j:32 * j + 32, :],
                                   bc(identb[:, tt:tt + 32].unsqueeze(2), [128, 32, NR]),
                                   bc(topf[:, tile, :].unsqueeze(1), [128, 32, NR]), ALU.mult).then_inc(s["d_done"], 1)

        @block.scalar
        def _(act):
            n_link = [0]

            def link(ins):
                n_link[0] += 1
                ins.then_inc(s["act_chain"], 1)
                act.wait_ge(s["act_chain"], n_link[0])

            act.wait_ge(s["eps_set"], 1)
            act.wait_ge(s["bq4"], 1)
            act.activation(std[:, :], mv[:, :, 1], ACT.Sqrt, bias=eps[:, :]).then_inc(s["x_std"], 1)
            act.wait_ge(s["xnT_ps"], 1)
            act.activation(xnT, bank(6).rearrange("p (a b) -> p a b", a=2), ACT.Copy).then_inc(s["xnT_sb"], 1)
            act.wait_ge(s["bias_in"], 64)

            def chunk(c):
                act.wait_ge(s["ctxT_ps"], c + 1)
                if c >= 2:
                    act.wait_ge(s["v_ps"], c - 1)
                act.activation(ctxT[c % 2][:, 0, :], bank(0), ACT.Copy).then_inc(s["ctxT_a"], 1)

            def k1(c):
                act.wait_ge(s["kT_ps"], c + 1)
                if c >= 2:
                    act.wait_ge(kd_out[c % 2], 48 * (c // 2))
                for m in range(2):
                    last = act.activation(kring[c % 2][0][:, m, :], bank(2 + m), ACT.Identity, bias=bkcol[:, m:m + 1])
                last.then_inc(s["k1_done"], 1)

            chunk(0)
            for g in range(4):
                act.wait_ge(s["qaT_ps"], g + 1)
                act.activation(QA[0:QROWS, 4 * g:4 * g + 4, :],
                               PS[0:QROWS, 6 + g % 2, :].bitcast(bf16).rearrange("p (a b) -> p a b", a=4),
                               ACT.Copy).then_inc(s["qa_sb"], 1)
            for c in range(CH):
                k1(c)
                if c + 1 < CH:
                    chunk(c + 1)
                if c == 1:
                    act.wait_ge(s["fw_in"], 48)
                    for n in range(3):
                        act.activation(fq[n], fraw[n], ACT.Abs, accum_out=fstat[:, n:n + 1]).then_inc(s["fabs"], 1)
                if c - 1 in FQ_AT:
                    n = FQ_AT.index(c - 1)
                    for half in range(2):
                        act.wait_ge(s["fqT_ps"], 2 * n + half + 1)
                        o = PS[:, 6 + half, :].bitcast(bf16)
                        if n < 2:
                            dst, src = (WgT, WuT)[n][:, half, :], o
                        else:
                            dst = WdT[:, :, 128 * half:128 * half + 128]
                            src = o.rearrange("p (a b) -> p a b", a=8)
                        act.activation(dst, src, ACT.Copy).then_inc(s["fqT_sb"], 1)
                act.wait_ge(s["kr_done"], 2 * (c + 1))
                act.activation(kring[c % 2][1], kres, ACT.Copy).then_inc(s["k2_done"], 1)
                act.wait_ge(s["vf_done"], c + 1)
                act.activation(vpart(c, 0), vf_v, ACT.Copy).then_inc(s["v1_done"], 1)
                act.wait_ge(s["vr_done"], c + 1)
                act.activation(vpart(c, 1), vf_v, ACT.Copy).then_inc(s["v2_done"], 1)
            act.wait_ge(s["rd_in"], 16 * 9)
            link(act.activation(trig[:, 0, :], rdel[:, :], ACT.Sigmoid))
            act.activation(trig[:, 2, :], trig[:, 0, :], ACT.Sin, scale=float(np.pi)).then_inc(s["dl_sin"], 1)
            act.activation(trig[:, 3, :], trig[:, 0, :], ACT.Sin, scale=-float(np.pi), bias=halfpi[:, :])\
               .then_inc(s["dl_sin"], 1)
            for n, src in enumerate((4, 5, 6)):
                act.wait_ge(s["wuT_ps"], n + 1)
                dst = (WuqT, WukT, WuvT)[n]
                w = dst.shape[2]
                act.activation(dst, bank(src)[:, 0:4 * w].rearrange("p (a b) -> p a b", a=4), ACT.Copy)\
                   .then_inc(s["wuT_sb"], 1)
            act.wait_ge(s["wa_ps"], 1)
            for e in range(2):
                last = act.activation(WA[:, :].rearrange("p (k e n) -> p k e n", e=2, n=64)[:, :, e, :],
                                      bank(7 - e)[:, 0:256].rearrange("p (k n) -> p k n", k=4), ACT.Copy)
            last.then_inc(s["wa_sb"], 1)
            act.wait_ge(s["wb_ps"], 1)
            for e in range(2):
                last = act.activation(WB[:, :, :].rearrange("p (k e) n -> p k e n", e=2)[:, :, e, :],
                                      PS[0:64, 2 + 2 * e:4 + 2 * e, :].rearrange("p a (b n) -> p (a b) n", b=2), ACT.Copy)
            last.then_inc(s["wb_sb"], 1)
            def head_rows(h):
                act.wait_ge(s["pv_done"], NB * (h + 1))
                act.activation(po[h % 2][0:VW, :], PS[0:VW, 6 + h % 2, 0:T], ACT.Copy).then_inc(s["po_sb"], 1)

            def max_rows(h):
                act.wait_ge(s["mT_ps"], h + 1)
                act.activation(QA[QROWS:SROWS, h, :], PS[QROWS:SROWS, 6 + h % 2, 0:128].bitcast(bf16), ACT.Copy)\
                   .then_inc(s["m_ready"], 1)

            max_rows(0)
            for n in range(STEPS):
                act.wait_ge(s["b_done"], n + 1)
                if n >= NP:
                    act.wait_ge(s["pv_done"], n - NP + 1)
                b = 2 + 2 * (n % 2)
                act.activation(Pm[n % NP], PS[:, b:b + 2, :].rearrange("p a (b n) -> p (a b) n", b=2), ACT.Exp)\
                   .then_inc(s["exp_done"], 1)
                if n % NB == LAG and n > NB:
                    head_rows(n // NB - 1)
                if n % NB == NB - 1 and n + 1 < STEPS:
                    max_rows(n // NB + 1)
            head_rows(H1 - 1)
            act.wait_ge(s["oT_ps"], 1)
            act.activation(OT, bank(0).rearrange("p (a b) -> p a b", a=2), ACT.Copy).then_inc(s["oT_sb"], 1)

            act.wait_ge(s["x1_done"], 2)
            act.activation(std[:, :], mv[:, :, 1], ACT.Sqrt, bias=eps[:, :]).then_inc(s["std2"], 1)
            act.wait_ge(s["xT2_ps"], 1)
            act.activation(xT, bank(0).rearrange("p (a b) -> p a b", a=2), ACT.Copy).then_inc(s["xT2_sb"], 1)
            act.wait_ge(s["qi_ps"], 1)
            act.activation(qiT[0:64], PS[0:64, 1:3, :].rearrange("p a (b n) -> p (a b) n", b=2), ACT.Copy)\
               .then_inc(s["qi_sb"], 1)
            act.wait_ge(s["cq_ps"], 1)
            act.activation(cqT, bank(5)[:, 0:256], ACT.Copy).then_inc(s["cq_sb"], 1)
            for n in range(2):
                act.wait_ge(s["ix0_ps"] if n == 0 else s["ix1_ps"], 1)
                src = bank(0)[:, 0:384].rearrange("p (a b) -> p a b", a=4) if n == 0 else \
                    bank(1, 2).rearrange("p (a b) -> p a b", a=4)[:, :, 0:192]
                act.activation(rl[n], src, ACT.Relu).then_inc(s["relu0"] if n == 0 else s["relu1"], 1)
            act.wait_ge(s["ck_sb"], 1)
            link(act.activation(kmua, CK2[:, :, 64:96], ACT.Abs))
            link(act.activation(kmua, kmua, ACT.Exp, scale=-1.0))
            act.wait_ge(s["mu_ps"], 1)
            link(act.activation(mua, bank(7).rearrange("p (a b) -> p a b", a=2), ACT.Abs))
            link(act.activation(mua, mua, ACT.Exp, scale=-1.0))
            act.activation(kmua, kmua, ACT.Ln, bias=1.0).then_inc(s["kmu_ln"], 1)
            act.activation(mua, mua, ACT.Ln, bias=1.0).then_inc(s["mu_ln"], 1)
            act.wait_ge(s["cs_ones"], 1)
            act.wait_ge(s["cw_ps"], 1)
            act.activation(CW[0:W80, :, 0:64], PS[0:W80, 6:8, :].rearrange("p a (b n) -> p (a b) n", b=8)[:, 0:GR, :],
                           ACT.Copy).then_inc(s["cw_sb"], 1)
            for tile in range(NT):
                act.wait_ge(s["qa2_ps"], tile + 1)
                src = bank(3 + 2 * tile).rearrange("p (h n) -> p h n", h=H2)
                act.activation(QL[:, tile, :, 0:64], src, ACT.Copy)
                act.activation(QR[:, tile, :, 0:64], src, ACT.Copy).then_inc(s["qa2_sb"], 1)
            act.wait_ge(s["klT_ps"], 1)
            act.activation(KLT[0:96], bank(4)[0:96, 0:256], ACT.Copy).then_inc(s["klT_sb"], 1)
            for n in range(8):
                act.wait_ge(s["qrT_ps"], n + 1)
                loc, tile, hh = n < 4, n % 4 // 2, n % 2
                rows = 96 if loc else 128
                dst = (QLT if loc else QRT)[0:rows, 32 * tile:32 * tile + 32, 4 * hh:4 * hh + 4, :]\
                    .rearrange("p c h q -> p h c q")
                src = PS[0:rows, (0, 1, 2, 7)[n % 4], :].rearrange("p (h c q) -> p h c q", h=4, c=32)
                act.activation(dst, src, ACT.Copy).then_inc(s["qrT_sb"], 1)
            for c in range(GR):
                act.wait_ge(s["cs_ps"], c + 1)
                act.activation(CS[:, c, :, 0:64], bank(4 + c % 2)[:, 0:256].rearrange("p (a b) -> p a b", a=4),
                               ACT.Copy).then_inc(s["cs_sb"], 1)
            act.wait_ge(s["sr_ps"], 3)
            for b in range(3):
                act.activation(SR[:, 4 * b:4 * b + 4, :], bank(b).rearrange("p (a n) -> p a n", a=4), ACT.Copy)\
                   .then_inc(s["sr_sb"], 1)
            act.wait_ge(s["nmT_ps"], 1)
            act.activation(nmT[0:16], bank(7)[0:16, 0:128], ACT.Copy).then_inc(s["nmT_sb"], 1)
            for b in range(4):
                act.wait_ge(s["st_ps"], b + 1)
                w = KK if b == 0 else W80
                act.activation(PL[0:w, 512 * b:512 * b + 512], bank(3 + b)[0:w, :], ACT.Exp, scale=SCALE2)\
                   .then_inc(s["p_loc"], 1)
            for b in range(3):
                act.wait_ge(s["st_ps"], 5 + b)
                act.activation(PR[:, 512 * b:512 * b + 512], bank(b), ACT.Exp, scale=SCALE2).then_inc(s["p_rank"], 1)
            for b in range(4):
                act.wait_ge(s["ocT_ps"], b + 1)
                act.activation(OCT[0:64, :, 64 * b:64 * b + 64].rearrange("p h (c q) -> p c h q", q=4),
                               bank(3 + b)[0:64, :].rearrange("p (c h q) -> p c h q", c=16, h=H2), ACT.Copy)\
                   .then_inc(s["ocT_sb"], 1)

            act.wait_ge(s["x2_done"], 2)
            act.activation(std[:, :], mv[:, :, 1], ACT.Sqrt, bias=eps[:, :]).then_inc(s["std3"], 1)
            act.wait_ge(s["hqT_ps"], 1)
            act.activation(hqT, PS[:, 0, 0:256].bitcast(bf16).rearrange("p (a b) -> p a b", a=2), ACT.Copy)\
               .then_inc(s["hqT_sb"], 1)
            for tile in range(NT):
                act.wait_ge(s["gu_ps"], 2 * tile + 1)
                act.wait_ge(s["dq"], 2 * tile + 2)
                act.activation(sg[:, tile, :], bank(4 * tile, 2), ACT.Silu, scale=small[:, 4 + tile:5 + tile])\
                   .then_inc(s["silu"], 1)
            for tile in range(NT):
                act.wait_ge(s["pqT_ps"], tile + 1)
                act.activation(pqT[:, :, 128 * tile:128 * tile + 128],
                               PS[:, tile, :].bitcast(bf16).rearrange("p (a b) -> p a b", a=8), ACT.Copy)\
                   .then_inc(s["pqT_sb"], 1)

        @block.tensor
        def _(pe):
            def mm(o, l, r, start=True, stop=True, shared=False):
                return pe.matmul(o, l, r, start=start, stop=stop, skip_group_check=shared)

            pe.wait_ge(s["const_in"], 16)
            for tile in range(NT):
                pe.wait_ge(s["xn_done"], tile + 1)
                for c in range(2):
                    last = pe.transpose(bank(6)[:, 256 * c + 128 * tile:256 * c + 128 * tile + 128],
                                        xn[:, tile, 128 * c:128 * c + 128], ident)
            last.then_inc(s["xnT_ps"], 1)
            pe.wait_ge(s["xnT_sb"], 1)
            pe.wait_ge(s["wq_in"], 16)
            for tile in range(NT):
                for c in range(2):
                    last = mm(bank(7)[:, 256 * tile:256 * tile + 256], xnT[:, c, 128 * tile:128 * tile + 128],
                              WQ[:, c, :], start=c == 0, stop=c == 1)
            last.then_inc(s["q_ps"], 1)

            def transpose_ctx(c):
                pe.wait_ge(ctx_in[c % 4], 16 * (c // 4 + 1))
                if c:
                    pe.wait_ge(s["ctxT_a"], c)
                    pe.wait_ge(s["ctxT_v"], c)
                for cc in range(2):
                    for k in range(TPC):
                        last = pe.transpose(bank(cc)[:, 128 * k:128 * k + 128],
                                            ctxr[c % 4][:, k, 128 * cc:128 * cc + 128], ident)
                last.then_inc(s["ctxT_ps"], 1)

            def project_k(c):
                pe.wait_ge(s["ctxT_a"], c + 1)
                pe.wait_ge(s["ctxT_v"], c + 1)
                if c == 0:
                    pe.wait_ge(s["wkv_in"], 32)
                else:
                    pe.wait_ge(s["kr_done"], 2 * c)
                for m in range(2):
                    for cc in range(2):
                        last = mm(bank(2 + m), WK[:, cc, 128 * m:128 * m + 128], ctxT[c % 2][:, cc, :],
                                  start=cc == 0, stop=cc == 1)
                last.then_inc(s["kT_ps"], 1)

            def project_v(c):
                if c:
                    pe.wait_ge(s["vf_done"], c)
                for k in range(TPC):
                    for cc in range(2):
                        last = mm(bank(4 + k // 2)[:, 256 * (k % 2):256 * (k % 2) + 256],
                                  ctxT[c % 2][:, cc, 128 * k:128 * k + 128], WV[:, cc, :], start=cc == 0, stop=cc == 1)
                last.then_inc(s["v_ps"], 1)

            def transpose_mlp(n):
                pe.wait_ge(s["fq"], n + 1)
                for half in range(2):
                    o = PS[:, 6 + half, :].bitcast(bf16)
                    if n:
                        pe.wait_ge(s["fqT_sb"], 2 * n - 1 + half)
                    for k in range(8):
                        if n < 2:
                            src = fq[n][:, 256 * k + 128 * half:256 * k + 128 * half + 128]
                        else:
                            src = fq[n][:, 1024 * half + 128 * k:1024 * half + 128 * k + 128]
                        last = pe.transpose(o[:, 128 * k:128 * k + 128], src, identb[:, :])
                    last.then_inc(s["fqT_ps"], 1)

            transpose_ctx(0)
            pe.wait_ge(s["qs_done"], 1)
            pe.wait_ge(s["ident_b"], 1)
            for g in range(4):
                if g >= 2:
                    pe.wait_ge(s["qa_sb"], g - 1)
                o = PS[:, 6 + g % 2, :].bitcast(bf16)
                for h in range(4):
                    for tile in range(NT):
                        n = 256 * h + 128 * tile
                        last = pe.transpose(o[0:QROWS, n:n + 128], QS[:, tile, 4 * g + h, 0:QROWS], identb[:, :])
                last.then_inc(s["qaT_ps"], 1)
            for c in range(CH):
                project_k(c)
                if c + 1 < CH:
                    transpose_ctx(c + 1)
                if c == 2:
                    pe.wait_ge(s["qa_sb"], 4)
                    pe.wait_ge(s["fones"], 2)
                    pe.wait_ge(s["fabs"], 3)
                    mm(PS[:, 6, 0:3], onesf[:, :], fstat[:, 0:3]).then_inc(s["fsum_ps"], 1)
                if c - 1 in FQ_AT:
                    transpose_mlp(FQ_AT.index(c - 1))
                project_v(c)

            pe.wait_ge(s["aw_in"], 16 * 11)
            pe.wait_ge(s["vf_done"], CH)
            for k in range(4):
                last = pe.transpose(bank(4)[:, 128 * k:128 * k + 128], Wuq[:, 128 * k:128 * k + 128], ident)
            last.then_inc(s["wuT_ps"], 1)
            for n, w in enumerate((Wuk, Wuv)):
                if n == 1:
                    pe.wait_ge(s["fqT_sb"], 6)
                for k in range(4):
                    last = pe.transpose(bank(5 + n)[:, 64 * k:64 * k + 64], w[:, 128 * k:128 * k + 128], ident[0:64, 0:64])
                last.then_inc(s["wuT_ps"], 1)
            pe.wait_ge(s["wuT_sb"], 3)
            pe.wait_ge(s["kr_done"], 2 * CH)
            for h in range(H2):
                lo, k = 64 * (h % 2), h // 2
                last = mm(bank(7 - h % 2)[:, 64 * k:64 * k + 64], WuqT[lo:lo + 64, k, :], WukT[lo:lo + 64, k, :])
            last.then_inc(s["wa_ps"], 1)
            for h in range(H2):
                lo, k = 64 * (h % 2), h // 2
                last = mm(PS[0:64, 2 + 2 * (h % 2) + k // 2, 256 * (k % 2):256 * (k % 2) + 256], WuvT[lo:lo + 64, k, :],
                          Wout[lo:lo + 64, k, :])
            last.then_inc(s["wb_ps"], 1)
            pe.wait_ge(s["ctxT_v"], CH)
            pe.wait_ge(s["wa_sb"], 1)
            pe.wait_ge(s["wb_sb"], 1)

            def a_unit(n):
                h, u = n // NA, n % NA
                if u == 0:
                    pe.wait_ge(kst_in[h % NKST], 16 * NBLK * (h // NKST + 1))
                if n >= 2:
                    pe.wait_ge(s["a_read"], n - 1)
                tile, c = u // CH, u % CH
                mm(bank(n % 2), QA[0:QROWS, h, 128 * tile:128 * tile + 128],
                   Kst[h % NKST][0:QROWS, CK * c:CK * c + CK]).then_inc(s["a_done"], 1)

            def max_rows(h):
                pe.wait_ge(s["m_split"], 2 * h + 2)
                if h >= 2:
                    pe.wait_ge(s["o_read"], h - 1)
                o = PS[:, 6 + h % 2, :].bitcast(bf16)
                for tile in range(NT):
                    last = pe.transpose(o[0:SROWS, 128 * tile:128 * tile + 128], QS[:, tile, h, :], identb[:, :])
                last.then_inc(s["mT_ps"], 1)

            def b_step(h, st):
                n = NB * h + st
                if st == 0:
                    pe.wait_ge(s["m_ready"], h + 1)
                if n >= 2:
                    pe.wait_ge(s["exp_done"], n - 1)
                for k in range(TPC):
                    b = 2 + 2 * (n % 2) + k // 2
                    key = 128 * (TPC * st + k)
                    last = mm(bank(b)[:, 256 * (k % 2):256 * (k % 2) + 256], Kst[h % NKST][0:SROWS, key:key + 128],
                              QA[0:SROWS, h, :])
                last.then_inc(s["b_done"], 1)

            def pv_step(n, first, end):
                h, st = n // NB, n % NB
                for k in range(first, end):
                    if k == 0:
                        pe.wait_ge(s["lo_pool"], n + 1)
                    if k == pool_tiles(n):
                        pe.wait_ge(s["lo_dve"], n + 1)
                    for part_ in range(2):
                        last = mm(PS[0:VW, 6 + h % 2, 0:T], V[:, TPC * st + k, h, :],
                                  Plo[n % NP][:, k, :] if part_ else p_hi(n)[:, k, :],
                                  start=st == 0 and k == 0 and part_ == 0, stop=st == NB - 1 and k == TPC - 1 and part_ == 1)
                if end == TPC:
                    last.then_inc(s["pv_done"], 1)

            def head_sum(h):
                pe.wait_ge(s["po_sb"], h + 1)
                for tile in range(NT):
                    last = mm(PS[:, 6 + h % 2, 256 + 32 * tile:256 + 32 * tile + DK + 1],
                              po[h % 2][0:VW, 128 * tile:128 * tile + 128], const("vsum")[0:VW, :])
                last.then_inc(s["comb_ps"], 1)

            for u in range(AHEAD):
                a_unit(u)
                if u == NA + 1:
                    max_rows(0)
            for n in range(STEPS):
                h, st = n // NB, n % NB
                b_step(h, st)
                for k in range(UPS):
                    if AHEAD + UPS * n + k < NA * H1:
                        a_unit(AHEAD + UPS * n + k)
                    if k == 1 and st == NB - 1 and h + 1 < H1:
                        max_rows(h + 1)
                    if n >= LAG:
                        pv_step(n - LAG, TPC // UPS * k, TPC // UPS * (k + 1))
                if st == LAG + 1 and h:
                    head_sum(h - 1)
            for n in range(STEPS - LAG, STEPS):
                pv_step(n, 0, TPC)
            head_sum(H1 - 1)

            pe.wait_ge(s["o_read"], H1)
            pe.wait_ge(s["a_read"], NA * H1)
            for tile in range(NT):
                for c in range(2):
                    last = pe.transpose(bank(0)[:, 256 * c + 128 * tile:256 * c + 128 * tile + 128],
                                        O[:, tile, 128 * c:128 * c + 128], ident)
            last.then_inc(s["oT_ps"], 1)
            pe.wait_ge(s["oT_sb"], 1)
            pe.wait_ge(s["wo_in"], 16)
            for tile in range(NT):
                for c in range(2):
                    last = mm(bank(2 + tile)[:, 0:256], OT[:, c, 128 * tile:128 * tile + 128], WO[:, c, :],
                              start=c == 0, stop=c == 1)
                last.then_inc(s["y1_ps"], 1)

            for tile in range(NT):
                pe.wait_ge(s["xn2"], tile + 1)
                for c in range(2):
                    last = pe.transpose(bank(0)[:, 256 * c + 128 * tile:256 * c + 128 * tile + 128],
                                        xn2[:, tile, 128 * c:128 * c + 128], ident)
            last.then_inc(s["xT2_ps"], 1)
            pe.wait_ge(s["xT2_sb"], 1)
            for h in range(NI):
                for c in range(2):
                    last = mm(PS[0:64, 1 + h // 2, 256 * (h % 2):256 * (h % 2) + 256], Wiq[:, c, 64 * h:64 * h + 64],
                              xT[:, c, :], start=c == 0, stop=c == 1)
            last.then_inc(s["qi_ps"], 1)
            for c in range(2):
                last = mm(PS[0:64, 3, 0:256], Wik[:, c, :], xT[:, c, :], start=c == 0, stop=c == 1)
            last.then_inc(s["ki_ps"], 1)
            for tile in range(NT):
                for c in range(2):
                    last = mm(bank(4)[:, 96 * tile:96 * tile + 96], xT[:, c, 128 * tile:128 * tile + 128], Wck[:, c, :],
                              start=c == 0, stop=c == 1)
            last.then_inc(s["ck_ps"], 1)
            for c in range(2):
                last = mm(bank(5)[:, 0:256], Wdq[:, c, :], xT[:, c, :], start=c == 0, stop=c == 1)
            last.then_inc(s["cq_ps"], 1)
            pe.wait_ge(s["qi_sb"], 1)
            pe.wait_ge(s["ki_sb"], 1)
            for h in range(NI):
                last = mm(bank(0)[:, 96 * h:96 * h + 96], qiT[0:64, h, 0:128], kiT[0:64, 0:96])
            last.then_inc(s["ix0_ps"], 1)
            for h in range(NI):
                last = mm(bank(1 + h // 2)[:, 256 * (h % 2):256 * (h % 2) + 192], qiT[0:64, h, 128:256], kiT[0:64, 0:192])
            last.then_inc(s["ix1_ps"], 1)
            pe.wait_ge(s["cq_sb"], 1)
            for tile in range(NT):
                last = mm(bank(7)[:, 256 * tile:256 * tile + 256], cqT[:, 128 * tile:128 * tile + 128], Wqr[:, :])
            last.then_inc(s["mu_ps"], 1)
            for tile in range(NT):
                mm(bank(3 + 2 * tile), cqT[:, 128 * tile:128 * tile + 128], WA[:, :]).then_inc(s["qa2_ps"], 1)
            pe.wait_ge(s["mu_done"], 1)
            for g in range(GR):
                for c in range(2):
                    last = mm(PS[0:W80, 6 + g // 8, 64 * (g % 8):64 * (g % 8) + 64], xT[:, c, 16 * g:16 * g + W80],
                              Wck[:, c, 0:64], start=c == 0, stop=c == 1)
            last.then_inc(s["cw_ps"], 1)
            pe.wait_ge(s["krot"], 1)
            pe.wait_ge(s["ck_sb"], 1)
            for tile in range(NT):
                last = pe.transpose(bank(4)[0:96, 128 * tile:128 * tile + 128], KL[:, tile, :], ident)
            last.then_inc(s["klT_ps"], 1)
            pe.wait_ge(s["relu0"], 1)
            pe.wait_ge(s["relu1"], 1)
            pe.wait_ge(s["cw_sb"], 1)
            for n in range(8):
                loc, tile, hh = n < 4, n % 4 // 2, n % 2
                pe.wait_ge(s["rot_loc"] if loc else s["rot_rank"], tile + 1)
                pe.wait_ge(s["qa2_sb"], tile + 1)
                if n >= 4:
                    pe.wait_ge(s["qrT_sb"], n - 3)
                rows = 96 if loc else 128
                for h in range(4):
                    last = pe.transpose(PS[0:rows, (0, 1, 2, 7)[n % 4], 128 * h:128 * h + 128],
                                        (QL if loc else QR)[:, tile, 4 * hh + h, :], ident)
                last.then_inc(s["qrT_ps"], 1)
            pe.wait_ge(s["qrT_sb"], 4)
            pe.wait_ge(s["klT_sb"], 1)
            qlt = QLT.rearrange("p c h q -> p (c h q)")
            qrt = QRT.rearrange("p c h q -> p (c h q)")
            for g in range(G):
                w, k0 = (KK, 0) if g < 4 else (W80, 16 * g - LW)
                o = bank(3 + g // 4)[:, 128 * (g % 4):128 * (g % 4) + w]
                if g >= 4:
                    mm(o, identb[:, :], lmaskb[:, :], start=g % 4 == 0, stop=False, shared=True)
                last = mm(o, qlt[0:96, 128 * g:128 * g + 128], KLT[0:96, k0:k0 + w],
                          start=g < 4 and g % 4 == 0, stop=True, shared=True)
                if g % 4 == 3:
                    last.then_inc(s["sl_ps"], 1)
            pe.wait_ge(s["kaug"], 1)
            pe.wait_ge(s["qrT_sb"], 8)
            pe.wait_ge(s["sl_max"], 4)
            DDf = DD.rearrange("p t r -> p (t r)")
            for c in range(GR + 1):
                if c < GR:
                    pe.wait_ge(s["d_done"], c // 2 + 1)
                    if c >= 2:
                        pe.wait_ge(s["e_done"], c - 1)
                    mm(bank(c % 2), onesb[:, :], DDf[:, 512 * c:512 * c + 512]).then_inc(s["bc_ps"], 1)
                if c:
                    g = c - 1
                    pe.wait_ge(s["e_done"], g + 1)
                    if g >= 2:
                        pe.wait_ge(s["kg_sb"], g - 1)
                        pe.wait_ge(s["cs_sb"], g - 1)
                    terms = [(E0[:, 512 * g:512 * g + 512], 0)]
                    if g >= 8:
                        terms.append((E1[:, 512 * (g - 8):512 * (g - 8) + 512], 1))
                    todo = [(e, tile, k) for e, tile in terms for k in (KA1, KA2, KA3)]
                    for n, (e, tile, k) in enumerate(todo):
                        last = mm(bank(2 + g % 2), k[:, tile, :], e, start=n == 0, stop=n == len(todo) - 1)
                    last.then_inc(s["kg_ps"], 1)
                    for cc in range(4):
                        for n, (e, tile, k) in enumerate(todo):
                            last = mm(bank(4 + g % 2)[:, 64 * cc:64 * cc + 64], e[:, 128 * cc:128 * cc + 128],
                                      k[:, tile, 0:64], start=n == 0, stop=n == len(todo) - 1)
                    last.then_inc(s["cs_ps"], 1)
            pe.wait_ge(s["kg_sb"], GR)
            rmb = bc(rmaskb[:, :].unsqueeze(1), [128, 16, 32])
            for b in range(3):
                mm(bank(b).rearrange("p (a n) -> p a n", a=16), identb[:, :], rmb, start=True, stop=False, shared=True)
                for k in range(16):
                    col = 16 * b + k
                    last = mm(bank(b)[:, 32 * k:32 * k + 32], KGs[:, 128 * col:128 * col + 128],
                              qrt[:, 32 * (col + 16):32 * (col + 16) + 32], start=False, stop=False, shared=True)
                last.then_inc(s["sr_ps"], 1)
            pe.wait_ge(s["cs_sb"], GR)
            for gi in range(GR):
                pe.wait_ge(s["sr_sb"], gi // 4 + 1)
                last = pe.transpose(bank(3 + gi // 4)[:, 128 * (gi % 4):128 * (gi % 4) + 128], SR[:, gi, :], ident)
                if gi % 4 == 3:
                    last.then_inc(s["srT_ps"], 1)
            pe.wait_ge(s["nm_done"], 1)
            pe.transpose(bank(7)[0:16, 0:128], nm2, ident).then_inc(s["nmT_ps"], 1)
            pe.wait_ge(s["sr_max"], 3)
            for g in range(G):
                w, k0 = (KK, 0) if g < 4 else (W80, 16 * g - LW)
                o = PS[0:w, 3 + g // 4, 128 * (g % 4):128 * (g % 4) + 128]
                if g >= 4:
                    mm(o, lmaskb[:, :], identb[:, :], start=g % 4 == 0, stop=False, shared=True)
                mm(o, KLT[0:96, k0:k0 + w], qlt[0:96, 128 * g:128 * g + 128], start=g < 4 and g % 4 == 0, stop=False,
                   shared=True)
                if g == 0:
                    pe.wait_ge(s["nmT_sb"], 1)
                last = mm(o, bc(ident[0:16, g:g + 1], [16, w]), nmT[0:16], start=False, stop=True, shared=True)
                if g % 4 == 3:
                    last.then_inc(s["st_ps"], 1)
            for gi in range(GR):
                last = mm(bank(gi // 4)[:, 128 * (gi % 4):128 * (gi % 4) + 128], bc(ident[0:16, 4 + gi:5 + gi], [16, 128]),
                          nmT[0:16], start=False, stop=True, shared=True)
                if gi % 4 == 3:
                    last.then_inc(s["st_ps"], 1)
            pe.wait_ge(s["cko_done"], 1)
            for g in range(G):
                bo = (7, 0, 1, 2)[g // 4]
                o = bank(bo)[:, 128 * (g % 4):128 * (g % 4) + DC + 1]
                w = KK if g < 4 else W80
                pe.wait_ge(s["p_loc"], g // 4 + 1)
                if g >= 4:
                    pe.wait_ge(s["p_rank"], 3)
                mm(o, PL[0:w, 128 * g:128 * g + 128], CW0[0:KK] if g < 4 else CW[0:W80, g - 4, :],
                   start=g % 4 == 0, stop=g < 4, shared=True)
                last = None
                if g >= 4:
                    for cc in range(4):
                        n = 128 * (g - 4) + 32 * cc
                        last = mm(PS[32 * cc:32 * cc + 32, bo, 128 * (g % 4):128 * (g % 4) + DC + 1], PR[:, n:n + 32],
                                  CS[:, g - 4, cc, :], start=False, stop=True, shared=True)
                if g == 3:
                    pass
                if g % 4 == 3:
                    if last is None:
                        last = pe.transpose(bank(3)[0:16, 0:128], nm2, ident)
                    last.then_inc(s["pv2_ps"], 1)
            for g in range(G):
                pe.wait_ge(s["oc_done"], g // 4 + 1)
                last = pe.transpose(PS[0:64, 3 + g // 4, 128 * (g % 4):128 * (g % 4) + 128], OC[:, g, :], ident)
                if g % 4 == 3:
                    last.then_inc(s["ocT_ps"], 1)
            for tile in range(NT):
                pe.wait_ge(s["ocT_sb"], 2 * tile + 2)
                for h in range(H2):
                    last = mm(bank(tile)[:, 0:256], OCT[0:64, h, 128 * tile:128 * tile + 128], WB[:, h, :],
                              start=h == 0, stop=h == H2 - 1)
                last.then_inc(s["y2_ps"], 1)

            for tile in range(NT):
                pe.wait_ge(s["hq_done"], tile + 1)
                for c in range(2):
                    o = PS[:, 0, :].bitcast(bf16)
                    last = pe.transpose(o[:, 256 * c + 128 * tile:256 * c + 128 * tile + 128],
                                        hq[:, tile, 128 * c:128 * c + 128], identb[:, :])
            last.then_inc(s["hqT_ps"], 1)
            pe.wait_ge(s["hqT_sb"], 1)
            for tile in range(NT):
                for k, w in enumerate((WgT, WuT)):
                    for half in range(2):
                        for c in range(2):
                            last = mm(bank(4 * tile + 2 * k + half), hqT[:, c, 128 * tile:128 * tile + 128],
                                      w[:, c, 512 * half:512 * half + 512], start=c == 0, stop=c == 1)
                    last.then_inc(s["gu_ps"], 1)
            for tile in range(NT):
                pe.wait_ge(s["pq_done"], tile + 1)
                o = PS[:, tile, :].bitcast(bf16)
                for k in range(8):
                    last = pe.transpose(o[:, 128 * k:128 * k + 128], pq[:, tile, 128 * k:128 * k + 128], identb[:, :])
                last.then_inc(s["pqT_ps"], 1)
            for tile in range(NT):
                pe.wait_ge(s["pqT_sb"], tile + 1)
                for k in range(8):
                    last = mm(bank(2 + tile)[:, 0:256], pqT[:, k, 128 * tile:128 * tile + 128], WdT[:, k, :],
                              start=k == 0, stop=k == 7)
                last.then_inc(s["y3_ps"], 1)

        @block.vector
        def _(v):
            n_link = [0]

            def link(ins):
                n_link[0] += 1
                ins.then_inc(s["dve_chain"], 1)
                v.wait_ge(s["dve_chain"], n_link[0])

            def stats(tile):
                link(v.bn_stats(ln[:, tile, 0:6], xres[:, tile, :]))
                return v.bn_aggr(mv[:, tile, :], ln[:, tile, 0:6])

            def normalise(dst, std_sem, done):
                v.wait_ge(std_sem, 1)
                link(v.reciprocal(rstd[:, :], std[:, :]))
                for tile in range(NT):
                    v.tensor_scalar(dst[:, tile, :], xres[:, tile, :], mv[:, tile, 0:1], rstd[:, tile:tile + 1],
                                    ALU.subtract, ALU.mult).then_inc(done, 1)

            v.wait_ge(s["x_in"], 16)
            for tile in range(NT):
                link(stats(tile))
            v.wait_ge(s["bq_in"], 16)
            v.tensor_scalar(bqkvo[:, 0, :], bqkvo[:, 0, :], 0.25, None, ALU.mult).then_inc(s["bq4"], 1)
            normalise(xn, s["x_std"], s["xn_done"])
            v.wait_ge(s["const_in"], 16)
            v.tensor_copy(lmaskb[:, :], const("lmask"))
            v.tensor_copy(rmaskb[:, :], const("rmask"))
            v.tensor_copy(identb[:, :], ident).then_inc(s["ident_b"], 1)
            v.wait_ge(s["q_ps"], 1)
            v.wait_ge(s["bq4"], 1)
            link(v.scalar_tensor_tensor(qf, bank(7).rearrange("p (a b) -> p a b", a=2), 0.25,
                                        bc(bqkvo[:, 0:1, :], [128, NT, D]), ALU.mult, ALU.add))

            def blk(b, tile):
                return QS[:, tile, :, 16 * b:16 * b + 16]

            def hd(x_, tile):
                return x_[:, tile, :].rearrange("p (h d) -> p h d", h=H1)

            for b in (0, 3, 5):
                for tile in range(NT):
                    last = v.tensor_copy(blk(b, tile), hd(qf, tile))
            link(last)
            for tile in range(NT):
                last = v.tensor_tensor(hd(q2f, tile), hd(qf, tile), blk(0, tile), ALU.subtract)
            link(last)
            for b in (1, 4):
                for tile in range(NT):
                    last = v.tensor_copy(blk(b, tile), hd(q2f, tile))
            link(last)
            for tile in range(NT):
                last = v.tensor_tensor(blk(2, tile), hd(q2f, tile), blk(1, tile), ALU.subtract)
            last.then_inc(s["qs_done"], 1)

            def ctx_evac(c):
                v.wait_ge(s["ctxT_ps"], c + 1)
                if c >= 2:
                    v.wait_ge(s["v_ps"], c - 1)
                v.tensor_copy(ctxT[c % 2][:, 1, :], bank(1)).then_inc(s["ctxT_v"], 1)

            ctx_evac(0)
            v.wait_ge(s["bias_in"], 64)
            for c in range(CH):
                v.wait_ge(s["k1_done"], c + 1)
                if c:
                    v.wait_ge(s["k3_done"], c)
                for m in range(2):
                    v.scalar_tensor_tensor(kres[:, m, :], bank(2 + m), bkcol[:, m:m + 1], kring[c % 2][0][:, m, :],
                                           ALU.add, ALU.subtract).then_inc(s["kr_done"], 1)
                if c + 1 < CH:
                    ctx_evac(c + 1)
                v.wait_ge(s["v_ps"], c + 1)
                if c:
                    v.wait_ge(s["v3_done"], c)
                for k in range(2):
                    last = v.tensor_tensor(vf[:, 2 * k:2 * k + 2, :], bank(4 + k).rearrange("p (a n) -> p a n", a=2),
                                           bc(bqkvo[:, 1:2, :], [128, 2, D]), ALU.add)
                last.then_inc(s["vf_done"], 1)
                if c == 2:
                    v.wait_ge(s["fsum_ps"], 1)
                    link(v.tensor_scalar(fstat[:, 4:7], PS[:, 6, 0:3], 1.0 / (F * D), 1e-5, ALU.mult, ALU.max))
                    link(v.reciprocal(fstat[:, 8:11], fstat[:, 4:7]))
                if c in FQ_AT:
                    n = FQ_AT.index(c)
                    link(v.tensor_scalar(fraw[n], fraw[n], fstat[:, 8 + n:9 + n], -1.0, ALU.mult, ALU.max))
                    link(v.tensor_scalar(fraw[n], fraw[n], 1.0, MAGIC, ALU.min, ALU.add))
                    v.tensor_scalar(fq[n], fraw[n], MAGIC, None, ALU.subtract).then_inc(s["fq"], 1)
                v.wait_ge(s["v1_done"], c + 1)
                v.tensor_tensor(vf_v, vf_v, vpart(c, 0), ALU.subtract).then_inc(s["vr_done"], 1)
            v.wait_ge(s["dl_sin"], 2)
            link(v.tensor_tensor(trig[:, 0, :], trig[:, 2, :], trig[:, 2, :], ALU.mult))
            link(v.tensor_tensor(trig[:, 1, :], trig[:, 2, :], trig[:, 3, :], ALU.mult))
            link(v.tensor_scalar(trig[:, 2, :], trig[:, 0, :], -2.0, 1.0, ALU.mult, ALU.add))
            v.tensor_scalar(trig[:, 3, :], trig[:, 1, :], -2.0, None, ALU.mult).then_inc(s["dl_v"], 1)

            def a_unit(n):
                h, u = n // NA, n % NA
                v.wait_ge(s["a_done"], n + 1)
                return v.tensor_reduce(mxp[:, h % 2, u // CH, u % CH:u % CH + 1], bank(n % 2), axis=AX.X, op=ALU.max)\
                    .then_inc(s["a_read"], 1)

            def max_split(h):
                v.wait_ge(s["a_read"], NA * (h + 1))
                link(v.tensor_reduce(nm1[:, h % 2, :], mxp[:, h % 2, :, :], axis=AX.X, op=ALU.max, negate=True))
                v.tensor_copy(QS[:, :, h, QROWS], nm1[:, h % 2, :]).then_inc(s["m_split"], 1)
                v.wait_ge(s["m_split"], 2 * h + 1)
                v.tensor_tensor(QS[:, :, h, QROWS + 1], nm1[:, h % 2, :], QS[:, :, h, QROWS], ALU.subtract)\
                 .then_inc(s["m_split"], 1)

            def head_out(h):
                v.wait_ge(s["comb_ps"], h + 1)
                o = PS[:, 6 + h % 2, 256:320].rearrange("p (a b) -> p a b", a=2)
                link(v.reciprocal(rec1[:, h % 2, :], o[:, :, DK]))
                v.tensor_tensor(O[:, :, DK * h:DK * h + DK], o[:, :, 0:DK], bc(rec1[:, h % 2, :].unsqueeze(2), [128, NT, DK]),
                                ALU.mult).then_inc(s["o_read"], 1)

            def p_low(n):
                v.wait_ge(s["exp_done"], n + 1)
                k = pool_tiles(n)
                v.tensor_tensor(Plo[n % NP][:, k:TPC, :], Pm[n % NP][:, k:TPC, :],
                                p_hi(n)[:, k:TPC, :], ALU.subtract).then_inc(s["lo_dve"], 1)

            for u in range(NA):
                a_unit(u)
            max_split(0)
            for u in range(NA, AHEAD):
                a_unit(u)
            for n in range(STEPS):
                h, st = n // NB, n % NB
                for k in range(UPS):
                    if AHEAD + UPS * n + k < NA * H1:
                        a_unit(AHEAD + UPS * n + k)
                    if k == 0 and n:
                        p_low(n - 1)
                if st == NB - 1 - LEAD and h + 1 < H1:
                    max_split(h + 1)
                if st == LAG + 2 and h:
                    head_out(h - 1)
            p_low(STEPS - 1)
            head_out(H1 - 1)
            v.wait_ge(s["xb_done"], 1)
            for tile in range(NT):
                v.wait_ge(s["y1_ps"], tile + 1)
                v.tensor_tensor(xres[:, tile, :], bank(2 + tile)[:, 0:256], xb[:, tile, :], ALU.add)\
                 .then_inc(s["dve_chain"], 1)
                n_link[0] += 1
                v.wait_ge(s["dve_chain"], n_link[0])
            for tile in range(NT):
                stats(tile).then_inc(s["x1_done"], 1)
            v.wait_ge(s["x1_done"], 2)
            normalise(xn2, s["std2"], s["xn2"])
            v.wait_ge(s["ki_ps"], 1)
            v.tensor_copy(kiT[0:64], PS[0:64, 3, 0:256]).then_inc(s["ki_sb"], 1)
            v.wait_ge(s["ck_ps"], 1)
            v.tensor_copy(CK2, bank(4)[:, 0:192].rearrange("p (a b) -> p a b", a=2)).then_inc(s["ck_sb"], 1)
            v.wait_ge(s["ck_sb"], 1)
            mups = bank(7).rearrange("p (a b) -> p a b", a=2)
            v.wait_ge(s["kmu_ln"], 1)
            v.scalar_tensor_tensor(kmu, CK2[:, :, 64:96], 0.0, kmua, ALU.max, ALU.add).then_inc(s["kmu_done"], 1)
            v.wait_ge(s["mu_ln"], 1)
            v.scalar_tensor_tensor(mu, mups, 0.0, mua, ALU.max, ALU.add).then_inc(s["mu_done"], 1)
            for tile in range(NT):
                v.wait_ge(s["relu0"] if tile == 0 else s["relu1"], 1)
                n = (96, 192)[tile]
                kp = const("keep").rearrange("p (a b) -> p a b", a=2)[:, tile, 0:n]
                fl = const("fill").rearrange("p (a b) -> p a b", a=2)[:, tile, 0:n]
                link(v.tensor_scalar(IX[tile], rl[tile][:, 0, :], iwb[:, 0:1], None, ALU.mult))
                for h in range(1, NI):
                    link(v.scalar_tensor_tensor(IX[tile], rl[tile][:, h, :], iwb[:, h:h + 1], IX[tile], ALU.mult, ALU.add))
                link(v.tensor_tensor(IX[tile], IX[tile], kp, ALU.mult))
                link(v.tensor_tensor(IX[tile], IX[tile], fl, ALU.add))
                for r in range(NR // 8):
                    tv, ti = topv[:, tile, 8 * r:8 * r + 8], topi[:, tile, 8 * r:8 * r + 8].bitcast(u32)
                    link(v.max(tv, IX[tile]))
                    last = v.max_index(ti, tv, IX[tile])
                    link(last)
                    if r < NR // 8 - 1:
                        link(v.match_replace(IX[tile], tv, IX[tile], FMIN))
                v.tensor_copy(topf[:, tile, :], topi[:, tile, :].bitcast(u32)).then_inc(s["idx_done"], 1)
            for b in range(4):
                v.wait_ge(s["sl_ps"], b + 1)
                w = KK if b == 0 else W80
                v.tensor_reduce(mxl[:, 4 * b:4 * b + 4], bank(3 + b).rearrange("p (a n) -> p a n", a=4)[:, :, 0:w],
                                axis=AX.X, op=ALU.max).then_inc(s["sl_max"], 1)
            v.wait_ge(s["tabs_done"], 1)
            for c in range(GR + 1):
                if c < GR:
                    v.wait_ge(s["bc_ps"], c + 1)
                    last = v.tensor_scalar(E0[:, 512 * c:512 * c + 512], bank(c % 2), const("iota")[:, 0:1], None,
                                           ALU.is_equal)
                    if c >= 8:
                        last = v.tensor_scalar(E1[:, 512 * (c - 8):512 * (c - 8) + 512], bank(c % 2),
                                               const("iota")[:, 1:2], None, ALU.is_equal)
                    last.then_inc(s["e_done"], 1)
                if c:
                    g = c - 1
                    v.wait_ge(s["kg_ps"], g + 1)
                    v.tensor_tensor(KGs[:, 512 * g:512 * g + 512].rearrange("p (a r) -> p a r", a=16),
                                    bank(2 + g % 2).rearrange("p (a r) -> p a r", a=16),
                                    bc(rtab[:, :].unsqueeze(1), [128, 16, NR]), ALU.mult).then_inc(s["kg_sb"], 1)
            for b in range(3):
                v.wait_ge(s["srT_ps"], b + 1)
                v.tensor_reduce(mxr[:, 4 * b:4 * b + 4], bank(3 + b).rearrange("p (a n) -> p a n", a=4),
                                axis=AX.X, op=ALU.max).then_inc(s["sr_max"], 1)
            v.wait_ge(s["sr_max"], 3)
            v.wait_ge(s["sl_max"], 4)
            v.tensor_scalar(nm2[:, 0:4], mxl[:, 0:4], -1.0, None, ALU.mult)
            link(v.tensor_tensor(nm2[:, 4:16], mxl[:, 4:16], mxr[:, 0:12], ALU.max))
            v.tensor_scalar(nm2[:, 4:16], nm2[:, 4:16], -1.0, None, ALU.mult).then_inc(s["nm_done"], 1)
            for b in range(4):
                v.wait_ge(s["pv2_ps"], b + 1)
                o = bank((7, 0, 1, 2)[b]).rearrange("p (a n) -> p a n", a=4)
                link(v.reciprocal(rec2[:, 4 * b:4 * b + 4], o[:, :, DC]))
                v.tensor_tensor(OC[:, 4 * b:4 * b + 4, :], o[:, :, 0:64], bc(rec2[:, 4 * b:4 * b + 4].unsqueeze(2), [128, 4, 64]),
                                ALU.mult).then_inc(s["oc_done"], 1)
            for tile in range(NT):
                v.wait_ge(s["y2_ps"], tile + 1)
                link(v.tensor_tensor(xres[:, tile, :], xres[:, tile, :], bank(tile)[:, 0:256], ALU.add))

            for tile in range(NT):
                stats(tile).then_inc(s["x2_done"], 1)
            v.wait_ge(s["x2_done"], 2)
            normalise(h3, s["std3"], s["xn3"])
            v.wait_ge(s["xn3"], 2)

            def quantise(tile, src, work, dst, col, done):
                am, sc, dq = small[:, 16 + tile:17 + tile], small[:, 20 + tile:21 + tile], small[:, col + tile:col + tile + 1]
                link(v.tensor_reduce(am, src, axis=AX.X, op=ALU.max, apply_absolute_value=True))
                link(v.tensor_scalar(am, am, 1e-5, None, ALU.max))
                link(v.reciprocal(sc, am))
                link(v.tensor_scalar(sc, sc, 127.0, None, ALU.mult))
                v.tensor_scalar(dq, am, 1.0 / 127.0, None, ALU.mult)
                link(v.tensor_scalar(work, src, sc, -128.0, ALU.mult, ALU.max))
                link(v.tensor_scalar(work, work, 127.0, MAGIC, ALU.min, ALU.add))
                v.tensor_scalar(dst, work, MAGIC, None, ALU.subtract).then_inc(done, 1)

            for tile in range(NT):
                quantise(tile, h3[:, tile, :], hr[:, tile, :], hq[:, tile, :], 0, s["hq_done"])
                v.wait_ge(s["hq_done"], tile + 1)
                for n in range(2):
                    v.tensor_scalar(small[:, 4 + 2 * n + tile:5 + 2 * n + tile], small[:, tile:tile + 1],
                                    fstat[:, 4 + n:5 + n], None, ALU.mult).then_inc(s["dq"], 1)
            v.wait_ge(s["dq"], 4)
            for tile in range(NT):
                v.wait_ge(s["gu_ps"], 2 * tile + 2)
                v.wait_ge(s["silu"], tile + 1)
                link(v.scalar_tensor_tensor(pr[:, tile, :], bank(4 * tile + 2, 2), small[:, 6 + tile:7 + tile], sg[:, tile, :],
                                            ALU.mult, ALU.mult))
                quantise(tile, pr[:, tile, :], pr2[:, tile, :], pq[:, tile, :], 8, s["pq_done"])
                link(v.tensor_scalar(small[:, 12 + tile:13 + tile], small[:, 8 + tile:9 + tile], fstat[:, 6:7], None, ALU.mult))
            for tile in range(NT):
                v.wait_ge(s["y3_ps"], tile + 1)
                last = v.scalar_tensor_tensor(res[:, tile, :], bank(2 + tile)[:, 0:256], small[:, 12 + tile:13 + tile],
                                              xres[:, tile, :], ALU.mult, ALU.add)
            last.then_inc(s["out_done"], 1)


_INS = ['x', 'ctx_1024', 'L0_xattn_W_Q', 'L0_xattn_b_Q', 'L0_xattn_W_K', 'L0_xattn_b_K', 'L0_xattn_W_V',
        'L0_xattn_b_V', 'L0_xattn_W_O', 'L0_xattn_b_O', 'L0_attn_W_dkv', 'L0_attn_W_uk', 'L0_attn_W_uv',
        'L0_attn_W_dq', 'L0_attn_W_uq', 'L0_attn_W_qr', 'L0_attn_W_kr', 'L0_attn_W_out', 'L0_attn_idx_wq',
        'L0_attn_idx_wk', 'L0_attn_idx_w', 'L0_attn_raw_delta', 'L0_ffn_w_gate', 'L0_ffn_w_up', 'L0_ffn_w_down']


def kernel(**inputs):
    import numpy as _np
    import concourse.bacc as _bacc
    from concourse import mybir as _mybir
    from concourse.bass_utils import run_bass_kernel_spmd as _run

    nc = _bacc.Bacc("TRN2", target_bir_lowering=False, num_devices=1)
    arrays = {"consts_dram": constants()}
    consts = nc.dram_tensor("consts_dram", (128, NCONST), fp32, kind="ExternalInput").ap()
    args = {}
    for name in _INS:
        arr = _np.ascontiguousarray(inputs[name])
        arrays[f"in_{name}_dram"] = arr
        args[name] = nc.dram_tensor(f"in_{name}_dram", arr.shape, _mybir.dt.from_np(arr.dtype), kind="ExternalInput").ap()
    out = nc.dram_tensor("out_0_dram", (1, T, D), fp32, kind="ExternalOutput").ap()
    build(nc, consts, args, out)
    r = _run(nc, [arrays], core_ids=[0])
    return r.results[0]["out_0_dram"]
```

```python
import concourse.bass as bass
from concourse import mybir
from contextlib import ExitStack
import numpy as np

fp32 = mybir.dt.float32
bf16 = mybir.dt.bfloat16
u32 = mybir.dt.uint32
fp16 = mybir.dt.float16
ALU = mybir.AluOpType
ACT = mybir.ActivationFunctionType
AX = mybir.AxisListType

T, D = 256, 256
S = 4096
NT = T // 128
H1, DK = 16, 16
KT = S // 128
CH = 8
CK = S // CH
TPC = KT // CH
NBLK = 6
QROWS = NBLK * DK
SROWS = QROWS + 2
KBLK = [0, 0, 0, 1, 1, 2]
QBLK = [0, 1, 2, 0, 1, 0]
NKST = 3
NP = 4
LAG = 2
VW = 3 * DK + 1
LEAD = 1
H2, DH, DR, DC = 8, 64, 32, 64
NI = 4
HALF = DR // 2
LW, KK = 64, 96
NR = KK - LW
DVE_DD = 2
G = T // 16
GR = G - LW // 16
W80 = LW + 16
SW = W80 + 4 * NR
WAVES = G // 4
SCALE2 = (DH + DR) ** -0.5
BIG = 1e30
FMIN = -3.4e38
MAGIC = 12582912.0
F = 1024
EPS = 1e-5

_COLS = [("ident", 128), ("mod16", HALF), ("smask", W80 + 128), ("iota", 2), ("cidx", 2 * HALF), ("sidx", 2 * HALF),
         ("cloc", 2 * HALF), ("sloc", 2 * HALF), ("tabx", NR), ("taby", NR), ("fill", 2 * 192), ("vsum", DK + 1)]
COL, NCONST = {}, 0
for _n, _w in _COLS:
    COL[_n] = (NCONST, NCONST + _w)
    NCONST += _w


def constants():
    c = np.zeros((128, NCONST), np.float64)

    def put(name, value):
        a, b = COL[name]
        c[:, a:b] = value.reshape(128, b - a)

    p = np.arange(128)
    put("ident", np.eye(128))
    put("mod16", (p[:, None] % HALF == np.arange(HALF)[None]).astype(float))
    q = 4 * (p // 32) + p % 4
    j = np.arange(W80)
    window = np.where((j[None] >= q[:, None] + 1) & (j[None] <= q[:, None] + LW), 0.0, -BIG)
    ranks = np.where((p % 4)[:, None] == (np.arange(128) // NR)[None], 0.0, -BIG)
    put("smask", np.concatenate([window, ranks], 1))
    put("iota", np.stack([p, p + 128], 1).astype(float))
    theta = (np.float32(1.0) / np.float32(10000.0) ** (np.float32(2.0) * np.arange(HALF, dtype=np.float32)
                                                       / np.float32(DR))).astype(np.float32).astype(np.float64)
    t = p[:, None] + 128 * np.arange(2)[None]
    ang = t[:, :, None] * theta
    put("cidx", np.cos(ang)); put("sidx", np.sin(ang))
    ang = (t + np.maximum(0, t - (LW - 1)))[:, :, None] * theta
    put("cloc", np.cos(ang)); put("sloc", np.sin(ang))
    rank = LW + np.arange(NR)
    a = rank[None] * np.tile(theta, 8)[:, None]
    x, y = np.ones((128, NR)), np.zeros((128, NR))
    x[64:96], y[64:96] = np.cos(a[64:96]), -np.sin(a[64:96])
    x[96:112], y[96:112] = -np.sin(a[96:112]), -np.cos(a[96:112])
    x[112:], y[112:] = np.sin(a[112:]), np.cos(a[112:])
    put("tabx", x); put("taby", y)
    fill = np.full((128, 2, 192), -3.3e38)
    s = np.arange(192)
    for tile in range(2):
        past = s[None] <= t[:, tile][:, None] - LW
        fill[:, tile][past] = 0.0
    ahead = (s[None] > t[:, 0][:, None]) & (s[None] < KK) | ((t[:, 0] < LW)[:, None] & (s[None] < KK))
    fill[:, 0] = np.where(ahead, -(2e38 + s * 1e35)[None], fill[:, 0])
    put("fill", fill)
    vsum = np.zeros((128, DK + 1))
    for n in range(3):
        vsum[16 * n:16 * n + 16, 0:16] = np.eye(16)
    vsum[3 * DK, DK] = 1.0
    put("vsum", vsum)
    return c.astype(np.float32)


SEMS = """
    kst_in0 kst_in1 kst_in2 ctx_in0 ctx_in1 ctx_in2 ctx_in3 kd_out0 kd_out1 id_in ctxT_ps rd_in wkv_in bias_in
    x_in bq_in wq_in fw_in const_in k1_done k2_done k3_done wo_in aw_in fq kst_ones kst_piece2 b_done out_done
    out_dma pool_chain ones_set xb_done v2_done v3_done dl_v tabs_done exp_done lo_pool x1_done kmu_done krot
    mu_done rot_loc rot_rank ka1_done kar_done ka2_done kaug idx_done d_pool act_chain v_ps ctxT_a kT_ps qaT_ps
    qa_sb rd_col dl_sin fqT_ps fqT_sb vf_done v1_done bq4 std_done xnT_ps xnT_sb vr_done fround kr_done fabs
    wuT_ps wuT_sb wa_ps wa_sb wb_ps wb_sb pv_done po_sb mT_ps m_ready oT_ps oT_sb xT2_ps xT2_sb qi_ps qi_sb
    ix_ps relu cq_ps cq_sb ck_sb mu_ps kmu_ln mu_ln qa2_ps qa2_sb kl_sb cw_ps cw_sb klT_ps klT_sb qlT_ps qrT_ps
    qlT_sb qrT_sb s_max p_done pT_ps ptw_sb o2_ps oct_sb rot_dup cs_ps cs_sb x2_done hqT_ps hqT_sb gu_ps dq silu
    pqT_ps pqT_sb ctxT_v xn_done q_ps a_read a_done fscale fsum_ps qs_done ident_b m_split o_read lo_dve comb_ps
    y1_ps xn2 ki_ps ck_ps ki_sb d_dve e_done bc_ps kg_sb s_ps dg_done ptg_sb y2_ps kg_ps hq_done pq_done y3_ps
    dve_chain kst_piece0 kst_piece1
""".split()


def build(nc, consts, a, out):
    ctx = ExitStack()
    with ctx:
        def sb(name, shape, dt=fp32):
            return ctx.enter_context(nc.sbuf_tensor(name, shape, dt))

        s = {n: ctx.enter_context(nc.semaphore(n)) for n in SEMS}
        PS = ctx.enter_context(nc.psum_tensor("PS", [128, 8, 512], fp32))
        kd = nc.dram_tensor("k_parts", (3, D, S), bf16, kind="Internal").ap()

        C = sb("C", [128, NCONST])

        def const(name):
            return C[:, COL[name][0]:COL[name][1]]

        ident = const("ident")
        identb = sb("identb", [128, 128], bf16)
        onesb = sb("onesb", [128, 128], bf16)
        onesf = sb("onesf", [128, 128])
        smaskb = sb("smaskb", [128, SW], bf16)
        xres = sb("xres", [128, NT, D])
        ln = sb("ln", [128, NT, 16])
        mv = sb("mv", [128, NT, 2])
        std = sb("std", [128, NT])
        rstd = sb("rstd", [128, NT])
        eps = sb("eps", [128, 1])
        halfpi = sb("halfpi", [128, 1])
        nmagic = sb("nmagic", [128, 1])
        scrap = sb("scrap", [128, 1])
        bqkvo = sb("bqkvo", [128, 3, D])
        bkcol = sb("bkcol", [128, 2])
        small = sb("small", [128, 64])
        Wuq = sb("Wuq", [128, 512]); Wuk = sb("Wuk", [64, 512]); Wuv = sb("Wuv", [64, 512])
        Wout = sb("Wout", [128, 4, 256]); Wdq = sb("Wdq", [128, 2, 128]); Wqr = sb("Wqr", [128, 256])
        Wiq = sb("Wiq", [128, 2, 256]); Wik = sb("Wik", [128, 2, 128]); Wck = sb("Wck", [128, 2, 96])
        iwb = sb("iwb", [128, NI])
        WA = sb("WA", [128, 512])
        WB = sb("WB", [128, H2 // 2, 256])
        rdel = sb("rdel", [128, 17])
        trig = sb("trig", [128, 4, 17])
        ctab = sb("ctab", [128, 2, 2, NT, DR])
        rtab = sb("rtab", [128, NR])
        tmp32 = sb("tmp32", [128, 4 * HALF])
        WgT = sb("WgT", [128, 2, F], bf16); WuT = sb("WuT", [128, 2, F], bf16); WdT = sb("WdT", [128, 8, D], bf16)
        fstat = sb("fstat", [128, 12])

        ARENA = sb("ARENA", [128, 160000 // 4])
        here = [0]

        def part(shape, dt=fp32, at=None):
            n = int(np.prod(shape)) * (2 if dt in (bf16, fp16) else 4)
            o = here[0] if at is None else at
            if at is None:
                here[0] += (n + 31) // 32 * 32
                assert here[0] <= 160000, here
            v = ARENA[:, o // 4:(o + n + 3) // 4]
            if dt != fp32:
                v = v.bitcast(dt)
            if len(shape) > 1:
                names = "abcd"[:len(shape)]
                v = v.rearrange(f"p ({' '.join(names)}) -> p {' '.join(names)}",
                                **{k: n_ for k, n_ in zip(names, shape)})
            return v

        V = part([KT, H1, VW], bf16)
        Kst = [part([S], bf16) for _ in range(NKST)]
        QA = part([H1, T], bf16)
        kring = [[part([2, CK], bf16) for _ in range(3)] for _ in range(2)]
        kres = part([2, CK])
        p_at = here[0]
        ctxr = [part([TPC, D]) for _ in range(4)]
        ctxT = [part([2, CK]) for _ in range(2)]
        Pm = [part([TPC, T], at=p_at + 4096 * i) for i in range(NP)]
        Plo = [part([TPC, T], fp16, at=p_at + 4096 * NP + 2048 * i) for i in range(NP)]
        QS = part([NT, H1, SROWS], bf16)
        w_at = here[0]
        WQ, WK, WV, WO = (part([2, D]) for _ in range(4))
        xb = part([NT, D])
        mxp = part([2, NT, 8]); nm1 = part([2, NT]); rec1 = part([2, NT])
        O = part([NT, D], at=w_at); OT = part([2, T], at=w_at + 2048)
        po = [part([T]) for _ in range(2)]
        fraw = [part([8 * 256], at=KT * H1 * VW * 2 + 8192 * i) for i in range(3)]
        f_at = here[0]
        fq = [part([2048], bf16) for _ in range(2)]
        fq.append(fq[0])
        qf = part([NT, D], at=f_at); q2f = part([NT, D], at=f_at + 2048)
        xn = part([NT, D], at=f_at + 4096); xnT = part([2, T], at=f_at + 6144)
        vf = [part([TPC, D]) for _ in range(2)]
        WuqT = part([4, 128], at=f_at); WukT = part([4, 64], at=f_at + 2048)
        WuvT = part([4, 64], at=f_at + 3072)

        here[0] = 0
        DD = part([GR * 16, NR], bf16)
        E0 = part([GR * 512], bf16); E1 = part([4 * 512], bf16)
        KGs = part([GR * 512])
        CS = part([GR, 4, DC])
        QR = part([NT, H2, 128]); QL = part([NT, H2, 96])
        QRT = part([G * 4, H2, 4]); QLT = part([G * 4, H2, 4])
        xn2 = part([NT, D], at=0); xT = part([2, T])
        qiT = part([2, T]); kiT = part([T]); cqT = part([T])
        ckr = part([NT, DR]); CW = part([GR, DC])
        rl = [part([2, 2, 96]), part([2, 2, 192])]
        IX = [part([96]), part([192])]
        topv = part([NT, NR]); topi = part([NT, NR]); topf = part([NT, NR], bf16)
        mu = part([NT, H2, DR]); mua = part([NT, H2, DR], at=2048)
        rot = part([NT, H2, DR], at=2048 + 2048); rot2 = part([NT, H2, DR])
        kmua = part([NT, DR]); krt = part([NT, DR]); krt2 = part([NT, DR])
        KA = part([NT, 128]); KAr = part([NT, 128]); KA1, KA2, KA3 = (part([NT, 128], bf16) for _ in range(3))
        KL = part([NT, 96]); KLT = part([T])
        P2 = [part([4, SW]) for _ in range(2)]; DG = [part([4, 128]) for _ in range(2)]
        PTw = [part([512]) for _ in range(2)]; PTg = [part([512]) for _ in range(2)]
        OCT = part([H2 // 2, T])
        smax = part([G]); nmb = part([G]); rsum = part([G]); rec2 = part([G])

        here[0] = 0
        h3 = part([NT, D]); hr = part([NT, D]); hq = part([NT, D], bf16); hqT = part([2, T], bf16)
        sg = part([NT, F]); pr = part([NT, F]); pr2 = part([NT, F]); pq = part([NT, F], bf16)
        pqT = part([8, T], bf16)
        res = part([NT, D])

        ctx_v = a["ctx_1024"].rearrange("b (p t) n -> (b p) t n", p=128)
        x_v = a["x"].rearrange("b (t p) n -> p (b t) n", p=128)
        out_v = out.rearrange("b (t p) n -> p (b t) n", p=128)
        kst_in = [s["kst_in0"], s["kst_in1"], s["kst_in2"]]
        ctx_in = [s["ctx_in0"], s["ctx_in1"], s["ctx_in2"], s["ctx_in3"]]
        kd_out = [s["kd_out0"], s["kd_out1"]]
        ORDER = [(kind, c - (kind == "vb")) for c in range(CH + 1) for kind in ("k", "vb", "va")]
        ORDER = [(kind, c) for kind, c in ORDER if 0 <= c < CH]
        NA = 2 * CH
        NB = KT // TPC
        STEPS = H1 * NB
        UPS = NA // NB
        AHEAD = NA + UPS * LEAD
        fw = [a["L0_ffn_w_gate"].rearrange("(t p) n -> p t n", p=128),
              a["L0_ffn_w_up"].rearrange("(t p) n -> p t n", p=128),
              a["L0_ffn_w_down"].rearrange("(t p) n -> p t n", p=128)]
        FQ_AT = [3, 4, 5]
        PIECES = [0, 4, 6, CH]
        PIECE_AT = [4, 6]
        EARLY = 4
        EARLY_AT = {6: 0, 7: 2}

        def bank(b, n=1):
            return PS[:, b:b + n, :].rearrange("p a b -> p (a b)")

        def bc(v, shape):
            return v.broadcast_to(shape)

        def a_bank(n):
            return n % 2 + (6 if n < EARLY else 0)

        def pool_tiles(n):
            if n >= STEPS - NB:
                return 1
            return TPC - 2 if n % 4 == 3 else TPC - 1

        def p_hi(n):
            return Pm[n % NP].rearrange("p a b -> p (a b)").bitcast(bf16).rearrange("p (a b e) -> p a b e", a=TPC, e=2)[:, :, :, 1]

        def vpart(c, n):
            return V[:, TPC * c:TPC * c + TPC, :, DK * n:DK * n + DK]

        vf_v = [x_.rearrange("p a (h d) -> p a h d", h=H1) for x_ in vf]

        def seed(engine, j):
            t0 = LW + 32 * j
            tile, tt = t0 // 128, t0 % 128
            return engine.tensor_tensor(DD[:, 32 * j:32 * j + 32, :],
                                        bc(identb[:, tt:tt + 32].unsqueeze(2), [128, 32, NR]),
                                        bc(topf[:, tile, :].unsqueeze(1), [128, 32, NR]), ALU.mult)

        def scores(k):
            return PS[:, 6 + k // 2, 256 * (k % 2):256 * (k % 2) + SW]

        S_AT, T_AT, V_AT = {1: 5, 2: 9}, {0: 2, 1: 7, 2: 11}, {0: 3, 1: 8, 2: 11}
        Q_AT = {3: (0,), 4: (1, 2, 3)}

        GATE_AT, UP_AT = (6, 0), (2, 4)

        block = ctx.enter_context(nc.Block())

        @block.sync
        def _(sp):
            first = COL["mod16"][1]
            sp.dma_start(C[:, 0:first], consts[:, 0:first]).then_inc(s["id_in"], 16)

            def w256(dst, src, sem):
                sp.dma_start(dst, src.rearrange("(c p) n -> p c n", p=128)).then_inc(sem, 16)

            def load_ctx(c):
                if c >= 4:
                    sp.wait_ge(s["ctxT_ps"], c - 3)
                sp.dma_start(ctxr[c % 4], ctx_v[:, c * TPC:(c + 1) * TPC, :]).then_inc(ctx_in[c % 4], 16)

            load_ctx(0)
            sp.dma_start(rdel[:, 0:16], a["L0_attn_raw_delta"].partition_broadcast(128)).then_inc(s["rd_in"], 16)
            w256(WK, a["L0_xattn_W_K"], s["wkv_in"])
            for m in range(2):
                sp.dma_start(bkcol[:, m:m + 1], a["L0_xattn_b_K"][128 * m:128 * m + 128].rearrange("(p o) -> p o", o=1))\
                  .then_inc(s["bias_in"], 16)
            w256(WV, a["L0_xattn_W_V"], s["wkv_in"])
            sp.dma_start(bqkvo[:, 1, :], a["L0_xattn_b_V"].partition_broadcast(128)).then_inc(s["bias_in"], 16)
            sp.dma_start(bqkvo[:, 2, :], a["L0_xattn_b_O"].partition_broadcast(128)).then_inc(s["bias_in"], 16)
            load_ctx(1)
            sp.dma_start(xres[:, :, :], x_v).then_inc(s["x_in"], 16)
            sp.dma_start(bqkvo[:, 0, :], a["L0_xattn_b_Q"].partition_broadcast(128)).then_inc(s["bq_in"], 16)
            w256(WQ, a["L0_xattn_W_Q"], s["wq_in"])
            load_ctx(2)
            load_ctx(3)
            for n in range(3):
                sp.dma_start(fraw[n].rearrange("p (t n) -> p t n", t=8 if n < 2 else 2), fw[n]).then_inc(s["fw_in"], 16)
            sp.dma_start(C[:, first:], consts[:, first:]).then_inc(s["const_in"], 16)

            def store_k(c):
                for n, done in enumerate((s["k1_done"], s["k2_done"], s["k3_done"])):
                    sp.wait_ge(done, c + 1)
                    sp.dma_start(kd[n, :, c * CK:(c + 1) * CK].rearrange("(m p) n -> p m n", p=128),
                                 kring[c % 2][n]).then_inc(kd_out[c % 2], 16)

            def load_k(h, keys, sem):
                for b in range(NBLK):
                    sp.dma_start(Kst[h % NKST][16 * b:16 * b + 16, keys], kd[KBLK[b], 16 * h:16 * h + 16, keys])\
                      .then_inc(sem, 16)

            for c in range(CH):
                if c + 4 < CH:
                    load_ctx(c + 4)
                if c == 3:
                    w256(WO, a["L0_xattn_W_O"], s["wo_in"])
                    w256(Wdq[:, :, :], a["L0_attn_W_dq"], s["aw_in"])
                    w256(Wiq[:, :, :], a["L0_attn_idx_wq"], s["aw_in"])
                    for n in range(2):
                        w256(Wik[:, :, 64 * n:64 * n + 64], a["L0_attn_idx_wk"], s["aw_in"])
                    w256(Wck[:, :, 0:64], a["L0_attn_W_dkv"], s["aw_in"])
                    w256(Wck[:, :, 64:96], a["L0_attn_W_kr"], s["aw_in"])
                    sp.dma_start(Wuq[:, :], a["L0_attn_W_uq"]).then_inc(s["aw_in"], 16)
                    sp.dma_start(Wqr[:, :], a["L0_attn_W_qr"]).then_inc(s["aw_in"], 16)
                    sp.dma_start(Wuk[:, :], a["L0_attn_W_uk"]).then_inc(s["aw_in"], 16)
                    sp.dma_start(Wuv[:, :], a["L0_attn_W_uv"]).then_inc(s["aw_in"], 16)
                    sp.dma_start(Wout[:, :, :], a["L0_attn_W_out"].rearrange("(c p) n -> p c n", p=128)).then_inc(s["aw_in"], 16)
                    sp.dma_start(iwb[:, :], a["L0_attn_idx_w"].partition_broadcast(128)).then_inc(s["aw_in"], 16)
                if c in PIECE_AT:
                    p = PIECE_AT.index(c)
                    for n in range(2):
                        sp.wait_ge(kd_out[n], 48 * ((c + 1 - n) // 2))
                    if p == 0:
                        sp.wait_ge(s["fq"], 1)
                    load_k(0, slice(CK * PIECES[p], CK * PIECES[p + 1]), s[f"kst_piece{p}"])
                store_k(c)
            for n in range(3):
                sp.wait_ge(s["fq"], n + 1)
                sp.dma_start(Kst[n][QROWS:SROWS, :].rearrange("r (a n) -> r a n", a=32),
                             onesb[0:2, :].unsqueeze(1).broadcast_to([2, 32, 128])).then_inc(s["kst_ones"], 16)
            for n in range(2):
                sp.wait_ge(kd_out[n], CH // 2 * 3 * 16)
            load_k(0, slice(CK * PIECES[2], S), s["kst_piece2"])
            for h in range(1, H1):
                if h >= NKST:
                    sp.wait_ge(s["b_done"], NB * (h - NKST + 1))
                load_k(h, slice(0, S), kst_in[h % NKST])
            sp.wait_ge(s["out_done"], 1)
            sp.dma_start(out_v, res).then_inc(s["out_dma"], 16)
            sp.wait_ge(s["out_dma"], 16)

        @block.gpsimd
        def _(pool):
            n_link = [0]

            def link(ins):
                n_link[0] += 1
                ins.then_inc(s["pool_chain"], 1)
                pool.wait_ge(s["pool_chain"], n_link[0])

            pool.memset(eps[:, :], EPS)
            pool.memset(halfpi[:, :], float(np.pi / 2))
            pool.memset(nmagic[:, :], -MAGIC)
            pool.memset(onesf[:, :], 1.0)
            pool.memset(onesb[:, :], 1.0).then_inc(s["ones_set"], 1)
            pool.memset(V[:, :, :, 3 * DK:VW], 1.0).then_inc(s["ones_set"], 1)
            pool.wait_ge(s["x_in"], 16)
            pool.wait_ge(s["bias_in"], 64)
            pool.tensor_tensor(xb, xres[:, :, :], bc(bqkvo[:, 2:3, :], [128, NT, D]), ALU.add).then_inc(s["xb_done"], 1)
            def k3(c):
                pool.wait_ge(s["k2_done"], c + 1)
                if c >= 2:
                    pool.wait_ge(kd_out[c % 2], 48 * (c // 2))
                pool.tensor_tensor(kring[c % 2][2], kres, kring[c % 2][1], ALU.subtract).then_inc(s["k3_done"], 1)

            def v3(c):
                pool.wait_ge(s["v2_done"], c + 1)
                pool.tensor_tensor(vpart(c, 2), vf_v[c % 2], vpart(c, 1), ALU.subtract).then_inc(s["v3_done"], 1)

            def tables():
                pool.wait_ge(s["dl_v"], 1)
                pool.wait_ge(s["const_in"], 16)
                cd = bc(trig[:, 2:3, 0:16], [128, 2, 16])
                sd = bc(trig[:, 3:4, 0:16], [128, 2, 16])
                for n, (cn, sn) in enumerate((("cidx", "sidx"), ("cloc", "sloc"))):
                    cc = const(cn).rearrange("p (a b) -> p a b", a=2)
                    ss = const(sn).rearrange("p (a b) -> p a b", a=2)
                    t1 = tmp32[:, 0:32].rearrange("p (a b) -> p a b", a=2)
                    t2 = tmp32[:, 32:64].rearrange("p (a b) -> p a b", a=2)
                    pool.tensor_tensor(t1, cc, cd, ALU.mult)
                    link(pool.tensor_tensor(t2, ss, sd, ALU.mult))
                    pool.tensor_tensor(ctab[:, n, 0, :, 0:16], t1, t2, ALU.subtract)
                    link(pool.tensor_tensor(ctab[:, n, 1, :, 16:32], t1, t2, ALU.subtract))
                    pool.tensor_tensor(t1, ss, cd, ALU.mult)
                    link(pool.tensor_tensor(t2, cc, sd, ALU.mult))
                    pool.tensor_tensor(ctab[:, n, 0, :, 16:32], t1, t2, ALU.add)
                    link(pool.tensor_tensor(ctab[:, n, 1, :, 0:16], t1, t2, ALU.add))
                link(pool.tensor_copy(rtab[:, :], const("tabx")))
                link(pool.tensor_scalar(rtab[64:128, :], const("tabx")[64:128, :], trig[64:128, 2, 16:17], None, ALU.mult))
                link(pool.tensor_scalar(tmp32[64:128, 0:32], const("taby")[64:128, :], trig[64:128, 3, 16:17], None, ALU.mult))
                pool.tensor_tensor(rtab[64:128, :], rtab[64:128, :], tmp32[64:128, 0:32], ALU.add).then_inc(s["tabs_done"], 1)
                pool.wait_ge(s["tabs_done"], 1)

            for kind, c in ORDER:
                if kind == "k":
                    k3(c)
                elif kind == "vb":
                    v3(c)
                    if c == CH - 2:
                        tables()
            for n in range(STEPS):
                pool.wait_ge(s["exp_done"], n + 1)
                k = pool_tiles(n)
                pool.tensor_tensor(Plo[n % NP][:, 0:k, :], Pm[n % NP][:, 0:k, :],
                                   p_hi(n)[:, 0:k, :], ALU.subtract).then_inc(s["lo_pool"], 1)

            pool.wait_ge(s["x1_done"], 2)
            pool.wait_ge(s["kmu_done"], 1)
            km = KA[:, :, 64:96]
            pool.tensor_tensor(krt, km, ctab[:, 0, 0], ALU.mult)
            link(pool.tensor_tensor(krt2, km, ctab[:, 0, 1], ALU.mult))
            pool.tensor_tensor(KL[:, :, 64:80], krt[:, :, 0:16], krt[:, :, 16:32], ALU.subtract)
            pool.tensor_tensor(KL[:, :, 80:96], krt2[:, :, 0:16], krt2[:, :, 16:32], ALU.add).then_inc(s["krot"], 1)
            pool.wait_ge(s["mu_done"], 1)
            for n, dst in ((1, QL), (0, QR)):
                pool.tensor_tensor(rot, mu, bc(ctab[:, n, 0].unsqueeze(2), [128, NT, H2, DR]), ALU.mult)
                link(pool.tensor_tensor(rot2, mu, bc(ctab[:, n, 1].unsqueeze(2), [128, NT, H2, DR]), ALU.mult))
                pool.tensor_tensor(dst[:, :, :, 64:80], rot[:, :, :, 0:16], rot[:, :, :, 16:32], ALU.subtract)
                last = pool.tensor_tensor(dst[:, :, :, 80:96], rot2[:, :, :, 0:16], rot2[:, :, :, 16:32], ALU.add)
                last.then_inc(s["rot_loc"] if n else s["rot_rank"], 1)
                if n:
                    pool.wait_ge(s["rot_loc"], 1)
                    pool.wait_ge(s["ka1_done"], 1)
                    pool.tensor_tensor(KAr, KA, KA1, ALU.subtract).then_inc(s["kar_done"], 1)
                    pool.wait_ge(s["ka2_done"], 1)
                    pool.tensor_tensor(KA3, KAr, KA2, ALU.subtract).then_inc(s["kaug"], 1)
            pool.wait_ge(s["idx_done"], 2)
            pool.wait_ge(s["rot_rank"], 1)
            for j in range(DVE_DD, GR * 16 // 32):
                seed(pool, j).then_inc(s["d_pool"], 1)

        @block.scalar
        def _(act):
            n_link = [0]

            def link(ins):
                n_link[0] += 1
                ins.then_inc(s["act_chain"], 1)
                act.wait_ge(s["act_chain"], n_link[0])

            def load_table(func):
                link(act.activation(scrap[:, :], eps[:, :], func))

            def chunk(c):
                act.wait_ge(s["ctxT_ps"], c + 1)
                if c >= 2:
                    act.wait_ge(s["v_ps"], c - 1)
                act.activation(ctxT[c % 2][:, 0, :], bank(0), ACT.Copy).then_inc(s["ctxT_a"], 1)

            def k1(c):
                act.wait_ge(s["kT_ps"], c + 1)
                if c >= 2:
                    act.wait_ge(kd_out[c % 2], 48 * (c // 2))
                for m in range(2):
                    last = act.activation(kring[c % 2][0][:, m, :], bank(2 + m), ACT.Identity, bias=bkcol[:, m:m + 1])
                last.then_inc(s["k1_done"], 1)

            def qa(g):
                act.wait_ge(s["qaT_ps"], g + 1)
                act.activation(QA[0:QROWS, 4 * g:4 * g + 4, :],
                               PS[0:QROWS, 7 - g % 2, :].bitcast(bf16).rearrange("p (a b) -> p a b", a=4),
                               ACT.Copy).then_inc(s["qa_sb"], 1)

            act.wait_ge(s["ones_set"], 1)
            act.wait_ge(s["rd_col"], 1)
            link(act.activation(trig[:, 0, :], rdel[:, :], ACT.Sigmoid))
            act.activation(trig[:, 2, :], trig[:, 0, :], ACT.Sin, scale=float(np.pi)).then_inc(s["dl_sin"], 1)
            act.activation(trig[:, 3, :], trig[:, 0, :], ACT.Sin, scale=-float(np.pi), bias=halfpi[:, :])\
               .then_inc(s["dl_sin"], 1)
            chunk(0)
            act.wait_ge(s["bias_in"], 64)

            def mlp_columns(n):
                for half in range(2):
                    act.wait_ge(s["fqT_ps"], 2 * n + half + 1)
                    o = PS[:, 6 + half, :].bitcast(bf16)
                    if n < 2:
                        dst, src = (WgT, WuT)[n][:, half, :], o
                    else:
                        dst = WdT[:, :, 128 * half:128 * half + 128]
                        src = o.rearrange("p (a b) -> p a b", a=8)
                    act.activation(dst, src, ACT.Copy).then_inc(s["fqT_sb"], 1)

            for kind, c in ORDER:
                if kind == "va":
                    act.wait_ge(s["vf_done"], c + 1)
                    act.activation(vpart(c, 0), vf_v[c % 2], ACT.Copy).then_inc(s["v1_done"], 1)
                    if c == 0:
                        act.wait_ge(s["bq4"], 1)
                        act.activation(std[:, :], mv[:, :, 1], ACT.Sqrt, bias=eps[:, :]).then_inc(s["std_done"], 1)
                    if c == 1:
                        act.wait_ge(s["xnT_ps"], 1)
                        act.activation(xnT, bank(6).rearrange("p (a b) -> p a b", a=2), ACT.Copy).then_inc(s["xnT_sb"], 1)
                    if c == 3:
                        qa(0)
                        qa(1)
                    continue
                if kind == "vb":
                    act.wait_ge(s["vr_done"], c + 1)
                    act.activation(vpart(c, 1), vf_v[c % 2], ACT.Copy).then_inc(s["v2_done"], 1)
                    if c in FQ_AT:
                        n = FQ_AT.index(c)
                        act.wait_ge(s["fround"], n + 1)
                        if n == 2:
                            act.wait_ge(s["fqT_ps"], 2)
                        act.activation(fq[n], fraw[n], ACT.Identity, bias=nmagic[:, :]).then_inc(s["fq"], 1)
                    continue
                k1(c)
                if c + 1 < CH:
                    chunk(c + 1)
                if c == 4:
                    qa(2)
                    qa(3)
                act.wait_ge(s["kr_done"], 2 * (c + 1))
                act.activation(kring[c % 2][1], kres, ACT.Copy).then_inc(s["k2_done"], 1)
                if 1 <= c <= 3:
                    n = c - 1
                    act.wait_ge(s["fw_in"], 48)
                    act.activation((WgT, WuT, WdT)[n][:, :, :].rearrange("p a b -> p (a b)"), fraw[n], ACT.Abs,
                                   accum_out=fstat[:, n:n + 1]).then_inc(s["fabs"], 1)
                if c >= 5:
                    mlp_columns(c - 5)
            for n, src in enumerate((4, 5, 6)):
                act.wait_ge(s["wuT_ps"], n + 1)
                dst = (WuqT, WukT, WuvT)[n]
                w = dst.shape[2]
                act.activation(dst, bank(src)[:, 0:4 * w].rearrange("p (a b) -> p a b", a=4), ACT.Copy)\
                   .then_inc(s["wuT_sb"], 1)
            load_table(ACT.Exp)
            act.wait_ge(s["wa_ps"], 1)
            for e in range(2):
                last = act.activation(WA[:, :].rearrange("p (k e n) -> p k e n", e=2, n=64)[:, :, e, :],
                                      bank(7 - e)[:, 0:256].rearrange("p (k n) -> p k n", k=4), ACT.Copy)
            last.then_inc(s["wa_sb"], 1)
            act.wait_ge(s["wb_ps"], 1)
            for e in range(2):
                rows = slice(64 * e, 64 * e + 64)
                last = act.activation(WB[rows, :, :], PS[rows, 2 + 2 * e:4 + 2 * e, :].rearrange("p a (b n) -> p (a b) n", b=2),
                                      ACT.Copy)
            last.then_inc(s["wb_sb"], 1)

            def head_rows(h):
                act.wait_ge(s["pv_done"], NB * (h + 1))
                act.activation(po[h % 2][0:VW, :], PS[0:VW, 6 + h % 2, 0:T], ACT.Copy).then_inc(s["po_sb"], 1)

            def max_rows(h):
                act.wait_ge(s["mT_ps"], h + 1)
                act.activation(QA[QROWS:SROWS, h, :], PS[QROWS:SROWS, 6 + h % 2, 0:128].bitcast(bf16), ACT.Copy)\
                   .then_inc(s["m_ready"], 1)

            max_rows(0)
            for n in range(STEPS):
                act.wait_ge(s["b_done"], n + 1)
                if n >= NP:
                    act.wait_ge(s["pv_done"], n - NP + 1)
                b = 2 + 2 * (n % 2)
                act.activation(Pm[n % NP], PS[:, b:b + 2, :].rearrange("p a (b n) -> p (a b) n", b=2), ACT.Exp)\
                   .then_inc(s["exp_done"], 1)
                if n % NB == LAG and n > NB:
                    head_rows(n // NB - 1)
                if n % NB == NB - 1 and n + 1 < STEPS:
                    max_rows(n // NB + 1)
            head_rows(H1 - 1)
            load_table(ACT.Sqrt)
            act.wait_ge(s["oT_ps"], 1)
            act.activation(OT, bank(0).rearrange("p (a b) -> p a b", a=2), ACT.Copy).then_inc(s["oT_sb"], 1)

            act.wait_ge(s["x1_done"], 2)
            act.activation(std[:, :], mv[:, :, 1], ACT.Sqrt, bias=eps[:, :]).then_inc(s["std_done"], 1)
            load_table(ACT.Exp)
            act.wait_ge(s["xT2_ps"], 1)
            act.activation(xT, bank(0).rearrange("p (a b) -> p a b", a=2), ACT.Copy).then_inc(s["xT2_sb"], 1)
            act.wait_ge(s["qi_ps"], 1)
            act.activation(qiT, bank(1).rearrange("p (a b) -> p a b", a=2), ACT.Copy).then_inc(s["qi_sb"], 1)
            for tile in range(NT):
                act.wait_ge(s["ix_ps"], tile + 1)
                w = (96, 192)[tile]
                for par, b in enumerate(((5, 6), (0, 7))[tile]):
                    last = act.activation(rl[tile][:, par], bank(b)[:, 0:2 * w].rearrange("p (a b) -> p a b", a=2), ACT.Relu)
                last.then_inc(s["relu"], 1)
            act.wait_ge(s["cq_ps"], 1)
            act.activation(cqT, bank(3)[:, 0:256], ACT.Copy).then_inc(s["cq_sb"], 1)
            act.wait_ge(s["ck_sb"], 1)
            link(act.activation(kmua, ckr, ACT.Abs))
            link(act.activation(kmua, kmua, ACT.Exp, scale=-1.0))
            act.wait_ge(s["mu_ps"], 1)
            link(act.activation(mua, bank(1).rearrange("p (a h b) -> p a h b", a=2, h=H2), ACT.Abs))
            link(act.activation(mua, mua, ACT.Exp, scale=-1.0))
            act.activation(kmua, kmua, ACT.Ln, bias=1.0).then_inc(s["kmu_ln"], 1)
            act.activation(mua, mua, ACT.Ln, bias=1.0).then_inc(s["mu_ln"], 1)
            for tile in range(NT):
                act.wait_ge(s["qa2_ps"], tile + 1)
                src = bank(2 + tile).rearrange("p (h n) -> p h n", h=H2)
                act.activation(QL[:, tile, :, 0:64], src, ACT.Copy)
                act.activation(QR[:, tile, :, 0:64], src, ACT.Copy).then_inc(s["qa2_sb"], 1)
            act.activation(KL[:, :, 0:64], KA[:, :, 0:64], ACT.Copy).then_inc(s["kl_sb"], 1)
            act.wait_ge(s["kmu_done"], 1)
            act.activation(KA[:, :, 96:112], KA[:, :, 80:96], ACT.Copy)
            link(act.activation(KA[:, :, 112:128], KA[:, :, 64:80], ACT.Copy))
            act.activation(KA1, KA, ACT.Copy).then_inc(s["ka1_done"], 1)
            act.wait_ge(s["cw_ps"], 1)
            act.activation(CW[0:W80], PS[0:W80, 5:7, :].rearrange("p a (b n) -> p (a b) n", b=8)[:, 0:GR, :],
                           ACT.Copy).then_inc(s["cw_sb"], 1)
            act.wait_ge(s["klT_ps"], 1)
            act.activation(KLT[0:96], bank(4)[0:96, 0:256], ACT.Copy).then_inc(s["klT_sb"], 1)

            def q_columns(n, loc):
                tile, hh = n // 2, n % 2
                act.wait_ge(s["qlT_ps"] if loc else s["qrT_ps"], n + 1)
                rows = 96 if loc else 128
                dst = (QLT if loc else QRT)[0:rows, 32 * tile:32 * tile + 32, 4 * hh:4 * hh + 4, :]\
                    .rearrange("p c h q -> p h c q")
                b = 2 + n if loc else 7 - n % 2
                act.activation(dst, PS[0:rows, b, :].rearrange("p (h c q) -> p h c q", h=4, c=32), ACT.Copy)\
                   .then_inc(s["qlT_sb"] if loc else s["qrT_sb"], 1)

            def exps(w, half):
                act.wait_ge(s["s_max"], 2 * w + half + 1)
                n = SW if w else KK
                for k in (2 * half, 2 * half + 1):
                    g = 4 * w + k
                    last = act.activation(P2[w % 2][:, k, 0:n], scores(k)[:, 0:n], ACT.Exp, scale=SCALE2,
                                          bias=nmb[:, g:g + 1], accum_out=rsum[:, g:g + 1])
                last.then_inc(s["p_done"], 1)

            def p_window(w):
                act.wait_ge(s["pT_ps"], w + 1)
                act.activation(PTw[w % 2], bank(2 if w == WAVES - 1 else 6), ACT.Copy).then_inc(s["ptw_sb"], 1)

            def o_columns(w):
                act.wait_ge(s["o2_ps"], w + 1)
                src = PS[0:64, 4 if w == WAVES - 1 else 6, :].rearrange("p (c k e q) -> p c k e q", c=16, k=H2 // 2, e=2)
                for e in range(2):
                    last = act.activation(OCT[64 * e:64 * e + 64, :, 64 * w:64 * w + 64].rearrange("p k (c q) -> p c k q", q=4),
                                          src[:, :, :, e, :], ACT.Copy)
                last.then_inc(s["oct_sb"], 1)

            load_table(ACT.Exp)
            act.wait_ge(s["kar_done"], 1)
            act.activation(KA2, KAr, ACT.Copy).then_inc(s["ka2_done"], 1)
            for n in range(4):
                q_columns(n, True)
            exps(0, 0)
            exps(0, 1)
            act.wait_ge(s["rot_rank"], 1)
            act.activation(QR[:, :, :, 96:128], QR[:, :, :, 64:96], ACT.Copy).then_inc(s["rot_dup"], 1)
            for c in range(1, GR + 2):
                for w in range(WAVES - 1):
                    if S_AT.get(w) == c - 1:
                        exps(w, 0)
                        exps(w, 1)
                    if V_AT[w] == c - 1:
                        o_columns(w)
                    if T_AT[w] == c:
                        p_window(w)
                for n in Q_AT.get(c - 1, ()):
                    q_columns(n, False)
                if c >= 2:
                    act.wait_ge(s["cs_ps"], c - 1)
                    act.activation(CS[:, c - 2], bank(4 + c % 2)[:, 0:256].rearrange("p (a b) -> p a b", a=4),
                                   ACT.Copy).then_inc(s["cs_sb"], 1)
                if c >= GR:
                    exps(WAVES - 1, c - GR)
            load_table(ACT.Sqrt)
            p_window(WAVES - 1)

            def deviation(tile):
                act.wait_ge(s["x2_done"], tile + 1)
                act.activation(std[:, tile:tile + 1], mv[:, tile, 1:2], ACT.Sqrt, bias=eps[:, :]).then_inc(s["std_done"], 1)

            deviation(0)
            o_columns(WAVES - 1)

            def h_columns(tile):
                act.wait_ge(s["hqT_ps"], tile + 1)
                act.activation(hqT[:, :, 128 * tile:128 * tile + 128],
                               PS[:, 5, 0:128].bitcast(bf16).rearrange("p (a b) -> p a b", a=2), ACT.Copy)\
                   .then_inc(s["hqT_sb"], 1)

            def gate(tile):
                act.wait_ge(s["gu_ps"], 2 * tile + 1)
                act.wait_ge(s["dq"], 2 * tile + 2)
                act.activation(sg[:, tile, :], bank(GATE_AT[tile], 2), ACT.Silu, scale=small[:, 4 + tile:5 + tile])\
                   .then_inc(s["silu"], 1)

            h_columns(0)
            deviation(1)
            gate(0)
            h_columns(1)
            gate(1)
            for tile in range(NT):
                act.wait_ge(s["pqT_ps"], tile + 1)
                act.activation(pqT[:, :, 128 * tile:128 * tile + 128],
                               PS[:, 6 + tile, :].bitcast(bf16).rearrange("p (a b) -> p a b", a=8), ACT.Copy)\
                   .then_inc(s["pqT_sb"], 1)

        @block.tensor
        def _(pe):
            def mm(o, l, r, start=True, stop=True, shared=False):
                return pe.matmul(o, l, r, start=start, stop=stop, skip_group_check=shared)

            def transpose_ctx(c):
                pe.wait_ge(ctx_in[c % 4], 16 * (c // 4 + 1))
                if c:
                    pe.wait_ge(s["ctxT_a"], c)
                    pe.wait_ge(s["ctxT_v"], c)
                for cc in range(2):
                    for k in range(TPC):
                        last = pe.transpose(bank(cc)[:, 128 * k:128 * k + 128],
                                            ctxr[c % 4][:, k, 128 * cc:128 * cc + 128], ident)
                last.then_inc(s["ctxT_ps"], 1)

            def project_k(c):
                pe.wait_ge(s["ctxT_a"], c + 1)
                pe.wait_ge(s["ctxT_v"], c + 1)
                if c == 0:
                    pe.wait_ge(s["wkv_in"], 32)
                else:
                    pe.wait_ge(s["kr_done"], 2 * c)
                for m in range(2):
                    for cc in range(2):
                        last = mm(bank(2 + m), WK[:, cc, 128 * m:128 * m + 128], ctxT[c % 2][:, cc, :],
                                  start=cc == 0, stop=cc == 1)
                last.then_inc(s["kT_ps"], 1)

            def project_v(c):
                if c:
                    pe.wait_ge(s["vf_done"], c)
                for k in range(TPC):
                    for cc in range(2):
                        last = mm(bank(4 + k // 2)[:, 256 * (k % 2):256 * (k % 2) + 256],
                                  ctxT[c % 2][:, cc, 128 * k:128 * k + 128], WV[:, cc, :], start=cc == 0, stop=cc == 1)
                last.then_inc(s["v_ps"], 1)

            def transpose_x():
                for tile in range(NT):
                    pe.wait_ge(s["xn_done"], tile + 1)
                    for c in range(2):
                        last = pe.transpose(bank(6)[:, 256 * c + 128 * tile:256 * c + 128 * tile + 128],
                                            xn[:, tile, 128 * c:128 * c + 128], ident)
                last.then_inc(s["xnT_ps"], 1)

            def project_q():
                pe.wait_ge(s["xnT_sb"], 1)
                pe.wait_ge(s["wq_in"], 16)
                for tile in range(NT):
                    for c in range(2):
                        last = mm(bank(7)[:, 256 * tile:256 * tile + 256], xnT[:, c, 128 * tile:128 * tile + 128],
                                  WQ[:, c, :], start=c == 0, stop=c == 1)
                last.then_inc(s["q_ps"], 1)

            def transpose_q(g):
                if g >= 2:
                    pe.wait_ge(s["qa_sb"], g - 1)
                o = PS[:, 7 - g % 2, :].bitcast(bf16)
                for h in range(4):
                    for tile in range(NT):
                        n = 256 * h + 128 * tile
                        last = pe.transpose(o[0:QROWS, n:n + 128], QS[:, tile, 4 * g + h, 0:QROWS], identb[:, :])
                last.then_inc(s["qaT_ps"], 1)

            def a_unit(n):
                h, u = n // NA, n % NA
                if h == 0:
                    if u // 2 in PIECES and u % 2 == 0:
                        pe.wait_ge(s[f"kst_piece{PIECES.index(u // 2)}"], 16 * NBLK)
                elif u == 0:
                    pe.wait_ge(kst_in[h % NKST], 16 * NBLK * (h // NKST + (h % NKST > 0)))
                if n >= 2:
                    pe.wait_ge(s["a_read"], n - 1)
                mm(bank(a_bank(n)), QA[0:QROWS, h, 128 * (u % 2):128 * (u % 2) + 128],
                   Kst[h % NKST][0:QROWS, CK * (u // 2):CK * (u // 2) + CK]).then_inc(s["a_done"], 1)

            def transpose_mlp(n):
                pe.wait_ge(s["fq"], n + 1)
                pe.wait_ge(s["fscale"], 3)
                pe.wait_ge(s["qa_sb"], 4)
                if n == 2:
                    pe.wait_ge(s["a_read"], 2)
                for half in range(2):
                    o = PS[:, 6 + half, :].bitcast(bf16)
                    if n:
                        pe.wait_ge(s["fqT_sb"], 2 * n - 1 + half)
                    for k in range(8):
                        if n < 2:
                            src = fq[n][:, 256 * k + 128 * half:256 * k + 128 * half + 128]
                        else:
                            src = fq[n][:, 1024 * half + 128 * k:1024 * half + 128 * k + 128]
                        last = pe.transpose(o[:, 128 * k:128 * k + 128], src, identb[:, :])
                    last.then_inc(s["fqT_ps"], 1)

            pe.wait_ge(s["id_in"], 16)
            transpose_ctx(0)
            for kind, c in ORDER:
                early = EARLY_AT.get(c) if kind == "va" else None
                if kind == "k":
                    project_k(c)
                    if c + 1 < CH:
                        transpose_ctx(c + 1)
                    if c == 2:
                        project_q()
                    if c == 4:
                        transpose_q(2)
                        transpose_q(3)
                    if c >= 5:
                        transpose_mlp(c - 5)
                elif kind == "va":
                    if c == 0:
                        pe.wait_ge(s["wkv_in"], 32)
                    project_v(c)
                    if c == 1:
                        transpose_x()
                    if 2 <= c <= 4:
                        n = c - 2
                        pe.wait_ge(s["ones_set"], 2)
                        pe.wait_ge(s["fabs"], n + 1)
                        pe.wait_ge(s["xnT_sb"], 1)
                        if n:
                            pe.wait_ge(s["fscale"], n)
                        if n == 2:
                            pe.wait_ge(s["qa_sb"], 4)
                        mm(PS[:, 6, n:n + 1], onesf[:, :], fstat[:, n:n + 1]).then_inc(s["fsum_ps"], 1)
                    if c == 3:
                        pe.wait_ge(s["qs_done"], 1)
                        pe.wait_ge(s["ident_b"], 1)
                        transpose_q(0)
                        pe.wait_ge(s["fscale"], 2)
                        transpose_q(1)
                if early is not None:
                    pe.wait_ge(s["fqT_sb"], 2 * (c - 4))
                    a_unit(early)
                    a_unit(early + 1)

            pe.wait_ge(s["ctxT_v"], CH)
            pe.wait_ge(s["ctxT_a"], CH)
            a_unit(EARLY)
            a_unit(EARLY + 1)
            pe.wait_ge(s["aw_in"], 16 * 12)
            pe.wait_ge(s["vf_done"], CH)
            for k in range(4):
                last = pe.transpose(bank(4)[:, 128 * k:128 * k + 128], Wuq[:, 128 * k:128 * k + 128], ident)
            last.then_inc(s["wuT_ps"], 1)
            a_unit(EARLY + 2)
            a_unit(EARLY + 3)
            for n, w in enumerate((Wuk, Wuv)):
                if n == 1:
                    pe.wait_ge(s["a_read"], EARLY)
                for k in range(4):
                    last = pe.transpose(bank(5 + n)[:, 64 * k:64 * k + 64], w[:, 128 * k:128 * k + 128], ident[0:64, 0:64])
                last.then_inc(s["wuT_ps"], 1)
            a_unit(EARLY + 4)
            a_unit(EARLY + 5)
            pe.wait_ge(s["wuT_sb"], 3)
            pe.wait_ge(s["kr_done"], 2 * CH)
            for h in range(H2):
                lo, k = 64 * (h % 2), h // 2
                last = mm(bank(7 - h % 2)[:, 64 * k:64 * k + 64], WuqT[lo:lo + 64, k, :], WukT[lo:lo + 64, k, :])
            last.then_inc(s["wa_ps"], 1)
            a_unit(EARLY + 6)
            a_unit(EARLY + 7)
            for h in range(H2):
                if h == H2 // 2:
                    a_unit(EARLY + 8)
                    a_unit(EARLY + 9)
                lo, k = 64 * (h % 2), h // 2
                last = mm(PS[lo:lo + 64, 2 + 2 * (h % 2) + k // 2, 256 * (k % 2):256 * (k % 2) + 256], WuvT[lo:lo + 64, k, :],
                          Wout[lo:lo + 64, k, :])
            last.then_inc(s["wb_ps"], 1)

            def max_rows(h):
                pe.wait_ge(s["m_split"], 2 * h + 2)
                if h >= 2:
                    pe.wait_ge(s["o_read"], h - 1)
                o = PS[:, 6 + h % 2, :].bitcast(bf16)
                for tile in range(NT):
                    last = pe.transpose(o[0:SROWS, 128 * tile:128 * tile + 128], QS[:, tile, h, :], identb[:, :])
                last.then_inc(s["mT_ps"], 1)

            def b_step(h, st):
                n = NB * h + st
                if st == 0:
                    pe.wait_ge(s["m_ready"], h + 1)
                    pe.wait_ge(s["kst_ones"], 48)
                if n >= 2:
                    pe.wait_ge(s["exp_done"], n - 1)
                for k in range(TPC):
                    b = 2 + 2 * (n % 2) + k // 2
                    key = 128 * (TPC * st + k)
                    last = mm(bank(b)[:, 256 * (k % 2):256 * (k % 2) + 256], Kst[h % NKST][0:SROWS, key:key + 128],
                              QA[0:SROWS, h, :])
                last.then_inc(s["b_done"], 1)

            def pv_step(n, first, end):
                h, st = n // NB, n % NB
                for k in range(first, end):
                    if k == 0:
                        pe.wait_ge(s["lo_pool"], n + 1)
                    if k == pool_tiles(n):
                        pe.wait_ge(s["lo_dve"], n + 1)
                    for part_ in range(2):
                        last = mm(PS[0:VW, 6 + h % 2, 0:T], V[:, TPC * st + k, h, :],
                                  Plo[n % NP][:, k, :] if part_ else p_hi(n)[:, k, :],
                                  start=st == 0 and k == 0 and part_ == 0, stop=st == NB - 1 and k == TPC - 1 and part_ == 1)
                if end == TPC:
                    last.then_inc(s["pv_done"], 1)

            def head_sum(h):
                pe.wait_ge(s["po_sb"], h + 1)
                for tile in range(NT):
                    last = mm(PS[:, 6 + h % 2, 256 + 32 * tile:256 + 32 * tile + DK + 1],
                              po[h % 2][0:VW, 128 * tile:128 * tile + 128], const("vsum")[0:VW, :])
                last.then_inc(s["comb_ps"], 1)

            for u in range(EARLY + 10, AHEAD):
                a_unit(u)
                if u == NA + 1:
                    pe.wait_ge(s["wa_sb"], 1)
                    pe.wait_ge(s["wb_sb"], 1)
                    max_rows(0)
            for n in range(STEPS):
                h, st = n // NB, n % NB
                b_step(h, st)
                for k in range(UPS):
                    if AHEAD + UPS * n + k < NA * H1:
                        a_unit(AHEAD + UPS * n + k)
                    if k == 1 and st == NB - 1 and h + 1 < H1:
                        max_rows(h + 1)
                    if n >= LAG:
                        pv_step(n - LAG, TPC // UPS * k, TPC // UPS * (k + 1))
                if st == LAG + 1 and h:
                    head_sum(h - 1)
            for n in range(STEPS - LAG, STEPS):
                pv_step(n, 0, TPC)
            head_sum(H1 - 1)

            pe.wait_ge(s["o_read"], H1)
            pe.wait_ge(s["a_read"], NA * H1)
            for tile in range(NT):
                for c in range(2):
                    last = pe.transpose(bank(0)[:, 256 * c + 128 * tile:256 * c + 128 * tile + 128],
                                        O[:, tile, 128 * c:128 * c + 128], ident)
            last.then_inc(s["oT_ps"], 1)
            pe.wait_ge(s["oT_sb"], 1)
            pe.wait_ge(s["wo_in"], 16)
            for tile in range(NT):
                for c in range(2):
                    last = mm(bank(2 + tile)[:, 0:256], OT[:, c, 128 * tile:128 * tile + 128], WO[:, c, :],
                              start=c == 0, stop=c == 1)
                last.then_inc(s["y1_ps"], 1)

            for tile in range(NT):
                pe.wait_ge(s["xn2"], tile + 1)
                for c in range(2):
                    last = pe.transpose(bank(0)[:, 256 * c + 128 * tile:256 * c + 128 * tile + 128],
                                        xn2[:, tile, 128 * c:128 * c + 128], ident)
            last.then_inc(s["xT2_ps"], 1)
            pe.wait_ge(s["xT2_sb"], 1)
            for k in range(2):
                for c in range(2):
                    last = mm(bank(1)[:, 256 * k:256 * k + 256], Wiq[:, c, 128 * k:128 * k + 128], xT[:, c, :],
                              start=c == 0, stop=c == 1)
            last.then_inc(s["qi_ps"], 1)
            for c in range(2):
                last = mm(bank(2)[:, 0:256], Wik[:, c, :], xT[:, c, :], start=c == 0, stop=c == 1)
            last.then_inc(s["ki_ps"], 1)
            for tile in range(NT):
                for c in range(2):
                    last = mm(bank(4)[:, 96 * tile:96 * tile + 96], xT[:, c, 128 * tile:128 * tile + 128], Wck[:, c, :],
                              start=c == 0, stop=c == 1)
            last.then_inc(s["ck_ps"], 1)
            pe.wait_ge(s["qi_sb"], 1)
            pe.wait_ge(s["ki_sb"], 1)
            for tile in range(NT):
                w = (96, 192)[tile]
                for par, b in enumerate(((5, 6), (0, 7))[tile]):
                    for k in range(2):
                        last = mm(bank(b)[:, w * k:w * k + w], qiT[64 * par:64 * par + 64, k, 128 * tile:128 * tile + 128],
                                  kiT[64 * par:64 * par + 64, 0:w])
                last.then_inc(s["ix_ps"], 1)
            for c in range(2):
                last = mm(bank(3)[:, 0:256], Wdq[:, c, :], xT[:, c, :], start=c == 0, stop=c == 1)
            last.then_inc(s["cq_ps"], 1)
            pe.wait_ge(s["cq_sb"], 1)
            for tile in range(NT):
                last = mm(bank(1)[:, 256 * tile:256 * tile + 256], cqT[:, 128 * tile:128 * tile + 128], Wqr[:, :])
            last.then_inc(s["mu_ps"], 1)
            for tile in range(NT):
                mm(bank(2 + tile), cqT[:, 128 * tile:128 * tile + 128], WA[:, :]).then_inc(s["qa2_ps"], 1)
            pe.wait_ge(s["relu"], 1)
            for g in range(GR):
                for c in range(2):
                    last = mm(PS[0:W80, 5 + g // 8, 64 * (g % 8):64 * (g % 8) + 64], xT[:, c, 16 * g:16 * g + W80],
                              Wck[:, c, 0:64], start=c == 0, stop=c == 1)
            last.then_inc(s["cw_ps"], 1)
            pe.wait_ge(s["krot"], 1)
            pe.wait_ge(s["kl_sb"], 1)
            for tile in range(NT):
                last = pe.transpose(bank(4)[0:96, 128 * tile:128 * tile + 128], KL[:, tile, :], ident)
            last.then_inc(s["klT_ps"], 1)

            def q_columns(n, loc):
                tile, hh = n // 2, n % 2
                rows = 96 if loc else 128
                for h in range(4):
                    last = pe.transpose(PS[0:rows, 2 + n if loc else 7 - n % 2, 128 * h:128 * h + 128],
                                        (QL if loc else QR)[:, tile, 4 * hh + h, :], ident)
                last.then_inc(s["qlT_ps"] if loc else s["qrT_ps"], 1)

            pe.wait_ge(s["relu"], 2)
            pe.wait_ge(s["mu_done"], 1)
            pe.wait_ge(s["qa2_sb"], 2)
            pe.wait_ge(s["rot_loc"], 1)
            pe.wait_ge(s["klT_sb"], 1)
            pe.wait_ge(s["cw_sb"], 1)
            q_columns(0, True)
            q_columns(1, True)
            DDf = DD.rearrange("p t r -> p (t r)")

            def broadcast_indices(c):
                if c < 2 * DVE_DD:
                    pe.wait_ge(s["d_dve"], c // 2 + 1)
                else:
                    pe.wait_ge(s["d_pool"], c // 2 + 1 - DVE_DD)
                if c >= 2:
                    pe.wait_ge(s["e_done"], c - 1)
                mm(bank(c % 2), onesb[:, :], DDf[:, 512 * c:512 * c + 512]).then_inc(s["bc_ps"], 1)

            broadcast_indices(0)
            broadcast_indices(1)
            q_columns(2, True)
            q_columns(3, True)
            qlt = QLT.rearrange("p c h q -> p (c h q)")
            qrt = QRT.rearrange("p c h q -> p (c h q)")

            def wave_scores(w, half):
                for k in (2 * half, 2 * half + 1):
                    g = 4 * w + k
                    o = scores(k)
                    if w == 0:
                        last = mm(o[:, 0:KK], qlt[0:96, 128 * g:128 * g + 128], KLT[0:96, 0:KK],
                                  start=k % 2 == 0, stop=True, shared=True)
                        continue
                    k0 = 16 * g - LW
                    mm(o, identb[:, :], smaskb[:, :], start=k % 2 == 0, stop=False, shared=True)
                    mm(o[:, 0:W80], qlt[0:96, 128 * g:128 * g + 128], KLT[0:96, k0:k0 + W80], start=False, stop=False,
                       shared=True)
                    pe.wait_ge(s["kg_sb"], g - 3)
                    for cc in range(4):
                        last = mm(o[32 * cc:32 * cc + 32, W80:SW], qrt[:, 128 * g + 32 * cc:128 * g + 32 * cc + 32],
                                  KGs[:, 512 * (g - 4) + 128 * cc:512 * (g - 4) + 128 * cc + 128], start=False, stop=True,
                                  shared=True)
                last.then_inc(s["s_ps"], 1)

            def p_columns(w):
                pe.wait_ge(s["dg_done"], 2 * w + 2)
                b = 2 if w == WAVES - 1 else 6
                n = W80 if w else KK
                for k in range(4):
                    last = mm(PS[0:n, b, 128 * k:128 * k + 128], P2[w % 2][:, k, 0:n], DG[w % 2][:, k, :])
                    if w:
                        last = mm(PS[:, b + 1, 128 * k:128 * k + 128], P2[w % 2][:, k, W80:SW], DG[w % 2][:, k, :])
                last.then_inc(s["pT_ps"], 1)

            def p_values(w):
                pe.wait_ge(s["ptw_sb"], w + 1)
                if w:
                    pe.wait_ge(s["ptg_sb"], w)
                    pe.wait_ge(s["cs_sb"], 4 * w)
                b = 4 if w == WAVES - 1 else 6
                n = W80 if w else KK
                for k in range(4):
                    g = 4 * w + k
                    last = mm(PS[0:64, b, 128 * k:128 * k + 128], KA[0:KK, 0, 0:64] if w == 0 else CW[0:W80, g - 4, :],
                              PTw[w % 2][0:n, 128 * k:128 * k + 128], start=k == 0, stop=w == 0, shared=True)
                    if w:
                        for cc in range(4):
                            n1 = 128 * k + 32 * cc
                            last = mm(PS[0:64, b, n1:n1 + 32], CS[:, g - 4, cc, :], PTg[w % 2][:, n1:n1 + 32],
                                      start=False, stop=True, shared=True)
                last.then_inc(s["o2_ps"], 1)

            def out_product(tile):
                pe.wait_ge(s["oct_sb"], 2 * tile + 2)
                for k in range(H2 // 2):
                    last = mm(bank(tile)[:, 0:256], OCT[:, k, 128 * tile:128 * tile + 128], WB[:, k, :],
                              start=k == 0, stop=k == H2 // 2 - 1)
                last.then_inc(s["y2_ps"], 1)

            pe.wait_ge(s["qlT_sb"], 4)
            wave_scores(0, 0)
            wave_scores(0, 1)
            pe.wait_ge(s["kaug"], 1)
            for c in range(1, GR + 2):
                if 2 <= c < GR:
                    broadcast_indices(c)
                for w in range(WAVES - 1):
                    if T_AT[w] == c:
                        p_columns(w)
                if 1 <= c <= GR:
                    g = c - 1
                    pe.wait_ge(s["e_done"], g + 1)
                    if g >= 2:
                        pe.wait_ge(s["kg_sb"], g - 1)
                    todo = [(E0[:, 512 * g:512 * g + 512], 0, k) for k in (KA1, KA2, KA3)]
                    if g >= 8:
                        todo += [(E1[:, 512 * (g - 8):512 * (g - 8) + 512], 1, k) for k in (KA1, KA2, KA3)]
                    for n, (e, tile, k) in enumerate(todo):
                        last = mm(bank(2 + g % 2), k[:, tile, :], e, start=n == 0, stop=n == len(todo) - 1)
                    last.then_inc(s["kg_ps"], 1)
                if c >= 2:
                    g = c - 2
                    pe.wait_ge(s["kg_sb"], g + 1)
                    if g >= 2:
                        pe.wait_ge(s["cs_sb"], g - 1)
                    for cc in range(4):
                        n = 512 * g + 128 * cc
                        last = pe.transpose(bank(4 + g % 2)[:, 64 * cc:64 * cc + 64], KGs[0:64, n:n + 128], ident[0:64, 0:64])
                    last.then_inc(s["cs_ps"], 1)
                for n in Q_AT.get(c, ()):
                    if n == 0:
                        pe.wait_ge(s["rot_dup"], 1)
                        pe.wait_ge(s["p_done"], 2)
                    if n == 1:
                        pe.wait_ge(s["oct_sb"], 1)
                    if n >= 2:
                        pe.wait_ge(s["qrT_sb"], n - 1)
                    q_columns(n, False)
                for w in range(WAVES - 1):
                    if S_AT.get(w) == c:
                        if w == 1:
                            pe.wait_ge(s["qrT_sb"], 4)
                        pe.wait_ge(s["oct_sb"], w)
                        if w > 1:
                            pe.wait_ge(s["ptg_sb"], w - 1)
                        wave_scores(w, 0)
                        wave_scores(w, 1)
                    if V_AT[w] == c:
                        p_values(w)
                if c >= GR:
                    pe.wait_ge(s["oct_sb"], WAVES - 1)
                    pe.wait_ge(s["ptg_sb"], WAVES - 2)
                    wave_scores(WAVES - 1, c - GR)
            pe.wait_ge(s["e_done"], GR)
            out_product(0)
            p_columns(WAVES - 1)
            pe.wait_ge(s["cs_sb"], GR)
            p_values(WAVES - 1)
            out_product(1)

            for tile in range(NT):
                pe.wait_ge(s["hq_done"], tile + 1)
                o = PS[:, 5, :].bitcast(bf16)
                for c in range(2):
                    last = pe.transpose(o[:, 128 * c:128 * c + 128], hq[:, tile, 128 * c:128 * c + 128], identb[:, :])
                last.then_inc(s["hqT_ps"], 1)
                if tile == 0:
                    pe.wait_ge(s["ptw_sb"], WAVES)
                    pe.wait_ge(s["ptg_sb"], WAVES - 1)
                else:
                    pe.wait_ge(s["x2_done"], 2)
                pe.wait_ge(s["hqT_sb"], tile + 1)
                for w, at in ((WgT, GATE_AT), (WuT, UP_AT)):
                    for half in range(2):
                        for c in range(2):
                            last = mm(bank(at[tile] + half), hqT[:, c, 128 * tile:128 * tile + 128],
                                      w[:, c, 512 * half:512 * half + 512], start=c == 0, stop=c == 1)
                    last.then_inc(s["gu_ps"], 1)
            def p_rows(tile):
                pe.wait_ge(s["pq_done"], tile + 1)
                pe.wait_ge(s["silu"], tile + 1)
                o = PS[:, 6 + tile, :].bitcast(bf16)
                for k in range(8):
                    last = pe.transpose(o[:, 128 * k:128 * k + 128], pq[:, tile, 128 * k:128 * k + 128], identb[:, :])
                last.then_inc(s["pqT_ps"], 1)

            for tile in range(NT):
                p_rows(tile)
                pe.wait_ge(s["pqT_sb"], tile + 1)
                for k in range(8):
                    last = mm(bank(2 + tile)[:, 0:256], pqT[:, k, 128 * tile:128 * tile + 128], WdT[:, k, :],
                              start=k == 0, stop=k == 7)
                last.then_inc(s["y3_ps"], 1)

        @block.vector
        def _(v):
            n_link = [0]

            def link(ins):
                n_link[0] += 1
                ins.then_inc(s["dve_chain"], 1)
                v.wait_ge(s["dve_chain"], n_link[0])

            def stats(tile):
                link(v.bn_stats(ln[:, tile, 0:6], xres[:, tile, :]))
                return v.bn_aggr(mv[:, tile, :], ln[:, tile, 0:6])

            def normalise(dst, n, done):
                v.wait_ge(s["std_done"], n)
                link(v.reciprocal(rstd[:, :], std[:, :]))
                for tile in range(NT):
                    v.tensor_scalar(dst[:, tile, :], xres[:, tile, :], mv[:, tile, 0:1], rstd[:, tile:tile + 1],
                                    ALU.subtract, ALU.mult).then_inc(done, 1)

            def blk(b, tile):
                return QS[:, tile, :, 16 * b:16 * b + 16]

            def hd(x_, tile):
                return x_[:, tile, :].rearrange("p (h d) -> p h d", h=H1)

            def split_q():
                v.wait_ge(s["q_ps"], 1)
                link(v.scalar_tensor_tensor(qf, bank(7).rearrange("p (a b) -> p a b", a=2), 0.25,
                                            bc(bqkvo[:, 0:1, :], [128, NT, D]), ALU.mult, ALU.add))
                for b in (0, 3, 5):
                    for tile in range(NT):
                        last = v.tensor_copy(blk(b, tile), hd(qf, tile))
                link(last)
                for tile in range(NT):
                    last = v.tensor_tensor(hd(q2f, tile), hd(qf, tile), blk(0, tile), ALU.subtract)
                link(last)
                for b in (1, 4):
                    for tile in range(NT):
                        last = v.tensor_copy(blk(b, tile), hd(q2f, tile))
                link(last)
                for tile in range(NT):
                    last = v.tensor_tensor(blk(2, tile), hd(q2f, tile), blk(1, tile), ALU.subtract)
                last.then_inc(s["qs_done"], 1)

            def ctx_evac(c):
                v.wait_ge(s["ctxT_ps"], c + 1)
                if c >= 2:
                    v.wait_ge(s["v_ps"], c - 1)
                v.tensor_copy(ctxT[c % 2][:, 1, :], bank(1)).then_inc(s["ctxT_v"], 1)

            def a_unit(n):
                h, u = n // NA, n % NA
                v.wait_ge(s["a_done"], n + 1)
                return v.tensor_reduce(mxp[:, h % 2, u % 2, u // 2:u // 2 + 1], bank(a_bank(n)), axis=AX.X, op=ALU.max)\
                    .then_inc(s["a_read"], 1)

            def v_first(c):
                v.wait_ge(s["v_ps"], c + 1)
                if c >= 2:
                    v.wait_ge(s["v3_done"], c - 1)
                for k in range(2):
                    last = v.tensor_tensor(vf[c % 2][:, 2 * k:2 * k + 2, :], bank(4 + k).rearrange("p (a n) -> p a n", a=2),
                                           bc(bqkvo[:, 1:2, :], [128, 2, D]), ALU.add)
                last.then_inc(s["vf_done"], 1)
                if 2 <= c <= 4:
                    n = c - 2
                    v.wait_ge(s["fsum_ps"], n + 1)
                    v.tensor_scalar(fstat[:, 4 + n:5 + n], PS[:, 6, n:n + 1], 1.0 / (F * D), 1e-5, ALU.mult, ALU.max)\
                     .then_inc(s["fscale"], 1)
                    v.wait_ge(s["fscale"], n + 1)
                    link(v.reciprocal(fstat[:, 8 + n:9 + n], fstat[:, 4 + n:5 + n]))

            def v_rest(c):
                v.wait_ge(s["v1_done"], c + 1)
                v.tensor_tensor(vf_v[c % 2], vf_v[c % 2], vpart(c, 0), ALU.subtract).then_inc(s["vr_done"], 1)
                if c in FQ_AT:
                    n = FQ_AT.index(c)
                    link(v.tensor_scalar(fraw[n], fraw[n], fstat[:, 8 + n:9 + n], -1.0, ALU.mult, ALU.max))
                    v.tensor_scalar(fraw[n], fraw[n], 1.0, MAGIC, ALU.min, ALU.add).then_inc(s["fround"], 1)

            v.wait_ge(s["id_in"], 16)
            v.wait_ge(s["rd_in"], 16)
            link(v.tensor_tensor(tmp32[:, 0:HALF], rdel[:, 0:HALF], const("mod16"), ALU.mult))
            v.tensor_reduce(rdel[:, HALF:HALF + 1], tmp32[:, 0:HALF], axis=AX.X, op=ALU.add).then_inc(s["rd_col"], 1)
            v.tensor_copy(identb[:, :], ident).then_inc(s["ident_b"], 1)
            ctx_evac(0)
            v.wait_ge(s["dl_sin"], 2)
            link(v.tensor_tensor(trig[:, 0, :], trig[:, 2, :], trig[:, 2, :], ALU.mult))
            link(v.tensor_tensor(trig[:, 1, :], trig[:, 2, :], trig[:, 3, :], ALU.mult))
            link(v.tensor_scalar(trig[:, 2, :], trig[:, 0, :], -2.0, 1.0, ALU.mult, ALU.add))
            v.tensor_scalar(trig[:, 3, :], trig[:, 1, :], -2.0, None, ALU.mult).then_inc(s["dl_v"], 1)
            v.wait_ge(s["bias_in"], 64)
            for kind, c in ORDER:
                early = EARLY_AT.get(c) if kind == "va" else None
                if kind == "k":
                    v.wait_ge(s["k1_done"], c + 1)
                    if c:
                        v.wait_ge(s["k3_done"], c)
                    for m in range(2):
                        v.scalar_tensor_tensor(kres[:, m, :], bank(2 + m), bkcol[:, m:m + 1], kring[c % 2][0][:, m, :],
                                               ALU.add, ALU.subtract).then_inc(s["kr_done"], 1)
                    if c + 1 < CH:
                        ctx_evac(c + 1)
                    if c == 1:
                        normalise(xn, 1, s["xn_done"])
                elif kind == "vb":
                    v_rest(c)
                else:
                    if c == 0:
                        v.wait_ge(s["x_in"], 16)
                        for tile in range(NT):
                            link(stats(tile))
                        v.wait_ge(s["bq_in"], 16)
                        v.tensor_scalar(bqkvo[:, 0, :], bqkvo[:, 0, :], 0.25, None, ALU.mult).then_inc(s["bq4"], 1)
                    v_first(c)
                    if c == 2:
                        split_q()
                    if c == 5:
                        v.wait_ge(s["const_in"], 16)
                        v.tensor_copy(smaskb[:, :], const("smask"))
                if early is not None:
                    a_unit(early)
                    a_unit(early + 1)

            def max_split(h):
                v.wait_ge(s["a_read"], NA * (h + 1))
                link(v.tensor_reduce(nm1[:, h % 2, :], mxp[:, h % 2, :, :], axis=AX.X, op=ALU.max, negate=True))
                v.tensor_copy(QS[:, :, h, QROWS], nm1[:, h % 2, :]).then_inc(s["m_split"], 1)
                v.wait_ge(s["m_split"], 2 * h + 1)
                v.tensor_tensor(QS[:, :, h, QROWS + 1], nm1[:, h % 2, :], QS[:, :, h, QROWS], ALU.subtract)\
                 .then_inc(s["m_split"], 1)

            def head_out(h):
                v.wait_ge(s["comb_ps"], h + 1)
                o = PS[:, 6 + h % 2, 256:320].rearrange("p (a b) -> p a b", a=2)
                link(v.reciprocal(rec1[:, h % 2, :], o[:, :, DK]))
                v.tensor_tensor(O[:, :, DK * h:DK * h + DK], o[:, :, 0:DK], bc(rec1[:, h % 2, :].unsqueeze(2), [128, NT, DK]),
                                ALU.mult).then_inc(s["o_read"], 1)

            def p_low(n):
                v.wait_ge(s["exp_done"], n + 1)
                k = pool_tiles(n)
                v.tensor_tensor(Plo[n % NP][:, k:TPC, :], Pm[n % NP][:, k:TPC, :],
                                p_hi(n)[:, k:TPC, :], ALU.subtract).then_inc(s["lo_dve"], 1)

            for u in range(EARLY, NA):
                a_unit(u)
            max_split(0)
            for u in range(NA, AHEAD):
                a_unit(u)
            for n in range(STEPS):
                h, st = n // NB, n % NB
                for k in range(UPS):
                    if AHEAD + UPS * n + k < NA * H1:
                        a_unit(AHEAD + UPS * n + k)
                    if k == 0 and n:
                        p_low(n - 1)
                if st == NB - 1 - LEAD and h + 1 < H1:
                    max_split(h + 1)
                if st == LAG + 2 and h:
                    head_out(h - 1)
            p_low(STEPS - 1)
            head_out(H1 - 1)
            v.wait_ge(s["xb_done"], 1)
            for tile in range(NT):
                v.wait_ge(s["y1_ps"], tile + 1)
                v.tensor_tensor(xres[:, tile, :], bank(2 + tile)[:, 0:256], xb[:, tile, :], ALU.add)\
                 .then_inc(s["dve_chain"], 1)
                n_link[0] += 1
                v.wait_ge(s["dve_chain"], n_link[0])
            for tile in range(NT):
                stats(tile).then_inc(s["x1_done"], 1)
            v.wait_ge(s["x1_done"], 2)
            normalise(xn2, 2, s["xn2"])
            v.wait_ge(s["ki_ps"], 1)
            v.tensor_copy(kiT, bank(2)[:, 0:256]).then_inc(s["ki_sb"], 1)
            v.wait_ge(s["ck_ps"], 1)
            ckp = bank(4)[:, 0:192].rearrange("p (a b) -> p a b", a=2)
            v.tensor_copy(KA[:, :, 0:64], ckp[:, :, 0:64])
            v.tensor_copy(ckr, ckp[:, :, 64:96]).then_inc(s["ck_sb"], 1)
            v.wait_ge(s["ck_sb"], 1)

            def step(ins):
                n_link[0] += 1
                ins.then_inc(s["dve_chain"], 1)
                return n_link[0]

            def after(count):
                v.wait_ge(s["dve_chain"], count)

            fills = const("fill").rearrange("p (a b) -> p a b", a=2)
            done = [0, 0]
            for h in range(NI):
                for tile in range(NT):
                    v.wait_ge(s["relu"], tile + 1)
                    n = (96, 192)[tile]
                    if h:
                        after(done[tile])
                    done[tile] = step(v.scalar_tensor_tensor(IX[tile], rl[tile][:, h % 2, h // 2, :], iwb[:, h:h + 1],
                                                             IX[tile] if h else fills[:, tile, 0:n], ALU.mult, ALU.add))
            for r in range(NR // 8):
                tv = [topv[:, tile, 8 * r:8 * r + 8] for tile in range(NT)]
                for tile in range(NT):
                    after(done[tile])
                    done[tile] = step(v.max(tv[tile], IX[tile]))
                for tile in range(NT):
                    after(done[tile])
                    done[tile] = step(v.max_index(topi[:, tile, 8 * r:8 * r + 8].bitcast(u32), tv[tile], IX[tile]))
                if r < NR // 8 - 1:
                    for tile in range(NT):
                        after(done[tile])
                        done[tile] = step(v.match_replace(IX[tile], tv[tile], IX[tile], FMIN))
                if r == 0:
                    v.wait_ge(s["kmu_ln"], 1)
                    v.scalar_tensor_tensor(KA[:, :, 64:96], ckr, 0.0, kmua, ALU.max, ALU.add).then_inc(s["kmu_done"], 1)
                    v.wait_ge(s["mu_ln"], 1)
                    v.scalar_tensor_tensor(mu, bank(1).rearrange("p (a h b) -> p a h b", a=2, h=H2), 0.0, mua,
                                           ALU.max, ALU.add).then_inc(s["mu_done"], 1)
            for tile in range(NT):
                after(done[tile])
                v.tensor_copy(topf[:, tile, :], topi[:, tile, :].bitcast(u32)).then_inc(s["idx_done"], 1)
            v.wait_ge(s["idx_done"], 2)
            seed(v, 0).then_inc(s["d_dve"], 1)

            def row_max(w, half):
                v.wait_ge(s["s_ps"], 2 * w + half + 1)
                g, n = 4 * w + 2 * half, SW if w else KK
                link(v.tensor_reduce(smax[:, g:g + 2], bank(6 + half).rearrange("p (a n) -> p a n", a=2)[:, :, 0:n],
                                     axis=AX.X, op=ALU.max))
                v.tensor_scalar(nmb[:, g:g + 2], smax[:, g:g + 2], -SCALE2, None, ALU.mult).then_inc(s["s_max"], 1)

            def diagonal(w, half):
                v.wait_ge(s["p_done"], 2 * w + half + 1)
                g = 4 * w + 2 * half
                link(v.reciprocal(rec2[:, g:g + 2], rsum[:, g:g + 2]))
                v.tensor_tensor(DG[w % 2][:, 2 * half:2 * half + 2, :], bc(ident.unsqueeze(1), [128, 2, 128]),
                                bc(rec2[:, g:g + 2].unsqueeze(2), [128, 2, 128]), ALU.mult).then_inc(s["dg_done"], 1)

            def p_ranks(w):
                v.wait_ge(s["pT_ps"], w + 1)
                v.tensor_copy(PTg[w % 2], bank(3 if w == WAVES - 1 else 7)).then_inc(s["ptg_sb"], 1)

            def one_hot(c):
                v.wait_ge(s["bc_ps"], c + 1)
                last = v.tensor_scalar(E0[:, 512 * c:512 * c + 512], bank(c % 2), const("iota")[:, 0:1], None,
                                       ALU.is_equal)
                if c >= 8:
                    last = v.tensor_scalar(E1[:, 512 * (c - 8):512 * (c - 8) + 512], bank(c % 2),
                                           const("iota")[:, 1:2], None, ALU.is_equal)
                last.then_inc(s["e_done"], 1)

            one_hot(0)
            one_hot(1)
            for j in range(1, DVE_DD):
                seed(v, j).then_inc(s["d_dve"], 1)
            row_max(0, 0)
            row_max(0, 1)
            v.wait_ge(s["tabs_done"], 1)
            for c in range(1, GR + 2):
                for w in range(WAVES - 1):
                    if S_AT.get(w) == c - 1:
                        row_max(w, 0)
                        row_max(w, 1)
                if 2 <= c < GR:
                    one_hot(c)
                if c == 1:
                    diagonal(0, 0)
                    diagonal(0, 1)
                if c <= GR:
                    g = c - 1
                    v.wait_ge(s["kg_ps"], g + 1)
                    v.tensor_tensor(KGs[:, 512 * g:512 * g + 512].rearrange("p (a r) -> p a r", a=16),
                                    bank(2 + g % 2).rearrange("p (a r) -> p a r", a=16),
                                    bc(rtab[:, :].unsqueeze(1), [128, 16, NR]), ALU.mult).then_inc(s["kg_sb"], 1)
                for w in range(1, WAVES - 1):
                    if S_AT[w] == c - 1:
                        diagonal(w, 0)
                        diagonal(w, 1)
                    if T_AT[w] == c:
                        p_ranks(w)
                if c >= GR:
                    row_max(WAVES - 1, c - GR)
            diagonal(WAVES - 1, 0)
            diagonal(WAVES - 1, 1)
            p_ranks(WAVES - 1)

            def quantise(tile, src, work, dst, col, done):
                am, sc, dq = small[:, 16 + tile:17 + tile], small[:, 20 + tile:21 + tile], small[:, col + tile:col + tile + 1]
                link(v.tensor_reduce(am, src, axis=AX.X, op=ALU.max, apply_absolute_value=True))
                link(v.tensor_scalar(am, am, 1e-5, None, ALU.max))
                link(v.reciprocal(sc, am))
                link(v.tensor_scalar(sc, sc, 127.0, None, ALU.mult))
                v.tensor_scalar(dq, am, 1.0 / 127.0, None, ALU.mult)
                link(v.tensor_scalar(work, src, sc, -128.0, ALU.mult, ALU.max))
                link(v.tensor_scalar(work, work, 127.0, MAGIC, ALU.min, ALU.add))
                v.tensor_scalar(dst, work, MAGIC, None, ALU.subtract).then_inc(done, 1)

            for tile in range(NT):
                v.wait_ge(s["y2_ps"], tile + 1)
                link(v.tensor_tensor(xres[:, tile, :], xres[:, tile, :], bank(tile)[:, 0:256], ALU.add))
                stats(tile).then_inc(s["x2_done"], 1)
                v.wait_ge(s["std_done"], 3 + tile)
                link(v.reciprocal(rstd[:, tile:tile + 1], std[:, tile:tile + 1]))
                link(v.tensor_scalar(h3[:, tile, :], xres[:, tile, :], mv[:, tile, 0:1], rstd[:, tile:tile + 1],
                                     ALU.subtract, ALU.mult))
                quantise(tile, h3[:, tile, :], hr[:, tile, :], hq[:, tile, :], 0, s["hq_done"])
                v.wait_ge(s["hq_done"], tile + 1)
                for n in range(2):
                    v.tensor_scalar(small[:, 4 + 2 * n + tile:5 + 2 * n + tile], small[:, tile:tile + 1],
                                    fstat[:, 4 + n:5 + n], None, ALU.mult).then_inc(s["dq"], 1)
            v.wait_ge(s["dq"], 4)
            for tile in range(NT):
                v.wait_ge(s["gu_ps"], 2 * tile + 2)
                v.wait_ge(s["silu"], tile + 1)
                link(v.scalar_tensor_tensor(pr[:, tile, :], bank(UP_AT[tile], 2), small[:, 6 + tile:7 + tile], sg[:, tile, :],
                                            ALU.mult, ALU.mult))
                quantise(tile, pr[:, tile, :], pr2[:, tile, :], pq[:, tile, :], 8, s["pq_done"])
                link(v.tensor_scalar(small[:, 12 + tile:13 + tile], small[:, 8 + tile:9 + tile], fstat[:, 6:7], None, ALU.mult))
            for tile in range(NT):
                v.wait_ge(s["y3_ps"], tile + 1)
                last = v.scalar_tensor_tensor(res[:, tile, :], bank(2 + tile)[:, 0:256], small[:, 12 + tile:13 + tile],
                                              xres[:, tile, :], ALU.mult, ALU.add)
            last.then_inc(s["out_done"], 1)


_INS = ['x', 'ctx_1024', 'L0_xattn_W_Q', 'L0_xattn_b_Q', 'L0_xattn_W_K', 'L0_xattn_b_K', 'L0_xattn_W_V',
        'L0_xattn_b_V', 'L0_xattn_W_O', 'L0_xattn_b_O', 'L0_attn_W_dkv', 'L0_attn_W_uk', 'L0_attn_W_uv',
        'L0_attn_W_dq', 'L0_attn_W_uq', 'L0_attn_W_qr', 'L0_attn_W_kr', 'L0_attn_W_out', 'L0_attn_idx_wq',
        'L0_attn_idx_wk', 'L0_attn_idx_w', 'L0_attn_raw_delta', 'L0_ffn_w_gate', 'L0_ffn_w_up', 'L0_ffn_w_down']


def kernel(**inputs):
    import numpy as _np
    import concourse.bacc as _bacc
    from concourse import mybir as _mybir
    from concourse.bass_utils import run_bass_kernel_spmd as _run

    nc = _bacc.Bacc("TRN2", target_bir_lowering=False, num_devices=1)
    arrays = {"consts_dram": constants()}
    consts = nc.dram_tensor("consts_dram", (128, NCONST), fp32, kind="ExternalInput").ap()
    args = {}
    for name in _INS:
        arr = _np.ascontiguousarray(inputs[name])
        arrays[f"in_{name}_dram"] = arr
        args[name] = nc.dram_tensor(f"in_{name}_dram", arr.shape, _mybir.dt.from_np(arr.dtype), kind="ExternalInput").ap()
    out = nc.dram_tensor("out_0_dram", (1, T, D), fp32, kind="ExternalOutput").ap()
    build(nc, consts, args, out)
    r = _run(nc, [arrays], core_ids=[0])
    return r.results[0]["out_0_dram"]
```
